# Optimizing a Trainium2 kernel written in Bass

```python
import numpy as np
import jax
import jax.numpy as jnp

def _softmax(x, axis=-1):
    return jax.nn.softmax(x, axis=axis)

def _gelu(x):
    return jax.nn.gelu(x, approximate=True)

def _silu(x):
    return jax.nn.silu(x)

def _sigmoid(x):
    return jax.nn.sigmoid(x)

def _layernorm(x, axis=-1, eps=1e-05):
    m = jnp.mean(x, axis=axis, keepdims=True)
    v = jnp.var(x, axis=axis, keepdims=True)
    return (x - m) / jnp.sqrt(v + eps)

def _scatter_add(tgt, idx, src, axis=0):
    return tgt.at[idx].add(src)

def _segment_sum(src, seg, n):
    return jax.ops.segment_sum(src, seg, n)
kernel_name = 'mk_decoder_preln_d1_seqx_r8_dc3245'

def setup_inputs(seed: int=0):
    np.random.seed(seed)
    _w = jnp.asarray

    def _rec_inputs():
        import jax
        import jax.numpy as jnp
        _rk = jax.random.key(seed)
        x = 4.136e-05 + 0.9999 * jax.random.normal(jax.random.fold_in(_rk, 1), (128, 64, 128), jnp.float32)
        _lenS = 64 - jax.random.randint(jax.random.fold_in(_rk, 7), (128,), 0, max(1, 64 // 4) + 1, jnp.int32)
        _lenS2 = 64 - jax.random.randint(jax.random.fold_in(_rk, 8), (128,), 0, max(1, 64 // 4) + 1, jnp.int32)
        _ctx_1024P = jax.random.normal(jax.random.fold_in(_rk, 11), (128, 16, 128), jnp.float32)
        _ctx_1024c = jax.random.dirichlet(jax.random.fold_in(_rk, 511), 0.3 * jnp.ones((16,), jnp.float32), (128, 64))
        _ctx_1024t = jnp.einsum('bsk,bkd->bsd', _ctx_1024c, _ctx_1024P)
        _ctx_1024t = _ctx_1024t * jax.lax.rsqrt(jnp.mean(jnp.square(_ctx_1024t)) + 1e-12) * 0.953939
        ctx_1024 = 7.22013e-05 + 1.00017 * (_ctx_1024t + 0.3 * jax.random.normal(jax.random.fold_in(_rk, 611), (128, 64, 128), jnp.float32))
        _validS = jnp.arange(64)[None, :] < _lenS[:, None]
        _validS2 = jnp.arange(64)[None, :] < _lenS2[:, None]
        _causal = jnp.tril(jnp.ones((64, 64), dtype=bool))
        mask_Bx1xSxS2_bf1 = jnp.ones((128, 1, 64, 64), dtype=bool)
        return (x, ctx_1024, mask_Bx1xSxS2_bf1)
    x, ctx_1024, mask_Bx1xSxS2_bf1 = _rec_inputs()

    def _L0_attn_setup():
        import jax, jax.numpy as jnp
        import numpy as np
        EMBED_DIM = 128
        NUM_HEADS = 16
        HEAD_DIM = EMBED_DIM // NUM_HEADS
        ALPHA = 1.0
        key = jax.random.key(seed)
        ks = jax.random.split(key, 9)
        B, T, D = (2, 256, EMBED_DIM)
        s = 1.0 / np.sqrt(D)
        return {'x': jax.random.normal(ks[0], (B, T, D), dtype=jnp.float32), 'Wq': jax.random.uniform(ks[1], (D, D), jnp.float32, -s, s), 'bq': jax.random.uniform(ks[2], (D,), jnp.float32, -s, s), 'Wk': jax.random.uniform(ks[3], (D, D), jnp.float32, -s, s), 'bk': jax.random.uniform(ks[4], (D,), jnp.float32, -s, s), 'Wv': jax.random.uniform(ks[5], (D, D), jnp.float32, -s, s), 'bv': jax.random.uniform(ks[6], (D,), jnp.float32, -s, s), 'Wo': jax.random.uniform(ks[7], (D, D), jnp.float32, -s, s), 'bo': jax.random.uniform(ks[8], (D,), jnp.float32, -s, s)}
    _L0_attn_all = _L0_attn_setup()
    _L0_attn_in = {k: v for k, v in _L0_attn_all.items() if k in ('Wq', 'bq', 'Wk', 'bk', 'Wv', 'bv', 'Wo', 'bo')}
    del _L0_attn_all

    def _L0_xattn_setup():
        import jax, jax.numpy as jnp
        import numpy as np
        NUM_HEADS = 16
        key = jax.random.key(seed)
        ks = jax.random.split(key, 8)
        B, S, F = (4, 256, 128)
        Fh = F // 2
        Fin = F + Fh
        d = {}
        d['kv'] = jax.random.normal(ks[0], (B, S, F), jnp.float32)
        d['q'] = jax.random.normal(ks[1], (B, S, F), jnp.float32)
        d['mask'] = jnp.ones((B, 1, S, S), jnp.bool_)
        d['Wsym'] = jax.random.normal(ks[2], (1, Fh), jnp.float32)
        d['Wq'] = jax.random.normal(ks[3], (Fin, F), jnp.float32) / np.sqrt(Fin)
        d['bq'] = jnp.zeros((F,), jnp.float32)
        d['Wk'] = jax.random.normal(ks[4], (Fin, F), jnp.float32) / np.sqrt(Fin)
        d['bk'] = jnp.zeros((F,), jnp.float32)
        d['Wv'] = jax.random.normal(ks[5], (Fin, F), jnp.float32) / np.sqrt(Fin)
        d['bv'] = jnp.zeros((F,), jnp.float32)
        d['Wo'] = jax.random.normal(ks[6], (F, F), jnp.float32) / np.sqrt(F)
        d['bo'] = jnp.zeros((F,), jnp.float32)
        d['distance_scale'] = jnp.full((1,), -1.0, jnp.float32)
        d['parity_strength'] = jnp.full((1,), 0.5, jnp.float32)
        d['localization_length'] = jnp.full((1,), 2.0, jnp.float32)
        return d
    _L0_xattn_all = _L0_xattn_setup()
    _L0_xattn_in = {k: v for k, v in _L0_xattn_all.items() if k in ('Wsym', 'Wq', 'bq', 'Wk', 'bk', 'Wv', 'bv', 'Wo', 'bo', 'distance_scale', 'parity_strength', 'localization_length')}
    del _L0_xattn_all

    def _L0_ffn_setup():
        import jax, jax.numpy as jnp
        import numpy as np
        key = jax.random.key(seed)
        k0, k1, k2, k3 = jax.random.split(key, 4)
        B, S, D, F, E = (8, 256, 128, 256, 8)
        x = jax.random.normal(k0, (B, S, D), dtype=jnp.float32)
        Wg = jax.random.normal(k1, (D, E), dtype=jnp.float32) * 0.02
        W1 = jax.random.normal(k2, (E, D, F), dtype=jnp.float32) * 0.02
        W2 = jax.random.normal(k3, (E, F, D), dtype=jnp.float32) * 0.02
        return {'x': x, 'Wg': Wg, 'W1': W1, 'W2': W2}
    _L0_ffn_all = _L0_ffn_setup()
    _L0_ffn_in = {k: v for k, v in _L0_ffn_all.items() if k in ('Wg', 'W1', 'W2')}
    del _L0_ffn_all
    return {'x': x, 'ctx_1024': ctx_1024, 'mask_Bx1xSxS2_bf1': mask_Bx1xSxS2_bf1, 'L0_attn_Wq': _L0_attn_in['Wq'], 'L0_attn_bq': _L0_attn_in['bq'], 'L0_attn_Wk': _L0_attn_in['Wk'], 'L0_attn_bk': _L0_attn_in['bk'], 'L0_attn_Wv': _L0_attn_in['Wv'], 'L0_attn_bv': _L0_attn_in['bv'], 'L0_attn_Wo': _L0_attn_in['Wo'], 'L0_attn_bo': _L0_attn_in['bo'], 'L0_xattn_Wsym': _L0_xattn_in['Wsym'], 'L0_xattn_Wq': _L0_xattn_in['Wq'], 'L0_xattn_bq': _L0_xattn_in['bq'], 'L0_xattn_Wk': _L0_xattn_in['Wk'], 'L0_xattn_bk': _L0_xattn_in['bk'], 'L0_xattn_Wv': _L0_xattn_in['Wv'], 'L0_xattn_bv': _L0_xattn_in['bv'], 'L0_xattn_Wo': _L0_xattn_in['Wo'], 'L0_xattn_bo': _L0_xattn_in['bo'], 'L0_xattn_distance_scale': _L0_xattn_in['distance_scale'], 'L0_xattn_parity_strength': _L0_xattn_in['parity_strength'], 'L0_xattn_localization_length': _L0_xattn_in['localization_length'], 'L0_ffn_Wg': _L0_ffn_in['Wg'], 'L0_ffn_W1': _L0_ffn_in['W1'], 'L0_ffn_W2': _L0_ffn_in['W2']}

def reference(x, ctx_1024, mask_Bx1xSxS2_bf1, L0_attn_Wq, L0_attn_bq, L0_attn_Wk, L0_attn_bk, L0_attn_Wv, L0_attn_bv, L0_attn_Wo, L0_attn_bo, L0_xattn_Wsym, L0_xattn_Wq, L0_xattn_bq, L0_xattn_Wk, L0_xattn_bk, L0_xattn_Wv, L0_xattn_bv, L0_xattn_Wo, L0_xattn_bo, L0_xattn_distance_scale, L0_xattn_parity_strength, L0_xattn_localization_length, L0_ffn_Wg, L0_ffn_W1, L0_ffn_W2):
    import jax
    import jax.numpy as jnp

    def _L0_attn_ref(x, Wq, bq, Wk, bk, Wv, bv, Wo, bo):
        import jax, jax.numpy as jnp
        import numpy as np
        EMBED_DIM = 128
        NUM_HEADS = 16
        HEAD_DIM = EMBED_DIM // NUM_HEADS
        ALPHA = 1.0
        B, T, D = x.shape
        H, hd = (NUM_HEADS, HEAD_DIM)

        def proj(W, b):
            return (x @ W.T + b).reshape(B, T, H, hd).transpose(0, 2, 1, 3)
        Q = proj(Wq, bq)
        K = proj(Wk, bk)
        V = proj(Wv, bv)
        scores = jnp.einsum('bhid,bhjd->bhij', Q, K) / jnp.sqrt(jnp.float32(hd))
        ti = jnp.arange(T)
        delta = ti[:, None] - ti[None, :]
        causal = delta < 0
        deltaf = delta.astype(jnp.float32)
        decay = jnp.where(causal, 0.0, -jnp.abs(deltaf) ** ALPHA)
        scores = jnp.where(causal[None, None], -jnp.inf, scores) + decay[None, None]
        attn = jax.nn.softmax(scores, axis=-1)
        out = jnp.einsum('bhij,bhjd->bhid', attn, V)
        out = out.transpose(0, 2, 1, 3).reshape(B, T, D)
        return out @ Wo.T + bo

    def _L0_xattn_ref(kv, q, mask, Wsym, Wq, bq, Wk, bk, Wv, bv, Wo, bo, distance_scale, parity_strength, localization_length):
        import jax, jax.numpy as jnp
        import numpy as np
        NUM_HEADS = 16
        B, S, F = kv.shape
        H = NUM_HEADS
        D = F // H
        dt = kv.dtype
        pos = jnp.arange(S)
        even_odd = (pos % 2).astype(dt)
        sym = even_odd[:, None] * Wsym
        sym_b = jnp.broadcast_to(sym[None], (B, S, sym.shape[-1]))
        q_cat = jnp.concatenate([q, sym_b], axis=-1)
        kv_cat = jnp.concatenate([kv, sym_b], axis=-1)
        query = (q_cat @ Wq + bq).reshape(B, S, H, D)
        key_ = (kv_cat @ Wk + bk).reshape(B, S, H, D)
        value = (kv_cat @ Wv + bv).reshape(B, S, H, D)
        logits = jnp.einsum('bqhd,bkhd->bhqk', query, key_)
        dist = jnp.abs(pos[:, None] - pos[None, :]).astype(dt)
        parity = ((pos[:, None] + pos[None, :]) % 2).astype(dt)
        bias = distance_scale * jnp.log1p(dist) + parity_strength * (1.0 - 2.0 * parity) - dist / jnp.exp(localization_length)
        logits = (logits + bias[None, None]) / jnp.sqrt(jnp.asarray(D, dt))
        logits = jnp.where(mask, logits, jnp.finfo(dt).min)
        weights = jax.nn.softmax(logits, axis=-1).astype(dt)
        attn = jnp.einsum('bhqk,bkhd->bqhd', weights, value).reshape(B, S, F)
        return attn @ Wo + bo

    def _L0_ffn_ref(x, Wg, W1, W2):
        import jax, jax.numpy as jnp
        import numpy as np
        B, S, D = x.shape
        E = Wg.shape[1]
        T = B * S
        cap = max(1, T // E)
        xt = x.reshape(T, D)
        logits = xt @ Wg
        probs = jax.nn.softmax(logits, axis=-1)
        pT = probs.T
        _, top_idx = jax.lax.top_k(pT, cap)
        sel = jnp.zeros((E, T), dtype=bool).at[jnp.arange(E)[:, None], top_idx].set(True)
        masked = jnp.where(sel, pT, -jnp.inf)
        assigned = sel.any(axis=0)
        tok2exp = jnp.where(assigned, jnp.argmax(masked, axis=0), jnp.argmax(pT, axis=0))
        weights = jnp.take_along_axis(probs, tok2exp[:, None], axis=1)[:, 0]
        out = jnp.zeros_like(xt)
        for e in range(E):
            gate = jnp.where(tok2exp == e, weights, 0.0)
            h = jax.nn.gelu(xt @ W1[e], approximate=False) @ W2[e]
            out = out + gate[:, None] * h
        return out.reshape(B, S, D)
    x = x + _L0_attn_ref(_layernorm(x, axis=-1), L0_attn_Wq, L0_attn_bq, L0_attn_Wk, L0_attn_bk, L0_attn_Wv, L0_attn_bv, L0_attn_Wo, L0_attn_bo)
    x = x + _L0_xattn_ref(ctx_1024, _layernorm(x, axis=-1), mask_Bx1xSxS2_bf1, L0_xattn_Wsym, L0_xattn_Wq, L0_xattn_bq, L0_xattn_Wk, L0_xattn_bk, L0_xattn_Wv, L0_xattn_bv, L0_xattn_Wo, L0_xattn_bo, L0_xattn_distance_scale, L0_xattn_parity_strength, L0_xattn_localization_length)
    x = x + _L0_ffn_ref(_layernorm(x, axis=-1), L0_ffn_Wg, L0_ffn_W1, L0_ffn_W2)
    return x

_drawn_inputs = setup_inputs


def setup_inputs(seed=0):
    import zlib

    import numpy as np

    out = dict(_drawn_inputs(seed))
    spreads = {'L0_xattn_bq': (0.0, 0.442),
     'L0_xattn_bk': (0.0, 0.8),
     'L0_xattn_bv': (0.0, 0.1),
     'L0_xattn_bo': (0.0, 0.1)}
    factors = {'L0_attn_bq': 8.0, 'L0_attn_bk': 8.0, 'L0_ffn_Wg': 8.0, 'L0_ffn_W1': 8.0, 'L0_ffn_W2': 8.0}
    for name, (base, spread) in spreads.items():
        noise = np.random.default_rng([zlib.crc32(name.encode()), seed]).standard_normal(out[name].shape)
        drawn = base * np.exp(spread * noise) if base else spread * noise
        out[name] = jnp.asarray(drawn.astype(out[name].dtype))
    for name, factor in factors.items():
        out[name] = (out[name] * factor).astype(out[name].dtype)
    return out
```

```python
from contextlib import ExitStack

import concourse.bass as bass
from concourse import mybir
from concourse.alu_op_type import AluOpType as ALU

ACT = mybir.ActivationFunctionType
F32 = mybir.dt.float32
BF16 = mybir.dt.bfloat16
I32 = mybir.dt.int32
U32 = mybir.dt.uint32
U8 = mybir.dt.uint8
AX = mybir.AxisListType

P = 128
BATCH, SEQ, D = 128, 64, 128
HEADS = 16
HD = D // HEADS
TOKENS = BATCH * SEQ
TILES = TOKENS // P
BLOCK = 4
BLOCKS = TILES // BLOCK
EXPERTS = 8
FF = 256
CAP = TOKENS // EXPERTS
SYM = 64
EPS = 1e-5
NEG = -(2.0 ** 100)
ROUTED = -(-(TILES + EXPERTS - 1) // 4) * 4

C_IDENT = 0
C_HEAD = C_IDENT + P
C_SEQ = C_HEAD + 4
C_DECAY = C_SEQ + 2
C_DIST = C_DECAY + SEQ
C_PARITY = C_DIST + SEQ
C_SAME = C_PARITY + SEQ
C_BEFORE = C_SAME + P
C_LOWER = C_BEFORE + P
C_ONES = C_LOWER + P
C_IOTA = C_ONES + P
C_REST = C_IOTA + P
C_RUN = C_REST + EXPERTS * TILES
C_TOKEN = C_RUN + EXPERTS * TILES
C_BITS = C_TOKEN + TILES
C_COLS = C_BITS + 31


def constants():
    import numpy as np

    c = np.zeros((P, C_COLS), np.float32)
    p = np.arange(P)
    c[:, C_IDENT:C_IDENT + P] = np.eye(P)
    c[p, C_HEAD + (p // HD) % 4] = 1.0
    c[p, C_SEQ + (p // 32) % 2] = HD ** -0.5
    q, k = np.arange(P)[:, None] % SEQ, np.arange(SEQ)[None, :]
    c[:, C_DECAY:C_DECAY + SEQ] = np.where(k <= q, k - q, NEG)
    c[:, C_DIST:C_DIST + SEQ] = abs(q - k)
    c[:, C_PARITY:C_PARITY + SEQ] = 1.0 - 2.0 * ((q + k) % 2)
    same = (p[:, None] % EXPERTS) == (p[None, :] % EXPERTS)
    c[:, C_SAME:C_SAME + P] = same
    c[:, C_BEFORE:C_BEFORE + P] = same & (p[:, None] < p[None, :])
    c[:, C_LOWER:C_LOWER + P] = p[:, None] < p[None, :]
    c[:, C_ONES:C_ONES + P] = 1.0
    c[:, C_IOTA:C_IOTA + P] = p[None, :]
    c[:, C_REST:C_RUN] = np.tile(EXPERTS - np.arange(EXPERTS), TILES)[None, :]
    c[:, C_RUN:C_TOKEN] = np.tile(np.arange(TILES) > 0, EXPERTS)[None, :]
    place = np.arange(TILES)
    c[:, C_TOKEN:C_BITS] = ((place % 16) * 4 + place // 16)[None, :] * P + p[:, None] + 1
    c[:, C_BITS:C_BITS + 30] = 2.0 ** np.arange(29, -1, -1)[None, :]
    rows = np.ones((6, BLOCK * P), np.float32)
    rows[3:] = np.arange(BLOCK * P)[None, :] % 2
    return c, rows


NAMES = ["q", "k", "v", "o"]


def after(engine, semaphore, value):
    if isinstance(value, int) and value <= 0:
        return
    engine.wait_ge(semaphore, value)


def passed(engine, semaphore):
    engine.sem_inc(semaphore, 1)


def build(nc, a, stop_after=3):
    ctx = ExitStack()
    with ctx:
        def sb(name, shape, dt=F32):
            return ctx.enter_context(nc.sbuf_tensor(name, shape, dt))

        def sem(name):
            return ctx.enter_context(nc.semaphore(name))

        x_all = sb("x_all", [P, TILES, D])
        cst = sb("cst", [P, C_COLS])
        attention(nc, a, x_all, cst)
        if stop_after >= 2:
            sh = dict(
                gate_of=sb("gate_of", [P, ROUTED]),
                expert_of=sb("expert_of", [P, ROUTED], I32),
                gather_at=sb("gather_at", [P, ROUTED], I32),
                scatter_at=sb("scatter_at", [P, ROUTED], I32),
            )
            router(nc, a, x_all, cst, sh)
            if stop_after >= 3:
                experts(nc, a, cst, sh)


def attention(nc, a, x_all, cst):
    ctx = ExitStack()
    with ctx:
        def sb(name, shape, dt=F32):
            return ctx.enter_context(nc.sbuf_tensor(name, shape, dt))

        def pb(name, shape):
            return ctx.enter_context(nc.psum_tensor(name, shape, F32))

        def sem(name):
            return ctx.enter_context(nc.semaphore(name))

        w_qk = [sb(f"w_qk{t}", [P, 2, 2, 2, 2, 32]) for t in range(4)]
        w_v = sb("w_v", [P, 2, D])
        w_o = sb("w_o", [P, 2, D])
        w_sym = sb("w_sym", [SYM, 3, D])
        sym_at = sb("sym_at", [SYM, 3, EXPERTS])
        tab = sb("tab", [8, 2, D])
        rem1 = sb("rem1", [8, 2, D])
        rem2 = sb("rem2", [8, 2, D])
        split = sb("split", [8, 2, 3, D], BF16)
        bt = sb("bt", [6, 8, D], BF16)
        b_qk = sb("b_qk", [6, 4, 2, 2, 2, 32], BF16)
        rows32 = sb("rows32", [6, BLOCK * P])
        rows = sb("rows", [6, BLOCK * P], BF16)
        scal = sb("scal", [P, 3])
        sc = sb("sc", [P, 4])
        xbias = sb("xbias", [P, SEQ])
        xb1 = sb("xb1", [P, SEQ])
        xb2 = sb("xb2", [P, SEQ])
        xb3 = sb("xb3", [P, SEQ])

        ctx_in = [sb(f"ctx_in{i}", [P, BLOCK, D]) for i in range(2)]
        mask_in = [sb(f"mask_in{i}", [P, BLOCK, SEQ], U8) for i in range(2)]
        mask_f = sb("mask_f", [P, BLOCK, SEQ])
        mbias = [sb(f"mbias{i}", [P, BLOCK, SEQ]) for i in range(2)]
        stats = sb("stats", [P, BLOCK, 6])
        mv = [sb(f"mv{i}", [P, BLOCK, 2]) for i in range(2)]
        vareps = sb("vareps", [P, BLOCK])
        mhalf = sb("mhalf", [P, BLOCK])
        rstd = [sb(f"rstd{i}", [P, BLOCK]) for i in range(2)]
        xn = sb("xn", [P, BLOCK, D])
        xT = sb("xT", [P, BLOCK, 2, SEQ])
        cT = sb("cT", [P, BLOCK, 2, SEQ])
        q_sb = sb("q_sb", [P, 2, BLOCK, SEQ])
        k_sb = sb("k_sb", [P, 2, BLOCK, SEQ])
        q_bd = [sb(f"q_bd{i}", [P, 2, BLOCK, 2, SEQ]) for i in range(2)]
        k_bd = [sb(f"k_bd{i}", [P, 2, BLOCK, 4, SEQ]) for i in range(2)]
        v_bd = [sb(f"v_bd{i}", [P, 2 * BLOCK, 8, 2, HD + 1]) for i in range(2)]
        logit = [sb(f"logit{i}", [P, HEADS, SEQ]) for i in range(4)]
        top = [sb(f"top{i}", [P, HEADS]) for i in range(4)]
        probT = [sb(f"probT{i}", [P, 8, P]) for i in range(2)]
        rden = sb("rden", [P, 8, 2])
        o_sb = sb("o_sb", [P, 8, 2, HD])
        oT = sb("oT", [P, P])

        score_ps = [pb(f"score_ps{i}", [P, HEADS, SEQ]) for i in range(2)]
        probT_ps = pb("probT_ps", [P, 8, P])
        front_ps = pb("front_ps", [P, BLOCK, P])
        v_ps = front_ps[:, :, :].rearrange("p t (s m e) -> p (t s) m e", s=2, m=8)
        out_ps = pb("out_ps", [P, 512])
        o_ps = out_ps[:, 0:288].rearrange("p (m s h e) -> p m s h e", m=8, s=2, h=2)
        oT_ps = out_ps[:, 288:288 + P]
        y_ps = out_ps[:, 0:D]

        ident = cst[:, C_IDENT:C_IDENT + P]

        s_cst = sem("s_cst")
        s_x = [sem(f"s_x{i}") for i in range(4)]
        s_wz = sem("s_wz")
        s_w = sem("s_w")
        s_small = sem("s_small")
        s_symz = sem("s_symz")
        s_sym = sem("s_sym")
        s_symps = sem("s_symps")
        s_tab = sem("s_tab")
        s_split = sem("s_split")
        s_bt = sem("s_bt")
        s_bqk = sem("s_bqk")
        s_rows = sem("s_rows")
        s_xbias = sem("s_xbias")
        s_xba = sem("s_xba")
        s_vz = sem("s_vz")
        s_mhalf = sem("s_mhalf")
        s_ctx = [sem(f"s_ctx{i}") for i in range(2)]
        s_mask = [sem(f"s_mask{i}") for i in range(2)]
        s_bn = sem("s_bn")
        s_stat = sem("s_stat")
        s_veps = sem("s_veps")
        s_rstd = sem("s_rstd")
        s_ln = sem("s_ln")
        s_xT = sem("s_xT")
        s_xTe = sem("s_xTe")
        s_cT = sem("s_cT")
        s_cTe = sem("s_cTe")
        s_q = sem("s_q")
        s_qe = sem("s_qe")
        s_k = sem("s_k")
        s_ke = sem("s_ke")
        s_v = sem("s_v")
        s_ve = sem("s_ve")
        s_qbd = sem("s_qbd")
        s_kbd = sem("s_kbd")
        s_mf = sem("s_mf")
        s_mb = sem("s_mb")
        s_score = sem("s_score")
        s_logit = sem("s_logit")
        s_top = sem("s_top")
        s_sub = sem("s_sub")
        s_prob = sem("s_prob")
        s_pT = sem("s_pT")
        s_pTe = sem("s_pTe")
        s_pv = sem("s_pv")
        s_rden = sem("s_rden")
        s_norm = sem("s_norm")
        s_oT = sem("s_oT")
        s_oTe = sem("s_oTe")
        s_y = sem("s_y")
        s_res = sem("s_res")
        s_st = sem("s_st")
        s_passed_v = sem("s_passed_v")
        s_passed_g = sem("s_passed_g")
        s_passed_s = sem("s_passed_s")

        x_dram = a["x"].rearrange("b s d -> (b s) d").rearrange("(t p) d -> p t d", p=P)
        ctx_dram = a["ctx_1024"].rearrange("b s d -> (b s) d").rearrange("(t p) d -> p t d", p=P)
        mask_dram = a["mask_Bx1xSxS2_bf1"].rearrange("b o q k -> (b o q) k").rearrange("(t p) k -> p t k", p=P)

        X_CHUNKS = [(0, 1), (1, 2), (2, 6), (6, BLOCKS)]
        N_W = 8 + 4
        N_SMALL = 8 + 1 + 3 + 3 + 3

        PAIRS = 2 * TILES
        HALF = 2
        ITERS = 2 * BLOCKS // HALF
        MID = ITERS // 2

        def schedule(engine, body, step):
            body(0, 0, 0, True)
            with engine.Fori(1, MID - 1) as it:
                body(it * HALF, 0, 0, False)
            body((MID - 1) * HALF, 0, 1, False)
            body(MID * HALF, 1, 1, False)
            with engine.Fori(MID + 1, ITERS - 1) as it:
                body(it * HALF, 1, 1, False)
            body((ITERS - 1) * HALF, 1, None, False)

        def steps(block0, att, nxt, first):
            for u in range(HALF * BLOCK):
                h = u // BLOCK
                ahead = att if h == 0 else nxt
                yield block0 * BLOCK + u, u, block0 + h, h, u % BLOCK, att, ahead

        block = ctx.enter_context(nc.Block())

        @block.sync
        def _(sp):
            sp.dma_start(cst[:, :], a["cst"]).then_inc(s_cst, 16)
            for i, (b0, b1) in enumerate(X_CHUNKS[:2]):
                sp.dma_start(x_all[:, b0 * BLOCK:b1 * BLOCK, :], x_dram[:, b0 * BLOCK:b1 * BLOCK, :]).then_inc(s_x[i], 16)
            for att, pre in enumerate(["L0_attn_b", "L0_xattn_b"]):
                for i, n in enumerate(NAMES):
                    sp.dma_start(tab[att * 4 + i:att * 4 + i + 1, 0, :],
                                 a[pre + n].rearrange("(o d) -> o d", o=1)).then_inc(s_small, 16)
            sp.dma_start(rows32[:, :], a["rows"]).then_inc(s_small, 16)
            for i, n in enumerate(["distance_scale", "parity_strength", "localization_length"]):
                sp.dma_start(scal[:, i:i + 1],
                             a["L0_xattn_" + n].rearrange("(o d) -> o d", o=1).to_broadcast([P, 1])).then_inc(s_small, 16)
            for i, n in enumerate("qkv"):
                sp.dma_start(w_sym[:, i, :], a["L0_xattn_W" + n][D:D + SYM, :]).then_inc(s_small, 16)
            sp.wait_ge(s_symz, 1)
            for i, n in enumerate("qkv"):
                sp.dma_start(sym_at[:, i, 4 + i:5 + i], a["L0_xattn_Wsym"].rearrange("o d -> d o")).then_inc(s_small, 16)
            sp.wait_ge(s_wz, 4)
            weights = [a["attn_WqT"], a["attn_WkT"], a["L0_xattn_Wq"][0:D, :], a["L0_xattn_Wk"][0:D, :]]
            for t, w in enumerate(weights):
                for s in range(2):
                    for g in range(2):
                        sp.dma_start(w_qk[t][:, g, s, :, s, :],
                                     w.rearrange("d (j g c) -> d g j c", j=2, g=2)[:, g]).then_inc(s_w, 16)
            for i, w in enumerate([a["attn_WvT"], a["L0_xattn_Wv"][0:D, :]]):
                sp.dma_start(w_v[:, i, :], w).then_inc(s_w, 16)
            for i, w in enumerate([a["attn_WoT"], a["L0_xattn_Wo"]]):
                sp.dma_start(w_o[:, i, :], w).then_inc(s_w, 16)
            for i, (b0, b1) in enumerate(X_CHUNKS[2:]):
                sp.dma_start(x_all[:, b0 * BLOCK:b1 * BLOCK, :], x_dram[:, b0 * BLOCK:b1 * BLOCK, :]).then_inc(s_x[2 + i], 16)
            sp.wait_ge(s_split, 5)
            for c in range(2):
                for part in range(3):
                    sp.dma_start(bt[c * 3 + part:c * 3 + part + 1, :, :], split[:, c, part, :]).then_inc(s_bt, 16)

            def load(c, par):
                after(sp, s_cT, c - 1)
                sp.dma_start(ctx_in[par][:, :, :], ctx_dram[:, bass.ds(c * BLOCK, BLOCK), :]).then_inc(s_ctx[par], 16)
                after(sp, s_mf, c - 1)
                passed(sp, s_passed_s)
                sp.dma_start(mask_in[par][:, :, :], mask_dram[:, bass.ds(c * BLOCK, BLOCK), :]).then_inc(s_mask[par], 16)

            for c in range(2):
                load(c, c)
            with sp.Fori(1, BLOCKS // 2) as i:
                for par in range(2):
                    load(i * 2 + par, par)

            if "x3" in a:
                sp.wait_ge(s_res, 2 * TILES)
                sp.dma_start(a["x3"].rearrange("(t p) d -> p t d", p=P), x_all[:, :, :]).then_inc(s_st, 16)
                sp.wait_ge(s_st, 16)

        @block.tensor
        def _(pe):
            pe.wait_ge(s_cst, 16)
            pe.wait_ge(s_small, 16 * N_SMALL)
            for i in range(3):
                mm = pe.matmul(out_ps[0:8, 0:D], sym_at[:, i, :], w_sym[:, i, :], start=(i == 0), stop=(i == 2))
            mm.then_inc(s_symps, 1)

            def transpose_x(b):
                pe.wait_ge(s_ln, b + 1)
                after(pe, s_ve, b)
                for t in range(BLOCK):
                    mm = pe.transpose(front_ps[:, t, :], xn[:, t, :], ident)
                mm.then_inc(s_xT, 1)

            def transpose_ctx(b, par):
                c = b - BLOCKS
                pe.wait_ge(s_ctx[par], (c - par) * 8 + 16)
                pe.wait_ge(s_xTe, b + 1)
                for t in range(BLOCK):
                    mm = pe.transpose(front_ps[:, t, :], ctx_in[par][:, t, :], ident)
                mm.then_inc(s_cT, 1)

            def project(t, src, signal):
                for g in range(2):
                    out = front_ps[:, :, :].rearrange("p t c -> p (t c)")[:, g * 256:g * 256 + 256]
                    pe.matmul(out, b_qk[:, t, g].rearrange("r j s c -> r (j s c)"), rows[:, 0:256],
                              start=(g == 0), stop=False, skip_group_check=True)
                    for s in range(2):
                        mm = pe.matmul(out, w_qk[t][:, g, s].rearrange("d j s c -> d (j s c)"), src[:, :, s, :],
                                       start=False, stop=(s == 1), skip_group_check=True)
                mm.then_inc(signal, 1)

            def project_q(b, att):
                pe.wait_ge(s_xTe, b + 1)
                if att:
                    pe.wait_ge(s_cTe, b - BLOCKS + 1)
                project(2 * att, xT, s_q)

            def project_k(b, att):
                pe.wait_ge(s_qe, b + 1)
                project(2 * att + 1, cT if att else xT, s_k)

            def project_v(b, att):
                src = cT if att else xT
                pe.wait_ge(s_ke, b + 1)
                bias = bt[:, 4 * att + 2, :].rearrange("r (m h e) -> r h m e", m=8, h=2)
                w = w_v[:, att, :].rearrange("d (m h e) -> d h m e", m=8, h=2)
                for h in range(2):
                    pe.matmul(v_ps[64 * h:64 * h + 64], rows[:, 0:SEQ],
                              bias[:, h].unsqueeze(1).to_broadcast([6, 2 * BLOCK, 8, HD]),
                              start=True, stop=False, skip_group_check=True)
                for i in range(2 * BLOCK):
                    for h in range(2):
                        mm = pe.matmul(v_ps[64 * h:64 * h + 64, i], src[:, i // 2, i % 2, :], w[:, h],
                                       start=False, stop=(i == 2 * BLOCK - 1), skip_group_check=True)
                mm.then_inc(s_v, 1)

            def front(b, par, att, slot):
                if att is None:
                    return
                if slot == 0:
                    transpose_x(b)
                elif slot == 1 and att:
                    transpose_ctx(b, par)
                elif slot == 2:
                    project_q(b, att)
                elif slot == 3:
                    project_k(b, att)
                elif slot == 4:
                    project_v(b, att)

            def scores(n, u, b, par, t):
                pe.wait_ge(s_qbd, b + 1)
                pe.wait_ge(s_kbd, b + 1)
                after(pe, s_logit, n - 1)
                for g in range(2):
                    for j in range(2):
                        mm = pe.matmul(score_ps[u % 2][:, j * 8 + g * 4:j * 8 + g * 4 + 4, :],
                                       q_bd[par][64 * j:64 * j + 64, g, t, :, :], k_bd[par][64 * j:64 * j + 64, g, t, :, :],
                                       start=True, stop=True)
                mm.then_inc(s_score, 1)

            def transpose_probs(n, u):
                pe.wait_ge(s_prob, n + 1)
                for half in range(2):
                    after(pe, s_pTe, 2 * n - 1 + half)
                    for m in range(4 * half, 4 * half + 4):
                        mm = pe.transpose(probT_ps[:, m, :], logit[u % 4][:, 2 * m:2 * m + 2, :], ident)
                    mm.then_inc(s_pT, 1)

            def values(n, u, b):
                par, t = u // BLOCK, u % BLOCK
                after(pe, s_res, n)
                pe.wait_ge(s_ve, b + 1)
                for m in range(8):
                    if m % 4 == 0:
                        pe.wait_ge(s_pTe, 2 * n + 1 + m // 4)
                    mm = pe.matmul(o_ps[:, m], probT[u % 2][:, m, :], v_bd[par][:, 2 * t:2 * t + 2, m],
                                   start=True, stop=True)
                mm.then_inc(s_pv, 1)

            def transpose_out(n):
                pe.wait_ge(s_norm, n + 1)
                pe.transpose(oT_ps, o_sb[:, :, :, :].rearrange("p m h e -> p (m h e)"), ident).then_inc(s_oT, 1)

            def project_out(n, att):
                pe.wait_ge(s_oTe, n + 1)
                pe.matmul(y_ps, rows[:, 0:P], bt[:, 4 * att + 3, :], start=True, stop=False)
                pe.matmul(y_ps, oT[:, :], w_o[:, att, :], start=False, stop=True).then_inc(s_y, 1)

            pe.wait_ge(s_w, 16 * (16 + 4))
            pe.wait_ge(s_bqk, 8)
            pe.wait_ge(s_rows, 1)
            for slot in range(6):
                front(0, 0, 0, slot)

            def body(block0, att, nxt, first):
                for n, u, b, par, t, here, ahead in steps(block0, att, nxt, first):
                    scores(n, u, b, par, t)
                    if not (first and u < 3):
                        transpose_out(n - 3)
                    if not (first and u < 2):
                        transpose_probs(n - 2, (u - 2) % 8)
                    if not (first and u < 3):
                        late = 0 if (att == 1 and isinstance(block0, int) and block0 == BLOCKS and u < 3) else att
                        project_out(n - 3, late)
                    front(b + 1, 1 - par, ahead, 2 * t)
                    if not (first and u < 2):
                        values(n - 2, (u - 2) % 8, b if t >= 2 else b - 1)
                    front(b + 1, 1 - par, ahead, 2 * t + 1)

            schedule(pe, body, None)
            n = PAIRS
            transpose_out(n - 3)
            transpose_probs(n - 2, 6)
            project_out(n - 3, 1)
            values(n - 2, 6, 2 * BLOCKS - 1)
            transpose_out(n - 2)
            transpose_probs(n - 1, 7)
            project_out(n - 2, 1)
            values(n - 1, 7, 2 * BLOCKS - 1)
            transpose_out(n - 1)
            project_out(n - 1, 1)

        @block.scalar
        def _(act):
            act.wait_ge(s_cst, 16)
            act.wait_ge(s_small, 16 * N_SMALL)
            act.activation(xb1[:, :], cst[:, C_DIST:C_DIST + SEQ], ACT.Ln, bias=1.0).then_inc(s_xba, 1)
            act.activation(sc[:, 0:1], scal[:, 2:3], ACT.Exp).then_inc(s_xba, 1)

            def evacuate_x(b):
                after(act, s_xT, b + 1)
                act.activation(xT[:, :, :, :].rearrange("p t s q -> p t (s q)"), front_ps[:, :, :],
                               ACT.Copy).then_inc(s_xTe, 1)

            def evacuate_ctx(b):
                act.wait_ge(s_cT, b - BLOCKS + 1)
                act.activation(cT[:, :, :, :].rearrange("p t s q -> p t (s q)"), front_ps[:, :, :],
                               ACT.Copy).then_inc(s_cTe, 1)

            def evacuate_q(b):
                act.wait_ge(s_q, b + 1)
                after(act, s_qbd, b)
                act.activation(q_sb[:, :, :, :].rearrange("p g t q -> p (g t q)"),
                               front_ps[:, :, :].rearrange("p t c -> p (t c)"), ACT.Copy).then_inc(s_qe, 1)

            def evacuate_k(b):
                act.wait_ge(s_k, b + 1)
                after(act, s_kbd, b)
                act.activation(k_sb[:, :, :, :].rearrange("p g t q -> p (g t q)"),
                               front_ps[:, :, :].rearrange("p t c -> p (t c)"), ACT.Copy).then_inc(s_ke, 1)

            def front(b, att, slot):
                if att is None:
                    return
                if slot == 0:
                    evacuate_x(b)
                elif slot == 1 and att:
                    evacuate_ctx(b)
                elif slot == 2:
                    evacuate_q(b)
                elif slot == 3:
                    evacuate_k(b)

            def exponentials(n, u):
                act.wait_ge(s_sub, n + 1)
                act.activation(logit[u % 4][:, :, :], logit[u % 4][:, :, :], ACT.Exp).then_inc(s_prob, 1)

            def evacuate_out(n):
                act.wait_ge(s_oT, n + 1)
                act.activation(oT[:, :], oT_ps, ACT.Copy).then_inc(s_oTe, 1)

            def evacuate_probs(n, u):
                after(act, s_pv, n - 1)
                for half in range(2):
                    act.wait_ge(s_pT, 2 * n + 1 + half)
                    act.activation(probT[u % 2][:, 4 * half:4 * half + 4, :], probT_ps[:, 4 * half:4 * half + 4, :],
                                   ACT.Copy).then_inc(s_pTe, 1)

            for slot in range(6):
                front(0, 0, slot)

            def body(block0, att, nxt, first):
                for n, u, b, par, t, here, ahead in steps(block0, att, nxt, first):
                    if not (first and u < 1):
                        exponentials(n - 1, (u - 1) % 8)
                    if not (first and u < 3):
                        evacuate_out(n - 3)
                    if not (first and u < 2):
                        evacuate_probs(n - 2, (u - 2) % 8)
                    front(b + 1, ahead, 2 * t)
                    front(b + 1, ahead, 2 * t + 1)

            schedule(act, body, None)
            n = PAIRS
            exponentials(n - 1, 7)
            evacuate_out(n - 3)
            evacuate_probs(n - 2, 6)
            evacuate_out(n - 2)
            evacuate_probs(n - 1, 7)
            evacuate_out(n - 1)

        @block.vector
        def _(dve):
            for i in range(2):
                dve.memset(v_bd[i][:, :, :, :, :], 0.0).then_inc(s_vz, 1)
            dve.wait_ge(s_vz, 2)
            for i in range(2):
                for h in range(2):
                    dve.memset(v_bd[i][64 * h:64 * h + 64, :, :, h, HD:HD + 1], 1.0).then_inc(s_vz, 1)

            def stats_of(n, t, b, par):
                dve.bn_stats(stats[:, t, :], x_all[:, n, :]).then_inc(s_bn, 1)

            def aggregate(b, par):
                dve.wait_ge(s_bn, BLOCK * (b + 1))
                if not isinstance(b, int) or b >= 2:
                    dve.wait_ge(s_rstd, b - 1)
                    dve.wait_ge(s_ln, b - 1)
                    passed(dve, s_passed_v)
                for t in range(BLOCK):
                    ins = dve.bn_aggr(mv[par][:, t, :], stats[:, t, :])
                ins.then_inc(s_stat, 1)

            def normalise(b, par):
                dve.wait_ge(s_rstd, b + 1)
                after(dve, s_xT, b)
                for t in range(BLOCK):
                    ins = dve.tensor_scalar(xn[:, t, :], xn_source(b, t), mv[par][:, t, 0:1], rstd[par][:, t:t + 1],
                                            ALU.subtract, ALU.mult)
                ins.then_inc(s_ln, 1)

            def tile_of(b, t):
                return (b * BLOCK + t) % TILES if isinstance(b, int) else b * BLOCK + t

            shift = [0]

            def xn_source(b, t):
                n = tile_of(b, t)
                return x_all[:, n, :] if isinstance(n, int) else x_all[:, bass.ds(n - shift[0], 1), :].rearrange(
                    "p o d -> p (o d)")

            def stat_source(b, t):
                return xn_source(b, t)

            for b in range(2):
                dve.wait_ge(s_x[b], 16)
                for t in range(BLOCK):
                    dve.bn_stats(stats[:, t, :], stat_source(b, t)).then_inc(s_bn, 1)
                aggregate(b, b)
                if b == 0:
                    dve.wait_ge(s_stat, 1)
            dve.wait_ge(s_cst, 16)
            normalise(0, 0)

            dve.wait_ge(s_small, 16 * N_SMALL)
            dve.wait_ge(s_symps, 1)
            dve.tensor_copy(tab[:, 1, :], out_ps[0:8, 0:D]).then_inc(s_tab, 1)
            dve.tensor_copy(rows[:, :], rows32[:, :]).then_inc(s_rows, 1)
            dve.wait_ge(s_tab, 1)
            dve.tensor_copy(split[:, :, 0, :], tab[:, :, :]).then_inc(s_split, 1)
            dve.wait_ge(s_split, 1)
            dve.tensor_tensor(rem1[:, :, :], tab[:, :, :], split[:, :, 0, :], ALU.subtract).then_inc(s_split, 1)
            dve.wait_ge(s_split, 2)
            dve.tensor_copy(split[:, :, 1, :], rem1[:, :, :]).then_inc(s_split, 1)
            dve.wait_ge(s_split, 3)
            dve.tensor_tensor(rem2[:, :, :], rem1[:, :, :], split[:, :, 1, :], ALU.subtract).then_inc(s_split, 1)
            dve.wait_ge(s_split, 4)
            dve.tensor_copy(split[:, :, 2, :], rem2[:, :, :]).then_inc(s_split, 1)
            dve.wait_ge(s_xba, 2)
            dve.reciprocal(sc[:, 1:2], sc[:, 0:1]).then_inc(s_xbias, 1)
            dve.tensor_scalar(xb1[:, :], xb1[:, :], scal[:, 0:1], None, ALU.mult).then_inc(s_xbias, 1)
            dve.wait_ge(s_xbias, 2)
            dve.scalar_tensor_tensor(out=xb2[:, :], in0=cst[:, C_PARITY:C_PARITY + SEQ], scalar=scal[:, 1:2],
                                     in1=xb1[:, :], op0=ALU.mult, op1=ALU.add).then_inc(s_xbias, 1)
            dve.tensor_scalar(xb3[:, :], cst[:, C_DIST:C_DIST + SEQ], sc[:, 1:2], None, ALU.mult).then_inc(s_xbias, 1)
            dve.wait_ge(s_xbias, 4)
            dve.tensor_tensor(xb2[:, :], xb2[:, :], xb3[:, :], ALU.subtract).then_inc(s_xbias, 1)
            dve.wait_ge(s_xbias, 5)
            dve.tensor_scalar(xbias[:, :], xb2[:, :], float(HD) ** -0.5, None, ALU.mult).then_inc(s_xbias, 1)
            dve.wait_ge(s_bt, 16 * 6)
            for t in range(4):
                for g in range(2):
                    src = bt[:, (t // 2) * 4 + t % 2, :].rearrange("r (j g c) -> r g j c", j=2, g=2)[:, g]
                    dve.tensor_copy(b_qk[:, t, g], src.unsqueeze(2).to_broadcast([6, 2, 2, 32])).then_inc(s_bqk, 1)

            def evacuate_v(b, par):
                dve.wait_ge(s_v, b + 1)
                after(dve, s_pv, (b - 1) * BLOCK)
                for h in range(2):
                    src = v_ps[64 * h:64 * h + 64].rearrange("p i m e -> p (i m) e")
                    dst = v_bd[par][64 * h:64 * h + 64].rearrange("p i m h e -> p (i m) h e")[:, :, h, 0:HD]
                    ins = dve.tensor_copy(dst, src)
                ins.then_inc(s_ve, 1)

            def front(b, par, att, slot):
                if att is not None and slot == 4:
                    evacuate_v(b, par)

            def add_bias(n, u, par, t, att):
                dve.wait_ge(s_score, n + 1)
                after(dve, s_pT, 2 * (n - 3))
                if att:
                    dve.wait_ge(s_mb, (n - t) // BLOCK - BLOCKS + 1 if isinstance(n, int) else block_of(n, t) - BLOCKS + 1)
                bias = mbias[par][:, t, :] if att else cst[:, C_DECAY:C_DECAY + SEQ]
                dve.tensor_tensor(logit[u % 4][:, :, :], score_ps[u % 2][:, :, :],
                                  bias.unsqueeze(1).to_broadcast([P, HEADS, SEQ]), ALU.add).then_inc(s_logit, 1)

            cur = [None]

            def block_of(n, t):
                return cur[0]

            def maximum(n, u):
                dve.wait_ge(s_logit, n + 1)
                dve.tensor_reduce(top[u % 4][:, :], logit[u % 4][:, :, :], AX.X, ALU.max).then_inc(s_top, 1)

            def normalise_out(n):
                dve.wait_ge(s_pv, n + 1)
                after(dve, s_norm, n)
                for s in range(2):
                    r = slice(64 * s, 64 * s + 64)
                    dve.reciprocal(rden[r, :, :], o_ps[r, :, s, :, HD]).then_inc(s_rden, 1)
                dve.wait_ge(s_rden, 2 * n + 2)
                for s in range(2):
                    r = slice(64 * s, 64 * s + 64)
                    ins = dve.tensor_tensor(o_sb[r, :, :, :], o_ps[r, :, s, :, 0:HD],
                                            rden[r, :, :].unsqueeze(3).to_broadcast([64, 8, 2, HD]), ALU.mult)
                ins.then_inc(s_norm, 1)

            def residual(n, off):
                dve.wait_ge(s_y, n + 1)
                if isinstance(n, int):
                    x = x_all[:, n % TILES, :]
                else:
                    x = x_all[:, bass.ds(n - off, 1), :].rearrange("p o d -> p (o d)")
                dve.tensor_tensor(x, x, y_ps, ALU.add).then_inc(s_res, 1)

            for slot in range(6):
                front(0, 0, 0, slot)

            def body(block0, att, nxt, first):
                static = isinstance(block0, int)
                for n, u, b, par, t, here, ahead in steps(block0, att, nxt, first):
                    cur[0] = b
                    shift[0] = TILES if att else 0
                    if not (first and u < 3):
                        normalise_out(n - 3)
                    if t == 0 and ahead is not None:
                        normalise(b + 1, 1 - par)
                    add_bias(n, u, par, t, att)
                    if not (first and u < 3):
                        residual(n - 3, TILES if att else 0)
                    maximum(n, u)
                    stats_ahead = not (static and block0 + par + 2 >= 2 * BLOCKS)
                    if stats_ahead:
                        if first and par == 0 and t == 0:
                            dve.wait_ge(s_x[2], 16)
                            dve.wait_ge(s_x[3], 16)
                        if t == 0:
                            dve.wait_ge(s_stat, b + 2)
                        if static:
                            src = x_all[:, ((b + 2) * BLOCK + t) % TILES, :]
                        else:
                            src = x_all[:, bass.ds((b + 2) * BLOCK + t - shift[0], 1), :].rearrange("p o d -> p (o d)")
                        dve.bn_stats(stats[:, t, :], src).then_inc(s_bn, 1)
                        if t == BLOCK - 1:
                            aggregate(b + 2, par)
                    front(b + 1, 1 - par, ahead, 2 * t)
                    front(b + 1, 1 - par, ahead, 2 * t + 1)

            schedule(dve, body, None)
            n = PAIRS
            normalise_out(n - 3)
            residual(n - 3, 0)
            normalise_out(n - 2)
            residual(n - 2, 0)
            normalise_out(n - 1)
            residual(n - 1, 0)

        @block.gpsimd
        def _(pool):
            pool.memset(mhalf[:, :], -0.5).then_inc(s_mhalf, 1)
            pool.memset(sym_at[:, :, :], 0.0).then_inc(s_symz, 1)
            for t in range(4):
                pool.memset(w_qk[t][:, :, :, :, :, :], 0.0).then_inc(s_wz, 1)
            pool.wait_ge(s_mhalf, 1)

            def inverse_deviation(b, par):
                pool.wait_ge(s_stat, b + 1)
                after(pool, s_rstd, b)
                passed(pool, s_passed_g)
                pool.tensor_scalar(vareps[:, :], mv[par][:, :, 1], EPS, 1.0, ALU.add, ALU.mult).then_inc(s_veps, 1)
                pool.wait_ge(s_veps, b + 1)
                after(pool, s_ln, b - 1)
                pool.tensor_tensor(rstd[par][:, :], vareps[:, :], mhalf[:, :], ALU.pow).then_inc(s_rstd, 1)

            def spread_q(b, par):
                pool.wait_ge(s_qe, b + 1)
                after(pool, s_score, (b - 1) * BLOCK)
                passed(pool, s_passed_g)
                for s in range(2):
                    dst = q_bd[par][:, :, :, s, :].rearrange("p g t q -> p (g t) q")
                    ins = pool.tensor_scalar(dst, q_sb[:, :, :, :].rearrange("p g t q -> p (g t) q"),
                                             cst[:, C_SEQ + s:C_SEQ + s + 1], 1.0, ALU.mult, ALU.mult)
                ins.then_inc(s_qbd, 1)

            def spread_k(b, par):
                pool.wait_ge(s_ke, b + 1)
                after(pool, s_score, (b - 1) * BLOCK)
                passed(pool, s_passed_g)
                for h in range(4):
                    dst = k_bd[par][:, :, :, h, :].rearrange("p g t q -> p (g t) q")
                    ins = pool.tensor_scalar(dst, k_sb[:, :, :, :].rearrange("p g t q -> p (g t) q"),
                                             cst[:, C_HEAD + h:C_HEAD + h + 1], 1.0, ALU.mult, ALU.mult)
                ins.then_inc(s_kbd, 1)

            def mask_bias(b, par):
                c = b - BLOCKS
                pool.wait_ge(s_mask[par], (c - par) * 8 + 16)
                after(pool, s_mb, c)
                passed(pool, s_passed_g)
                pool.tensor_scalar(mask_f[:, :, :], mask_in[par][:, :, :], -1.0, -NEG, ALU.add, ALU.mult).then_inc(s_mf, 1)
                pool.wait_ge(s_mf, c + 1)
                pool.wait_ge(s_xbias, 6)
                pool.wait_ge(s_logit, (b - 1) * BLOCK)
                pool.tensor_tensor(mbias[par][:, :, :], mask_f[:, :, :],
                                   xbias[:, :].unsqueeze(1).to_broadcast([P, BLOCK, SEQ]), ALU.add).then_inc(s_mb, 1)

            def front(b, par, att, slot):
                if att is None:
                    return
                if slot == 2:
                    spread_q(b, par)
                elif slot == 3:
                    spread_k(b, par)
                elif slot == 5 and att:
                    mask_bias(b, par)

            def subtract_max(n, u):
                pool.wait_ge(s_top, n + 1)
                pool.tensor_tensor(logit[u % 4][:, :, :], logit[u % 4][:, :, :],
                                   top[u % 4][:, :].unsqueeze(2).to_broadcast([P, HEADS, SEQ]),
                                   ALU.subtract).then_inc(s_sub, 1)

            inverse_deviation(0, 0)
            inverse_deviation(1, 1)
            pool.wait_ge(s_cst, 16)
            for slot in range(6):
                front(0, 0, 0, slot)

            def body(block0, att, nxt, first):
                static = isinstance(block0, int)
                for n, u, b, par, t, here, ahead in steps(block0, att, nxt, first):
                    subtract_max(n, u)
                    front(b + 1, 1 - par, ahead, 2 * t)
                    front(b + 1, 1 - par, ahead, 2 * t + 1)
                    if t == BLOCK - 1 and not (static and block0 + par + 2 >= 2 * BLOCKS):
                        inverse_deviation(b + 2, par)

            schedule(pool, body, None)


def router(nc, a, x_all, cst, sh):
    ctx = ExitStack()
    with ctx:
        def sb(name, shape, dt=F32):
            return ctx.enter_context(nc.sbuf_tensor(name, shape, dt))

        def pb(name, shape):
            return ctx.enter_context(nc.psum_tensor(name, shape, F32))

        def sem(name):
            return ctx.enter_context(nc.semaphore(name))

        E, HI = EXPERTS, 4
        LO = TILES // HI
        BITS = 30
        w_g = sb("w_g", [P, E])
        stats = sb("r_stats", [P, BLOCK, 6])
        mv = [sb(f"r_mv{i}", [P, BLOCK, 2]) for i in range(2)]
        vareps = sb("r_vareps", [P, BLOCK])
        mhalf = sb("r_mhalf", [P, BLOCK])
        rstd = [sb(f"r_rstd{i}", [P, BLOCK]) for i in range(2)]
        xn = [sb(f"r_xn{i}", [P, BLOCK, D]) for i in range(2)]
        xT = [sb(f"r_xT{i}", [P, BLOCK, P]) for i in range(2)]
        logits = sb("logits", [P, TILES, E])
        tmax = sb("tmax", [P, TILES])
        tsum = sb("tsum", [P, TILES])
        prob = sb("prob", [P, HI, LO, E])
        lane = sb("lane", [P, HI * P])
        junk = sb("junk", [P, HI * P])
        bits = sb("bits", [P, BITS + 1], I32)
        count = sb("count", [P, 1])
        thr = sb("thr", [P, 1], I32)
        cand = sb("cand", [P, 1], I32)
        keep = sb("keep", [P, 1], I32)
        above = sb("above", [P, HI * P])
        equal = sb("equal", [P, HI * P])
        rank = sb("rank", [P, HI * P])
        low = sb("low", [P, HI * P])
        tie = sb("tie", [P, HI * P])
        chosen = sb("chosen", [P, HI * P])
        n_above = sb("n_above", [P, 1])
        need = sb("need", [P, 1])
        before = sb("before", [P, 1])
        sel = sb("sel", [P, TILES, E])
        free = sb("free", [P, TILES])
        allow = sb("allow", [P, TILES, E])
        key0 = sb("key0", [P, TILES, E])
        key = sb("key", [P, TILES, E])
        gate = sb("gate", [P, TILES])
        hit = sb("hit", [P, TILES, E])
        hit2 = sb("hit2", [P, TILES, E])
        first = sb("first", [P, TILES])
        onehot = sb("onehot", [P, TILES, E])
        total = sb("total", [P, E, TILES])
        runs = sb("runs", [P, E, TILES])
        excl = sb("excl", [P, E, TILES])
        n_tiles_i = sb("n_tiles_i", [P, E], I32)
        n_tiles_s = sb("n_tiles_s", [P, E], I32)
        n_tiles = sb("n_tiles", [P, E])
        last_tile = sb("last_tile", [P, E])
        base = sb("base", [P, E])
        base2 = sb("base2", [P, E])
        place3 = sb("place3", [P, E, TILES])
        place2 = sb("place2", [P, TILES, E])
        place1 = sb("place1", [P, TILES, E])
        place = sb("place", [P, TILES])
        place_i = sb("place_i", [P, TILES], I32)
        part_i = sb("part_i", [P, 2, TILES], I32)
        part = sb("part", [P, 2, TILES])
        owner = sb("owner", [P, ROUTED, E])
        owner1 = sb("owner1", [P, ROUTED])
        row_is = [sb(f"row_is{i}", [P, P]) for i in range(4)]
        tile_is = [sb(f"tile_is{i}", [P, 2, ROUTED]) for i in range(4)]
        slot_token = sb("slot_token", [P, ROUTED])
        slot_empty = sb("slot_empty", [P, ROUTED])

        xT_ps = [pb(f"xT_ps{i}", [P, BLOCK, P]) for i in range(2)]
        logit_ps = [pb(f"logit_ps{i}", [P, BLOCK, E]) for i in range(2)]
        lane_ps = pb("lane_ps", [P, HI, P])
        count_ps = pb("count_ps", [P, 4])
        rank_ps = pb("rank_ps", [P, TILES, E])
        total_ps = pb("total_ps", [P, TILES, E])
        slot_ps = xT_ps[0][:, 0:2, :].rearrange("p a b -> p (a b)")[:, 0:2 * ROUTED]

        ident = cst[:, C_IDENT:C_IDENT + P]
        same = cst[:, C_SAME:C_SAME + P]

        s_w = sem("r_w")
        s_mh = sem("r_mh")
        s_bn = sem("r_bn")
        s_stat = sem("r_stat")
        s_veps = sem("r_veps")
        s_rstd = sem("r_rstd_s")
        s_ln = sem("r_ln")
        s_xT = sem("r_xTs")
        s_xTe = sem("r_xTe")
        s_lg = sem("r_lg")
        s_lge = sem("r_lge")
        s_st = [sem(f"r_st{i}") for i in range(2)]
        s_stx = sem("r_stx")
        s_sm = sem("r_sm")
        s_exp = sem("r_exp")
        s_shift = sem("r_shift")
        s_prob = sem("r_prob")
        s_lane = sem("r_lane")
        s_cnt = sem("r_cnt")
        s_tot = sem("r_tot")
        s_keep = sem("r_keep")
        s_thr = sem("r_thr")
        s_cand = sem("r_cand")
        s_above = sem("r_above")
        s_above_t = sem("r_above_t")
        s_eq = sem("r_eq")
        s_before = sem("r_before")
        s_chosen = sem("r_chosen")
        s_sel = sem("r_sel")
        s_onehot = sem("r_onehot")
        s_rank = sem("r_rank")
        s_parts = sem("r_parts")
        s_is = sem("r_is")
        s_map = sem("r_map")
        s_tab = sem("r_tab")
        s_passed_g = sem("r_passed_g")
        s_passed_v = sem("r_passed_v")

        rec = a["rec"].rearrange("(t p) c d -> p t c d", p=P)
        UNROLL = 5
        DEPTH = 4

        block = ctx.enter_context(nc.Block())

        @block.sync
        def _(sp):
            sp.dma_start(w_g[:, :], a["L0_ffn_Wg"]).then_inc(s_w, 16)

            def store(b, par):
                sp.dma_start(rec[:, bass.ds(b * BLOCK, BLOCK), 0, :],
                             x_all[:, bass.ds(b * BLOCK, BLOCK), :]).then_inc(s_stx, 16)
                sp.wait_ge(s_ln, b + 1)
                sp.dma_start(rec[:, bass.ds(b * BLOCK, BLOCK), 1, :], xn[par][:, :, :]).then_inc(s_st[par], 16)

            with sp.Fori(0, BLOCKS // 2) as i:
                for par in range(2):
                    store(i * 2 + par, par)
            for par in range(2):
                sp.wait_ge(s_st[par], 16 * (BLOCKS // 2))
            sp.wait_ge(s_stx, 16 * BLOCKS)

        @block.gpsimd
        def _(pool):
            pool.memset(mhalf[:, :], -0.5).then_inc(s_mh, 1)
            pool.wait_ge(s_mh, 1)

            def inverse_deviation(b, par):
                pool.wait_ge(s_stat, b + 1)
                after(pool, s_rstd, b)
                passed(pool, s_passed_g)
                pool.tensor_scalar(vareps[:, :], mv[par][:, :, 1], EPS, 1.0, ALU.add, ALU.mult).then_inc(s_veps, 1)
                pool.wait_ge(s_veps, b + 1)
                pool.tensor_tensor(rstd[par][:, :], vareps[:, :], mhalf[:, :], ALU.pow).then_inc(s_rstd, 1)

            for b in range(2):
                inverse_deviation(b, b)
            with pool.Fori(1, BLOCKS // 2) as i:
                for par in range(2):
                    inverse_deviation(i * 2 + par, par)

        @block.scalar
        def _(act):
            def evacuate(b, par):
                act.wait_ge(s_xT, b + 1)
                after(act, s_lg, b - 1)
                act.activation(xT[par][:, :, :], xT_ps[par][:, :, :], ACT.Copy).then_inc(s_xTe, 1)

            for b in range(2):
                evacuate(b, b)
            with act.Fori(1, BLOCKS // 2) as i:
                for par in range(2):
                    evacuate(i * 2 + par, par)
            act.wait_ge(s_shift, 1)
            act.activation(logits[:, :, :], logits[:, :, :], ACT.Exp).then_inc(s_exp, 1)

        @block.tensor
        def _(pe):
            pe.wait_ge(s_w, 16)

            def tile_block(b, par):
                pe.wait_ge(s_ln, b + 1)
                after(pe, s_xTe, b - 1)
                for t in range(BLOCK):
                    mm = pe.transpose(xT_ps[par][:, t, :], xn[par][:, t, :], ident)
                mm.then_inc(s_xT, 1)
                pe.wait_ge(s_xTe, b + 1)
                after(pe, s_lge, b - 1)
                for t in range(BLOCK):
                    mm = pe.matmul(logit_ps[par][:, t, :], xT[par][:, t, :], w_g[:, :], start=True, stop=True)
                mm.then_inc(s_lg, 1)

            for b in range(2):
                tile_block(b, b)
            with pe.Fori(1, BLOCKS // 2) as i:
                for par in range(2):
                    tile_block(i * 2 + par, par)

            pe.wait_ge(s_prob, 1)
            for h in range(HI):
                mm = pe.transpose(lane_ps[:, h, :], prob[:, h, :, :].rearrange("p l e -> p (l e)"), ident)
            mm.then_inc(s_lane, 1)

            with pe.Fori(0, BITS // UNROLL) as i:
                for k in range(UNROLL):
                    pe.wait_ge(s_cnt, i * UNROLL + (k + 1))
                    pe.matmul(count_ps[:, 0:1], same, count[:, :], start=True, stop=True).then_inc(s_tot, 1)
            pe.wait_ge(s_above, 1)
            pe.matmul(count_ps[:, 1:2], same, n_above[:, :], start=True, stop=True).then_inc(s_above_t, 1)
            pe.wait_ge(s_eq, 2)
            pe.wait_ge(s_above, 2)
            pe.matmul(count_ps[:, 2:3], cst[:, C_BEFORE:C_BEFORE + P], rank[:, HI * P - 1:HI * P],
                      start=True, stop=True).then_inc(s_before, 1)
            pe.wait_ge(s_chosen, 1)
            for h in range(HI):
                mm = pe.transpose(lane_ps[:, h, :], chosen[:, h * P:h * P + P], ident)
            mm.then_inc(s_sel, 1)
            pe.wait_ge(s_onehot, 1)
            pe.matmul(rank_ps[:, :, :], cst[:, C_LOWER:C_LOWER + P], onehot[:, :, :], start=True, stop=True)
            pe.matmul(total_ps[:, :, :], cst[:, C_ONES:C_ONES + P], onehot[:, :, :],
                      start=True, stop=True).then_inc(s_rank, 1)

            def add_tile(n, d, start, stop):
                pe.wait_ge(s_is, n + 1)
                pe.matmul(slot_ps, row_is[d][:, :], tile_is[d][:, :, :].rearrange("p a r -> p (a r)"),
                          start=start, stop=stop).then_inc(s_map, 1)

            for d in range(DEPTH):
                add_tile(d, d, d == 0, False)
            with pe.Fori(1, TILES // DEPTH - 1) as i:
                for d in range(DEPTH):
                    add_tile(i * DEPTH + d, d, False, False)
            for d in range(DEPTH):
                add_tile(TILES - DEPTH + d, d, False, d == DEPTH - 1)

        @block.vector
        def _(dve):
            def stats_block(b, par):
                after(dve, s_stat, b)
                for t in range(BLOCK):
                    dve.bn_stats(stats[:, t, :], x_all[:, bass.ds(b * BLOCK + t, 1), :].rearrange(
                        "p o d -> p (o d)")).then_inc(s_bn, 1)
                dve.wait_ge(s_bn, BLOCK * (b + 1))
                after(dve, s_ln, b - 1)
                passed(dve, s_passed_v)
                for t in range(BLOCK):
                    ins = dve.bn_aggr(mv[par][:, t, :], stats[:, t, :])
                ins.then_inc(s_stat, 1)

            def normalise(b, par):
                dve.wait_ge(s_rstd, b + 1)
                after(dve, s_xT, b - 1)
                after(dve, s_st[par], (b - par) * 8)
                for t in range(BLOCK):
                    x = x_all[:, bass.ds(b * BLOCK + t, 1), :].rearrange("p o d -> p (o d)")
                    ins = dve.tensor_scalar(xn[par][:, t, :], x, mv[par][:, t, 0:1], rstd[par][:, t:t + 1],
                                            ALU.subtract, ALU.mult)
                ins.then_inc(s_ln, 1)

            def take_logits(b, par):
                dve.wait_ge(s_lg, b + 1)
                dve.tensor_copy(logits[:, bass.ds(b * BLOCK, BLOCK), :], logit_ps[par][:, :, :]).then_inc(s_lge, 1)

            stats_block(0, 0)
            stats_block(1, 1)
            normalise(0, 0)
            stats_block(2, 0)
            normalise(1, 1)
            stats_block(3, 1)
            normalise(2, 0)
            take_logits(0, 0)
            with dve.Fori(1, BLOCKS // 2 - 1) as i:
                for par in range(2):
                    b = i * 2 + par + 2
                    stats_block(b, par)
                    normalise(b - 1, 1 - par)
                    take_logits(b - 3, 1 - par)
            normalise(BLOCKS - 1, 1)
            for b in range(BLOCKS - 3, BLOCKS):
                take_logits(b, b % 2)

            chain = [0]

            def link(ins):
                chain[0] += 1
                ins.then_inc(s_sm, 1)
                dve.wait_ge(s_sm, chain[0])

            def by_tile(x):
                return x.unsqueeze(2).to_broadcast([P, TILES, E])

            dve.wait_ge(s_lge, BLOCKS)
            link(dve.tensor_reduce(tmax[:, :], logits[:, :, :], AX.X, ALU.max))
            dve.tensor_tensor(logits[:, :, :], logits[:, :, :], by_tile(tmax[:, :]), ALU.subtract).then_inc(s_shift, 1)
            dve.wait_ge(s_exp, 1)
            link(dve.tensor_reduce(tsum[:, :], logits[:, :, :], AX.X, ALU.add))
            link(dve.reciprocal(tsum[:, :], tsum[:, :]))
            dve.tensor_tensor(prob[:, :, :, :].rearrange("p h l e -> p l h e"),
                              logits[:, :, :].rearrange("p (l h) e -> p l h e", h=HI),
                              tsum[:, :].rearrange("p (l h) -> p l h", h=HI).unsqueeze(3).to_broadcast([P, LO, HI, E]),
                              ALU.mult).then_inc(s_prob, 1)

            bits_f = cst[:, C_BITS:C_BITS + BITS + 1]
            link(dve.tensor_copy(bits[:, :], bits_f))
            link(dve.memset(thr[:, :], 0))
            dve.tensor_copy(cand[:, :], bits[:, 0:1]).then_inc(s_cand, 1)
            dve.wait_ge(s_lane, 1)
            link(dve.tensor_copy(lane[:, :], lane_ps[:, :, :].rearrange("p h t -> p (h t)")))
            with dve.Fori(0, BITS // UNROLL) as i:
                for k in range(UNROLL):
                    n = i * UNROLL + k
                    dve.wait_ge(s_cand, n + 1)
                    dve.tensor_scalar(junk[:, :], lane[:, :], cand[:, :].bitcast(F32), None, ALU.is_ge, ALU.add,
                                      accum_out=count[:, :]).then_inc(s_cnt, 1)
                    dve.wait_ge(s_tot, n + 1)
                    dve.tensor_scalar(keep[:, :], count_ps[:, 0:1], float(CAP), bits_f[:, bass.ds(n, 1)],
                                      ALU.is_ge, ALU.mult).then_inc(s_keep, 1)
                    dve.wait_ge(s_keep, n + 1)
                    dve.tensor_tensor(thr[:, :], thr[:, :], keep[:, :], ALU.bitwise_or).then_inc(s_thr, 1)
                    dve.wait_ge(s_thr, n + 1)
                    dve.tensor_tensor(cand[:, :], thr[:, :], bits[:, bass.ds(n + 1, 1)],
                                      ALU.bitwise_or).then_inc(s_cand, 1)
            dve.wait_ge(s_cand, BITS + 1)
            level = thr[:, :].bitcast(F32)
            dve.tensor_scalar(above[:, :], lane[:, :], level, None, ALU.is_gt, ALU.add,
                              accum_out=n_above[:, :]).then_inc(s_above, 1)
            dve.tensor_scalar(equal[:, :], lane[:, :], level, None, ALU.is_equal).then_inc(s_eq, 1)
            dve.wait_ge(s_above_t, 1)
            dve.tensor_scalar(need[:, :], count_ps[:, 1:2], -1.0, float(CAP), ALU.mult, ALU.add).then_inc(s_above, 1)
            dve.wait_ge(s_eq, 1)
            link(dve.memset(junk[:, :], 1.0))
            dve.tensor_tensor_scan(rank[:, :], junk[:, :], equal[:, :], 0.0, ALU.mult, ALU.add).then_inc(s_eq, 1)
            dve.wait_ge(s_before, 1)
            dve.wait_ge(s_eq, 2)
            dve.wait_ge(s_above, 2)
            link(dve.tensor_copy(before[:, :], count_ps[:, 2:3]))
            link(dve.tensor_scalar(low[:, :], rank[:, :], before[:, :], need[:, :], ALU.add, ALU.is_le))
            link(dve.tensor_tensor(tie[:, :], equal[:, :], low[:, :], ALU.mult))
            dve.tensor_tensor(chosen[:, :], above[:, :], tie[:, :], ALU.add).then_inc(s_chosen, 1)

            pr = prob[:, :, :, :].rearrange("p h l e -> p (h l) e")
            dve.wait_ge(s_sel, 1)
            link(dve.tensor_copy(sel[:, :, :].rearrange("p t e -> p (t e)"), lane_ps[:, :, :].rearrange("p h t -> p (h t)")))
            link(dve.tensor_reduce(first[:, :], sel[:, :, :], AX.X, ALU.max))
            link(dve.tensor_scalar(free[:, :], first[:, :], -1.0, 1.0, ALU.mult, ALU.add))
            link(dve.tensor_tensor(allow[:, :, :], sel[:, :, :], by_tile(free[:, :]), ALU.max))
            link(dve.tensor_tensor(key0[:, :, :], pr, allow[:, :, :], ALU.mult))
            link(dve.scalar_tensor_tensor(out=key[:, :, :], in0=allow[:, :, :], scalar=-1.0, in1=key0[:, :, :],
                                          op0=ALU.add, op1=ALU.add))
            link(dve.tensor_reduce(gate[:, :], key[:, :, :], AX.X, ALU.max))
            link(dve.tensor_tensor(hit[:, :, :], key[:, :, :], by_tile(gate[:, :]), ALU.is_equal))
            link(dve.tensor_tensor(hit2[:, :, :], hit[:, :, :],
                                   cst[:, C_REST:C_RUN].rearrange("p (t e) -> p t e", e=E), ALU.mult))
            link(dve.tensor_reduce(first[:, :], hit2[:, :, :], AX.X, ALU.max))
            dve.tensor_tensor(onehot[:, :, :], hit2[:, :, :], by_tile(first[:, :]), ALU.is_equal).then_inc(s_onehot, 1)

            dve.wait_ge(s_rank, 1)
            dve.wait_ge(s_onehot, 1)
            link(dve.tensor_copy(total[:, :, :], total_ps[:, :, :].rearrange("p t e -> p e t")))
            link(dve.tensor_tensor_scan(runs[:, :, :].rearrange("p e t -> p (e t)"), cst[:, C_RUN:C_TOKEN],
                                        total[:, :, :].rearrange("p e t -> p (e t)"), 0.0, ALU.mult, ALU.add))
            link(dve.tensor_tensor(excl[:, :, :], runs[:, :, :], total[:, :, :], ALU.subtract))
            link(dve.tensor_scalar(n_tiles_i[:, :], runs[:, :, TILES - 1], float(P - 1), None, ALU.add))
            link(dve.tensor_scalar(n_tiles_s[:, :], n_tiles_i[:, :], 7, None, ALU.logical_shift_right))
            link(dve.tensor_copy(n_tiles[:, :], n_tiles_s[:, :]))
            link(dve.tensor_tensor_scan(last_tile[:, :], cst[:, C_ONES:C_ONES + E], n_tiles[:, :], 0.0, ALU.mult, ALU.add))
            link(dve.tensor_tensor(base2[:, :], last_tile[:, :], n_tiles[:, :], ALU.subtract))
            link(dve.tensor_scalar(base[:, :], base2[:, :], float(P), None, ALU.mult))
            link(dve.tensor_tensor(place3[:, :, :], excl[:, :, :], base[:, :].unsqueeze(2).to_broadcast([P, E, TILES]),
                                   ALU.add))
            link(dve.tensor_tensor(place2[:, :, :], rank_ps[:, :, :], place3[:, :, :].rearrange("p e t -> p t e"), ALU.add))
            link(dve.tensor_tensor(place1[:, :, :], place2[:, :, :], onehot[:, :, :], ALU.mult))
            link(dve.tensor_reduce(place[:, :], place1[:, :, :], AX.X, ALU.add))
            link(dve.tensor_copy(place_i[:, :], place[:, :]))
            dve.tensor_scalar(part_i[:, 0, :], place_i[:, :], 7, None, ALU.logical_shift_right)
            link(dve.tensor_scalar(part_i[:, 1, :], place_i[:, :], P - 1, None, ALU.bitwise_and))
            dve.tensor_copy(part[:, :, :], part_i[:, :, :]).then_inc(s_parts, 1)
            dve.wait_ge(s_parts, 1)

            def one_tile(n, d):
                after(dve, s_map, n - (DEPTH - 1))
                at = bass.ds(n, 1)
                dve.tensor_scalar(row_is[d][:, :], cst[:, C_IOTA:C_IOTA + P], part[:, 1, at], None, ALU.is_equal)
                tile = part[:, 0, at]
                dve.tensor_scalar(tile_is[d][:, 0, :], cst[:, C_IOTA:C_IOTA + ROUTED], tile,
                                  cst[:, bass.ds(n + C_TOKEN, 1)], ALU.is_equal, ALU.mult)
                dve.tensor_scalar(tile_is[d][:, 1, :], cst[:, C_IOTA:C_IOTA + ROUTED], tile, gate[:, at],
                                  ALU.is_equal, ALU.mult).then_inc(s_is, 1)

            for d in range(DEPTH):
                one_tile(d, d)
            with dve.Fori(1, TILES // DEPTH) as i:
                for d in range(DEPTH):
                    one_tile(i * DEPTH + d, d)

            link(dve.tensor_tensor(owner[:, :, :], last_tile[:, :].unsqueeze(1).to_broadcast([P, ROUTED, E]),
                                   cst[:, C_IOTA:C_IOTA + ROUTED].unsqueeze(2).to_broadcast([P, ROUTED, E]), ALU.is_le))
            link(dve.tensor_reduce(owner1[:, :], owner[:, :, :], AX.X, ALU.add))
            link(dve.tensor_scalar(sh["expert_of"][:, :], owner1[:, :], float(E - 1), None, ALU.min))
            dve.wait_ge(s_map, TILES)
            dve.tensor_copy(sh["gate_of"][:, :], slot_ps[:, ROUTED:2 * ROUTED]).then_inc(s_tab, 1)
            link(dve.tensor_copy(slot_token[:, :], slot_ps[:, 0:ROUTED]))
            dve.tensor_scalar(sh["gather_at"][:, :], slot_token[:, :], -1.0, 0.0, ALU.add, ALU.max).then_inc(s_tab, 1)
            link(dve.tensor_scalar(slot_empty[:, :], slot_token[:, :], 0.0, float(TOKENS + 1), ALU.is_equal, ALU.mult))
            link(dve.scalar_tensor_tensor(out=sh["scatter_at"][:, :], in0=slot_token[:, :], scalar=-1.0,
                                          in1=slot_empty[:, :], op0=ALU.add, op1=ALU.add))
            dve.wait_ge(s_tab, 2)


def experts(nc, a, cst, sh):
    ctx = ExitStack()
    with ctx:
        def sb(name, shape, dt=F32):
            return ctx.enter_context(nc.sbuf_tensor(name, shape, dt))

        def pb(name, shape):
            return ctx.enter_context(nc.psum_tensor(name, shape, F32))

        def sem(name):
            return ctx.enter_context(nc.semaphore(name))

        DEPTH = 4
        FC = FF // P
        assert ROUTED % DEPTH == 0
        w1 = [sb(f"w1_{i}", [P, FF]) for i in range(DEPTH)]
        w2 = [sb(f"w2_{i}", [P, FC, D]) for i in range(DEPTH)]
        gat = [sb(f"gat{i}", [P, 1], I32) for i in range(DEPTH)]
        sca = [sb(f"sca{i}", [P, 1], I32) for i in range(DEPTH)]
        xr = [sb(f"xr{i}", [P, 2, D]) for i in range(DEPTH)]
        xT = [sb(f"f_xT{i}", [P, P]) for i in range(2)]
        hT = [sb(f"hT{i}", [P, FC, P]) for i in range(2)]
        res = [sb(f"res{i}", [P, D]) for i in range(DEPTH)]
        xT_ps = [pb(f"f_xT_ps{i}", [P, P]) for i in range(2)]
        h_ps = [pb(f"h_ps{i}", [P, FC, P]) for i in range(2)]
        y_ps = [pb(f"f_y_ps{i}", [P, D]) for i in range(2)]
        ident = cst[:, C_IDENT:C_IDENT + P]

        s_wt = [sem(f"f_wt{i}") for i in range(DEPTH)]
        s_idx = sem("f_idx")
        s_gat = [sem(f"f_gat{i}") for i in range(DEPTH)]
        s_xT = sem("f_xTs")
        s_xTe = sem("f_xTe")
        s_h = sem("f_h")
        s_gelu = sem("f_gelu")
        s_y = sem("f_y")
        s_res = sem("f_res")
        s_sca = [sem(f"f_sca{i}") for i in range(DEPTH)]
        s_passed_s = sem("f_passed_s")
        s_passed_g = sem("f_passed_g")

        rec = a["rec"].rearrange("t c d -> t (c d)")
        w1_dram = a["L0_ffn_W1"].rearrange("e d f -> (e d) f")
        w2_dram = a["L0_ffn_W2"].rearrange("e (c f) d -> e f c d", f=P)

        block = ctx.enter_context(nc.Block())

        def over(engine, body):
            for d in range(DEPTH):
                body(d, d)
            with engine.Fori(1, ROUTED // DEPTH) as i:
                for d in range(DEPTH):
                    body(i * DEPTH + d, d)

        def landed(n, d):
            return (n - d) * (16 // DEPTH) + 16

        @block.sync
        def _(sp):
            def load(n, d):
                after(sp, s_y, n - (DEPTH - 1))
                passed(sp, s_passed_s)
                e = sp.value_load(sh["expert_of"][0:1, bass.ds(n, 1)], min_val=0, max_val=EXPERTS - 1)
                sp.dma_start(w1[d][:, :], w1_dram[bass.ds(e * P, P), :]).then_inc(s_wt[d], 16)
                sp.dma_start(w2[d][:, :, :], w2_dram[bass.ds(e, 1), :, :, :].rearrange("o f c d -> (o f) c d")).then_inc(
                    s_wt[d], 16)

            over(sp, load)

        @block.gpsimd
        def _(pool):
            def gather(n, d):
                pool.wait_ge(s_idx, n + 1)
                after(pool, s_res, n - (DEPTH - 1))
                passed(pool, s_passed_g)
                pool.indirect_dma_start(xr[d][:, :, :].rearrange("p c d -> p (c d)"), None, rec,
                                        bass.IndirectOffsetOnAxis(ap=gat[d][:, :].bitcast(U32), axis=0)).then_inc(s_gat[d], 16)

            def scatter(n, d):
                pool.wait_ge(s_res, n + 1)
                passed(pool, s_passed_g)
                pool.indirect_dma_start(a["out"], bass.IndirectOffsetOnAxis(ap=sca[d][:, :].bitcast(U32), axis=0),
                                        res[d][:, :], None, bounds_check=TOKENS - 1, oob_is_err=False).then_inc(s_sca[d], 16)

            AHEAD = 3
            for n in range(AHEAD):
                gather(n, n)
            for d in range(DEPTH):
                gather(d + AHEAD, (d + AHEAD) % DEPTH)
                scatter(d, d)
            with pool.Fori(1, ROUTED // DEPTH - 1) as i:
                for d in range(DEPTH):
                    gather(i * DEPTH + d + AHEAD, (d + AHEAD) % DEPTH)
                    scatter(i * DEPTH + d, d)
            for d in range(DEPTH):
                n = ROUTED - DEPTH + d
                if n + AHEAD < ROUTED:
                    gather(n + AHEAD, (n + AHEAD) % DEPTH)
                scatter(n, d)
            for d in range(DEPTH):
                pool.wait_ge(s_sca[d], 16 * (ROUTED // DEPTH))

        @block.tensor
        def _(pe):
            def turn(n, d):
                pe.wait_ge(s_gat[d], landed(n, d))
                after(pe, s_xTe, n - 1)
                pe.transpose(xT_ps[d % 2][:, :], xr[d][:, 1, :], ident).then_inc(s_xT, 1)

            def up(n, d):
                pe.wait_ge(s_wt[d], landed(n, d) * 2)
                pe.wait_ge(s_xTe, n + 1)
                after(pe, s_gelu, n - 1)
                for c in range(FC):
                    mm = pe.matmul(h_ps[d % 2][:, c, :], w1[d][:, c * P:c * P + P], xT[d % 2][:, :], start=True, stop=True)
                mm.then_inc(s_h, 1)

            def down(n, d):
                pe.wait_ge(s_gelu, n + 1)
                after(pe, s_res, n - 1)
                for c in range(FC):
                    mm = pe.matmul(y_ps[d % 2][:, :], hT[d % 2][:, c, :], w2[d][:, c, :], start=(c == 0), stop=(c == FC - 1))
                mm.then_inc(s_y, 1)

            def tile(n, d, next_):
                if next_:
                    turn(n + 1, (d + 1) % DEPTH)
                if not (isinstance(n, int) and n == 0):
                    down(n - 1, (d - 1) % DEPTH)
                up(n, d)

            turn(0, 0)
            for d in range(DEPTH):
                tile(d, d, True)
            with pe.Fori(1, ROUTED // DEPTH - 1) as i:
                for d in range(DEPTH):
                    tile(i * DEPTH + d, d, True)
            for d in range(DEPTH):
                tile(ROUTED - DEPTH + d, d, d < DEPTH - 1)
            down(ROUTED - 1, DEPTH - 1)

        @block.scalar
        def _(act):
            def gelu(n, d):
                act.wait_ge(s_h, n + 1)
                after(act, s_y, n - 1)
                act.activation(hT[d % 2][:, :, :], h_ps[d % 2][:, :, :], ACT.Gelu).then_inc(s_gelu, 1)

            over(act, gelu)

        @block.vector
        def _(dve):
            def indices(n, d):
                if not (isinstance(n, int) and n < DEPTH):
                    dve.wait_ge(s_gat[d], landed(n, d) - 16)
                    dve.wait_ge(s_sca[d], landed(n, d) - 16)
                dve.tensor_copy(sca[d][:, :], sh["scatter_at"][:, bass.ds(n, 1)])
                dve.tensor_copy(gat[d][:, :], sh["gather_at"][:, bass.ds(n, 1)]).then_inc(s_idx, 1)

            def evacuate(n, d):
                dve.wait_ge(s_xT, n + 1)
                after(dve, s_h, n - 1)
                dve.tensor_copy(xT[d % 2][:, :], xT_ps[d % 2][:, :]).then_inc(s_xTe, 1)

            def weigh(n, d):
                dve.wait_ge(s_y, n + 1)
                dve.scalar_tensor_tensor(out=res[d][:, :], in0=y_ps[d % 2][:, :], scalar=sh["gate_of"][:, bass.ds(n, 1)],
                                         in1=xr[d][:, 0, :], op0=ALU.mult, op1=ALU.add).then_inc(s_res, 1)

            for d in range(DEPTH):
                indices(d, d)
            evacuate(0, 0)
            evacuate(1, 1)
            def step(n, d, ahead2, ahead4):
                if ahead2:
                    pass
                weigh(n, d)
                if ahead4:
                    indices(n + DEPTH, d)
                if ahead2:
                    evacuate(n + 2, (d + 2) % DEPTH)

            with dve.Fori(0, ROUTED // DEPTH - 1) as i:
                for d in range(DEPTH):
                    step(i * DEPTH + d, d, True, True)
            for d in range(DEPTH):
                step(ROUTED - DEPTH + d, d, d < 2, False)


_INS = ['x', 'ctx_1024', 'mask_Bx1xSxS2_bf1', 'L0_attn_bq', 'L0_attn_bk', 'L0_attn_bv', 'L0_attn_bo',
        'L0_xattn_Wsym', 'L0_xattn_Wq', 'L0_xattn_bq', 'L0_xattn_Wk', 'L0_xattn_bk', 'L0_xattn_Wv', 'L0_xattn_bv',
        'L0_xattn_Wo', 'L0_xattn_bo', 'L0_xattn_distance_scale', 'L0_xattn_parity_strength',
        'L0_xattn_localization_length', 'L0_ffn_Wg', 'L0_ffn_W1', 'L0_ffn_W2']


def layout(inputs):
    import numpy as np

    arrays = {n: np.ascontiguousarray(inputs[n]) for n in _INS}
    arrays['mask_Bx1xSxS2_bf1'] = arrays['mask_Bx1xSxS2_bf1'].view(np.uint8)
    for n in "qkvo":
        arrays[f"attn_W{n}T"] = np.ascontiguousarray(np.asarray(inputs[f"L0_attn_W{n}"]).T)
    arrays["cst"], arrays["rows"] = constants()
    return arrays


def declare(nc, arrays, stop_after=3):
    args = {n: nc.dram_tensor(f"in_{n}", v.shape, mybir.dt.from_np(v.dtype), kind="ExternalInput").ap()
            for n, v in arrays.items()}
    if stop_after < 3:
        args["x3"] = nc.dram_tensor("x3", [TOKENS, D], F32, kind="ExternalOutput").ap()
    args["rec"] = nc.dram_tensor("rec", [TOKENS, 2, D], F32, kind="Internal").ap()
    args["out"] = nc.dram_tensor("out", [TOKENS, D], F32, kind="ExternalOutput").ap()
    build(nc, args, stop_after)


def kernel(**inputs):
    import concourse.bacc as bacc
    from concourse.bass_utils import run_bass_kernel_spmd

    arrays = layout(inputs)
    nc = bacc.Bacc("TRN2", target_bir_lowering=False, num_devices=1)
    declare(nc, arrays)
    r = run_bass_kernel_spmd(nc, [{f"in_{n}": v for n, v in arrays.items()}], core_ids=[0])
    return r.results[0]["out"].reshape(BATCH, SEQ, D)
```

```python
from contextlib import ExitStack

import concourse.bass as bass
from concourse import mybir
from concourse.alu_op_type import AluOpType as ALU

ACT = mybir.ActivationFunctionType
F32 = mybir.dt.float32
BF16 = mybir.dt.bfloat16
I32 = mybir.dt.int32
U32 = mybir.dt.uint32
U8 = mybir.dt.uint8
AX = mybir.AxisListType

P = 128
BATCH, SEQ, D = 128, 64, 128
HEADS = 16
HD = D // HEADS
TOKENS = BATCH * SEQ
TILES = TOKENS // P
BLOCK = 4
BLOCKS = TILES // BLOCK
EXPERTS = 8
FF = 256
CAP = TOKENS // EXPERTS
SYM = 64
EPS = 1e-5
NEG = -(2.0 ** 100)
ROUTED = -(-(TILES + EXPERTS - 1) // 8) * 8

C_IDENT = 0
C_HEAD = C_IDENT + P
C_DECAY = C_HEAD + 4
C_DIST = C_DECAY + SEQ
C_PARITY = C_DIST + SEQ
C_SAME = C_PARITY + SEQ
C_BEFORE = C_SAME + P
C_LOWER = C_BEFORE + P
C_ONES = C_LOWER + P
C_IOTA = C_ONES + P
C_REST = C_IOTA + P
C_RUN = C_REST + EXPERTS * TILES
C_TOKEN = C_RUN + EXPERTS * TILES
C_BITS = C_TOKEN + TILES
C_COLS = C_BITS + 31


def constants():
    import numpy as np

    c = np.zeros((P, C_COLS), np.float32)
    p = np.arange(P)
    c[:, C_IDENT:C_IDENT + P] = np.eye(P)
    c[p, C_HEAD + (p // HD) % 4] = 1.0
    q, k = np.arange(P)[:, None] % SEQ, np.arange(SEQ)[None, :]
    c[:, C_DECAY:C_DECAY + SEQ] = np.where(k <= q, k - q, NEG)
    c[:, C_DIST:C_DIST + SEQ] = abs(q - k)
    c[:, C_PARITY:C_PARITY + SEQ] = 1.0 - 2.0 * ((q + k) % 2)
    same = (p[:, None] % EXPERTS) == (p[None, :] % EXPERTS)
    c[:, C_SAME:C_SAME + P] = same
    c[:, C_BEFORE:C_BEFORE + P] = same & (p[:, None] < p[None, :])
    c[:, C_LOWER:C_LOWER + P] = p[:, None] < p[None, :]
    c[:, C_ONES:C_ONES + P] = 1.0
    c[:, C_IOTA:C_IOTA + P] = p[None, :]
    c[:, C_REST:C_RUN] = np.tile(EXPERTS - np.arange(EXPERTS), TILES)[None, :]
    c[:, C_RUN:C_TOKEN] = np.tile(np.arange(TILES) > 0, EXPERTS)[None, :]
    place = np.arange(TILES)
    c[:, C_TOKEN:C_BITS] = ((place % 16) * 4 + place // 16)[None, :] * P + p[:, None] + 1
    c[:, C_BITS:C_BITS + 30] = 2.0 ** np.arange(29, -1, -1)[None, :]
    rows = np.ones((6, BLOCK * P), np.float32)
    rows[3:] = np.arange(BLOCK * P)[None, :] % 2
    return c, rows


NAMES = ["q", "k", "v", "o"]


def after(engine, semaphore, value):
    if isinstance(value, int) and value <= 0:
        return
    engine.wait_ge(semaphore, value)


def passed(engine, semaphore):
    engine.sem_inc(semaphore, 1)


def build(nc, a, stop_after=3):
    ctx = ExitStack()
    with ctx:
        def sb(name, shape, dt=F32):
            return ctx.enter_context(nc.sbuf_tensor(name, shape, dt))

        def sem(name):
            return ctx.enter_context(nc.semaphore(name))

        x_all = sb("x_all", [P, TILES, D])
        cst = sb("cst", [P, C_COLS])
        w1 = sb("w1", [P, EXPERTS * FF // P, P])
        w2 = sb("w2", [P, EXPERTS * FF // P, D])
        s_we = sem("s_we")
        attention(nc, a, x_all, cst, w1, w2, s_we)
        if stop_after >= 2:
            sh = dict(
                gate_of=sb("gate_of", [P, ROUTED]),
                expert_of=sb("expert_of", [P, ROUTED], I32),
                gather_at=sb("gather_at", [P, ROUTED], I32),
                scatter_at=sb("scatter_at", [P, ROUTED], I32),
                w1=w1, w2=w2,
            )
            router(nc, a, x_all, cst, sh)
            if stop_after >= 3:
                experts(nc, a, cst, sh)


def attention(nc, a, x_all, cst, w1, w2, s_we):
    ctx = ExitStack()
    with ctx:
        def sb(name, shape, dt=F32):
            return ctx.enter_context(nc.sbuf_tensor(name, shape, dt))

        def pb(name, shape):
            return ctx.enter_context(nc.psum_tensor(name, shape, F32))

        def sem(name):
            return ctx.enter_context(nc.semaphore(name))

        w_in = sb("w_in", [P, 2, 4, D])
        w_v, w_o = w_in[:, :, 2, :], w_in[:, :, 3, :]
        w_sym = sb("w_sym", [SYM, 3, D])
        sym_in = sb("sym_in", [SYM, 1])
        sym_at = sb("sym_at", [SYM, 3, EXPERTS])
        tab = sb("tab", [8, 2, D])
        rem1 = sb("rem1", [8, 2, D])
        rem2 = sb("rem2", [8, 2, D])
        split = sb("split", [8, 2, 3, D], BF16)
        bt = sb("bt", [6, 8, D], BF16)
        rows32 = sb("rows32", [6, BLOCK * P])
        rows = sb("rows", [6, BLOCK * P], BF16)
        scal = sb("scal", [P, 3])
        sc = sb("sc", [P, 4])
        xbias = sb("xbias", [P, SEQ])
        xb1 = sb("xb1", [P, SEQ])
        xb2 = sb("xb2", [P, SEQ])
        xb3 = sb("xb3", [P, SEQ])

        ctx_in = [sb(f"ctx_in{i}", [P, BLOCK, D]) for i in range(2)]
        mask_in = [sb(f"mask_in{i}", [P, BLOCK, SEQ], U8) for i in range(2)]
        mask_f = sb("mask_f", [P, BLOCK, SEQ])
        mbias = [sb(f"mbias{i}", [P, BLOCK, SEQ]) for i in range(2)]
        stats = sb("stats", [P, BLOCK, 6])
        mv = [sb(f"mv{i}", [P, BLOCK, 2]) for i in range(2)]
        vareps = sb("vareps", [P, BLOCK])
        mhalf = sb("mhalf", [P, BLOCK])
        rstd = [sb(f"rstd{i}", [P, BLOCK]) for i in range(2)]
        xn = sb("xn", [P, BLOCK, D])
        xT = sb("xT", [P, BLOCK, 2, SEQ])
        cT = sb("cT", [P, BLOCK, 2, SEQ])
        k_sb = sb("k_sb", [P, 2, BLOCK, SEQ])
        q_bd = [sb(f"q_bd{i}", [P, 2, BLOCK, 2, SEQ]) for i in range(2)]
        k_bd = [sb(f"k_bd{i}", [P, 2, BLOCK, 4, SEQ]) for i in range(2)]
        v_bd = [sb(f"v_bd{i}", [P, 2 * BLOCK, 8, 2, HD + 1]) for i in range(2)]
        logit = [sb(f"logit{i}", [P, HEADS, SEQ]) for i in range(4)]
        top = [sb(f"top{i}", [P, HEADS]) for i in range(4)]
        probT = [sb(f"probT{i}", [P, 8, P]) for i in range(2)]
        o_sb = sb("o_sb", [P, 8, 2, HD])
        oT = sb("oT", [P, P])
        rden = sb("rden", [P, 8, 2])

        score_ps = [pb(f"score_ps{i}", [P, HEADS, SEQ]) for i in range(2)]
        probT_ps = pb("probT_ps", [P, 8, P])
        front_ps = pb("front_ps", [P, BLOCK, P])
        v_ps = front_ps[:, :, :].rearrange("p t (s m e) -> p (t s) m e", s=2, m=8)
        out_ps = pb("out_ps", [P, 512])
        o_ps = out_ps[:, 0:288].rearrange("p (m s h e) -> p m s h e", m=8, s=2, h=2)
        oT_ps = out_ps[:, 288:288 + P]
        y_ps = out_ps[:, 288:288 + D]

        ident = cst[:, C_IDENT:C_IDENT + P]

        s_cst = sem("s_cst")
        s_x = [sem(f"s_x{i}") for i in range(4)]
        s_qz = sem("s_qz")
        s_w = [sem(f"s_w{i}") for i in range(2)]
        s_small = sem("s_small")
        s_symz = sem("s_symz")
        s_sym = sem("s_sym")
        s_symps = sem("s_symps")
        s_tab = sem("s_tab")
        s_split = sem("s_split")
        s_bt = sem("s_bt")
        s_rows = sem("s_rows")
        s_xbias = sem("s_xbias")
        s_xba = sem("s_xba")
        s_vz = sem("s_vz")
        s_mhalf = sem("s_mhalf")
        s_ctx = [sem(f"s_ctx{i}") for i in range(2)]
        s_mask = [sem(f"s_mask{i}") for i in range(2)]
        s_bn = sem("s_bn")
        s_stat = sem("s_stat")
        s_veps = sem("s_veps")
        s_rstd = sem("s_rstd")
        s_ln = sem("s_ln")
        s_xT = sem("s_xT")
        s_xTe = sem("s_xTe")
        s_cT = sem("s_cT")
        s_cTe = sem("s_cTe")
        s_q = sem("s_q")
        s_qe = sem("s_qe")
        s_k = sem("s_k")
        s_ke = sem("s_ke")
        s_v = sem("s_v")
        s_ve = sem("s_ve")
        s_kbd = sem("s_kbd")
        s_mf = sem("s_mf")
        s_mb = sem("s_mb")
        s_score = sem("s_score")
        s_logit = sem("s_logit")
        s_top = sem("s_top")
        s_sub = sem("s_sub")
        s_prob = sem("s_prob")
        s_pT = sem("s_pT")
        s_pTe = sem("s_pTe")
        s_pv = sem("s_pv")
        s_rden = sem("s_rden")
        s_norm = sem("s_norm")
        s_oT = sem("s_oT")
        s_oTe = sem("s_oTe")
        s_y = sem("s_y")
        s_res = sem("s_res")
        s_st = sem("s_st")
        s_passed_v = sem("s_passed_v")
        s_passed_g = sem("s_passed_g")
        s_passed_s = sem("s_passed_s")

        x_dram = a["x"].rearrange("b s d -> (b s) d").rearrange("(t p) d -> p t d", p=P)
        ctx_dram = a["ctx_1024"].rearrange("b s d -> (b s) d").rearrange("(t p) d -> p t d", p=P)
        mask_dram = a["mask_Bx1xSxS2_bf1"].rearrange("b o q k -> (b o q) k").rearrange("(t p) k -> p t k", p=P)

        X_CHUNKS = [(0, 1), (1, 2), (2, 4), (4, BLOCKS)]
        N_SMALL = 5

        PAIRS = 2 * TILES
        HALF = 2
        ITERS = 2 * BLOCKS // HALF
        MID = ITERS // 2

        def schedule(engine, body, step):
            body(0, 0, 0, True)
            with engine.Fori(1, MID - 1) as it:
                body(it * HALF, 0, 0, False)
            body((MID - 1) * HALF, 0, 1, False)
            body(MID * HALF, 1, 1, False)
            with engine.Fori(MID + 1, ITERS - 1) as it:
                body(it * HALF, 1, 1, False)
            body((ITERS - 1) * HALF, 1, None, False)

        def steps(block0, att, nxt, first):
            for u in range(HALF * BLOCK):
                h = u // BLOCK
                ahead = att if h == 0 else nxt
                yield block0 * BLOCK + u, u, block0 + h, h, u % BLOCK, att, ahead

        block = ctx.enter_context(nc.Block())

        @block.sync
        def _(sp):
            def load_x(i):
                b0, b1 = X_CHUNKS[i]
                sp.dma_start(x_all[:, b0 * BLOCK:b1 * BLOCK, :], x_dram[:, b0 * BLOCK:b1 * BLOCK, :]).then_inc(s_x[i], 16)

            load_x(0)
            sp.dma_start(cst[:, 0:C_SAME], a["cst"][:, 0:C_SAME]).then_inc(s_cst, 16)
            sp.dma_start(tab[:, 0, :], a["biases"]).then_inc(s_small, 16)
            sp.dma_start(rows32[:, :], a["rows"]).then_inc(s_small, 16)
            sp.dma_start(scal[:, :], a["scalars"].rearrange("(o c) -> o c", o=1).to_broadcast([P, 3])).then_inc(s_small, 16)
            sp.dma_start(w_sym[:, :, :], a["w_sym"]).then_inc(s_small, 16)
            sp.dma_start(sym_in[:, :], a["L0_xattn_Wsym"].rearrange("o d -> d o")).then_inc(s_small, 16)
            sp.dma_start(w_in[:, 0, :, :], a["w_self"]).then_inc(s_w[0], 16)
            load_x(1)
            sp.wait_ge(s_split, 5)
            for c in range(2):
                for part in range(3):
                    sp.dma_start(bt[c * 3 + part:c * 3 + part + 1, :, :], split[:, c, part, :]).then_inc(s_bt, 16)

            load_x(2)
            sp.dma_start(w_in[:, 1, :, :], a["w_cross"]).then_inc(s_w[1], 16)
            load_x(3)
            sp.dma_start(cst[:, C_SAME:C_COLS], a["cst"][:, C_SAME:C_COLS]).then_inc(s_cst, 16)

            def load(c, par):
                after(sp, s_cT, c - 1)
                sp.dma_start(ctx_in[par][:, :, :], ctx_dram[:, bass.ds(c * BLOCK, BLOCK), :]).then_inc(s_ctx[par], 16)
                after(sp, s_mf, c - 1)
                passed(sp, s_passed_s)
                sp.dma_start(mask_in[par][:, :, :], mask_dram[:, bass.ds(c * BLOCK, BLOCK), :]).then_inc(s_mask[par], 16)

            for c in range(2):
                load(c, c)
            with sp.Fori(1, BLOCKS // 2) as i:
                for par in range(2):
                    load(i * 2 + par, par)
            for e in range(EXPERTS):
                sp.dma_start(w1[:, e * (FF // P):(e + 1) * (FF // P), :].rearrange("p c f -> p (c f)"),
                             a["L0_ffn_W1"][e]).then_inc(s_we, 16)
                sp.dma_start(w2[:, e * (FF // P):(e + 1) * (FF // P), :],
                             a["L0_ffn_W2"][e].rearrange("(c f) d -> f c d", f=P)).then_inc(s_we, 16)
            sp.wait_ge(s_we, 2 * 16 * EXPERTS)
            sp.wait_ge(s_cst, 32)

            if "x3" in a:
                sp.wait_ge(s_res, 2 * TILES)
                sp.dma_start(a["x3"].rearrange("(t p) d -> p t d", p=P), x_all[:, :, :]).then_inc(s_st, 16)
                sp.wait_ge(s_st, 16)

        @block.tensor
        def _(pe):
            pe.wait_ge(s_cst, 16)
            pe.wait_ge(s_symz, 1 + 3)
            for i in range(3):
                mm = pe.matmul(out_ps[0:8, 0:D], sym_at[:, i, :], w_sym[:, i, :], start=(i == 0), stop=(i == 2))
            mm.then_inc(s_symps, 1)

            def transpose_x(b):
                pe.wait_ge(s_ln, b + 1)
                after(pe, s_ve, b)
                for t in range(BLOCK):
                    mm = pe.transpose(front_ps[:, t, :], xn[:, t, :], ident)
                mm.then_inc(s_xT, 1)

            def transpose_ctx(b, par):
                c = b - BLOCKS
                pe.wait_ge(s_ctx[par], (c - par) * 8 + 16)
                pe.wait_ge(s_xTe, b + 1)
                for t in range(BLOCK):
                    mm = pe.transpose(front_ps[:, t, :], ctx_in[par][:, t, :], ident)
                mm.then_inc(s_cT, 1)

            def project(t, src, signal):
                out = front_ps[:, :, :].rearrange("p t c -> p (t c)")
                att, i = t // 2, t % 2
                pe.matmul(out, bt[:, 4 * att + i, :], rows[:, :], start=True, stop=False)
                pe.matmul(out, w_in[:, att, i, :], src[:, :, :, :].rearrange("d t s q -> d (t s q)"),
                          start=False, stop=True).then_inc(signal, 1)

            def project_q(b, att):
                pe.wait_ge(s_xTe, b + 1)
                if att:
                    pe.wait_ge(s_cTe, b - BLOCKS + 1)
                project(2 * att, xT, s_q)

            def project_k(b, att):
                pe.wait_ge(s_qe, b + 1)
                project(2 * att + 1, cT if att else xT, s_k)

            def project_v(b, att):
                src = cT if att else xT
                pe.wait_ge(s_ke, b + 1)
                bias = bt[:, 4 * att + 2, :].rearrange("r (m h e) -> r h m e", m=8, h=2)
                w = w_v[:, att, :].rearrange("d (m h e) -> d h m e", m=8, h=2)
                for h in range(2):
                    pe.matmul(v_ps[64 * h:64 * h + 64], rows[:, 0:SEQ],
                              bias[:, h].unsqueeze(1).to_broadcast([6, 2 * BLOCK, 8, HD]),
                              start=True, stop=False, skip_group_check=True)
                for i in range(2 * BLOCK):
                    for h in range(2):
                        mm = pe.matmul(v_ps[64 * h:64 * h + 64, i], src[:, i // 2, i % 2, :], w[:, h],
                                       start=False, stop=(i == 2 * BLOCK - 1), skip_group_check=True)
                mm.then_inc(s_v, 1)

            def front(b, par, att, slot):
                if att is None:
                    return
                if slot == 0:
                    transpose_x(b)
                elif slot == 1 and att:
                    transpose_ctx(b, par)
                elif slot == 2:
                    project_q(b, att)
                elif slot == 4:
                    project_k(b, att)
                elif slot == 6:
                    project_v(b, att)

            def scores(n, u, b, par, t, g):
                if g == 0:
                    pe.wait_ge(s_qe, b + 1)
                    pe.wait_ge(s_kbd, b + 1)
                    after(pe, s_logit, n - 1)
                for j in range(2):
                    mm = pe.matmul(score_ps[u % 2][:, j * 8 + g * 4:j * 8 + g * 4 + 4, :],
                                   q_bd[par][64 * j:64 * j + 64, g, t, :, :], k_bd[par][64 * j:64 * j + 64, g, t, :, :],
                                   start=True, stop=True)
                if g == 1:
                    mm.then_inc(s_score, 1)

            def transpose_probs(n, u):
                pe.wait_ge(s_prob, n + 1)
                for half in range(2):
                    after(pe, s_pTe, 2 * n - 1 + half)
                    for m in range(4 * half, 4 * half + 4):
                        mm = pe.transpose(probT_ps[:, m, :], logit[u % 4][:, 2 * m:2 * m + 2, :], ident)
                    mm.then_inc(s_pT, 1)

            def values(n, u, b):
                par, t = u // BLOCK, u % BLOCK
                after(pe, s_res, n)
                pe.wait_ge(s_ve, b + 1)
                for m in range(8):
                    if m % 4 == 0:
                        pe.wait_ge(s_pTe, 2 * n + 1 + m // 4)
                    mm = pe.matmul(o_ps[:, m], probT[u % 2][:, m, :], v_bd[par][:, 2 * t:2 * t + 2, m],
                                   start=True, stop=True)
                mm.then_inc(s_pv, 1)

            def transpose_out(n):
                pe.wait_ge(s_norm, n + 1)
                pe.transpose(oT_ps, o_sb[:, :, :, :].rearrange("p m h e -> p (m h e)"), ident).then_inc(s_oT, 1)

            def project_out(n, att):
                pe.wait_ge(s_oTe, n + 1)
                pe.matmul(y_ps, rows[:, 0:P], bt[:, 4 * att + 3, :], start=True, stop=False)
                pe.matmul(y_ps, oT[:, :], w_o[:, att, :], start=False, stop=True).then_inc(s_y, 1)

            for slot in range(2 * BLOCK):
                if slot == 2:
                    pe.wait_ge(s_w[0], 16)
                    pe.wait_ge(s_bt, 16 * 6)
                    pe.wait_ge(s_rows, 1)
                front(0, 0, 0, slot)
            pe.wait_ge(s_w[1], 16)

            def body(block0, att, nxt, first):
                for n, u, b, par, t, here, ahead in steps(block0, att, nxt, first):
                    if not (first and u < 2):
                        transpose_probs(n - 2, (u - 2) % 8)
                    if not (first and u < 3):
                        transpose_out(n - 3)
                    scores(n, u, b, par, t, 0)
                    if not (first and u < 3):
                        late = 0 if (att == 1 and isinstance(block0, int) and block0 == BLOCKS and u < 3) else att
                        project_out(n - 3, late)
                    scores(n, u, b, par, t, 1)
                    front(b + 1, 1 - par, ahead, 2 * t)
                    if not (first and u < 2):
                        values(n - 2, (u - 2) % 8, b if t >= 2 else b - 1)
                    front(b + 1, 1 - par, ahead, 2 * t + 1)

            schedule(pe, body, None)
            n = PAIRS
            transpose_probs(n - 2, 6)
            transpose_out(n - 3)
            project_out(n - 3, 1)
            values(n - 2, 6, 2 * BLOCKS - 1)
            transpose_probs(n - 1, 7)
            transpose_out(n - 2)
            project_out(n - 2, 1)
            values(n - 1, 7, 2 * BLOCKS - 1)
            transpose_out(n - 1)
            project_out(n - 1, 1)

        @block.scalar
        def _(act):
            act.wait_ge(s_cst, 16)
            act.wait_ge(s_small, 16 * N_SMALL)
            act.activation(xb1[:, :], cst[:, C_DIST:C_DIST + SEQ], ACT.Ln, bias=1.0).then_inc(s_xba, 1)
            act.activation(sc[:, 0:1], scal[:, 2:3], ACT.Exp).then_inc(s_xba, 1)

            def evacuate_x(b):
                after(act, s_xT, b + 1)
                act.activation(xT[:, :, :, :].rearrange("p t s q -> p t (s q)"), front_ps[:, :, :],
                               ACT.Copy).then_inc(s_xTe, 1)

            def evacuate_ctx(b):
                act.wait_ge(s_cT, b - BLOCKS + 1)
                act.activation(cT[:, :, :, :].rearrange("p t s q -> p t (s q)"), front_ps[:, :, :],
                               ACT.Copy).then_inc(s_cTe, 1)

            def quarters():
                for j in range(2):
                    for g in range(2):
                        for s in range(2):
                            yield g, s, slice(64 * j + 32 * g, 64 * j + 32 * g + 32), slice(64 * j + 32 * s,
                                                                                            64 * j + 32 * s + 32)

            def evacuate_q(b, par):
                act.wait_ge(s_q, b + 1)
                after(act, s_score, (b - 1) * BLOCK)
                for g, s, src, dst in quarters():
                    ins = act.activation(q_bd[par][dst, g, :, s, :], front_ps[src, :, 64 * s:64 * s + 64],
                                         ACT.Copy, scale=HD ** -0.5)
                ins.then_inc(s_qe, 1)

            def evacuate_k(b):
                act.wait_ge(s_k, b + 1)
                after(act, s_kbd, b)
                for g, s, src, dst in quarters():
                    ins = act.activation(k_sb[dst, g, :, :], front_ps[src, :, 64 * s:64 * s + 64], ACT.Copy)
                ins.then_inc(s_ke, 1)

            def front(b, par, att, slot):
                if att is None:
                    return
                if slot == 0:
                    evacuate_x(b)
                elif slot == 1 and att:
                    evacuate_ctx(b)
                elif slot == 2:
                    evacuate_q(b, par)
                elif slot == 4:
                    evacuate_k(b)

            def exponentials(n, u):
                act.wait_ge(s_sub, n + 1)
                act.activation(logit[u % 4][:, :, :], logit[u % 4][:, :, :], ACT.Exp).then_inc(s_prob, 1)

            def evacuate_out(n):
                act.wait_ge(s_oT, n + 1)
                act.activation(oT[:, :], oT_ps, ACT.Copy).then_inc(s_oTe, 1)

            def evacuate_probs(n, u, half):
                if half == 0:
                    after(act, s_pv, n - 1)
                act.wait_ge(s_pT, 2 * n + 1 + half)
                act.activation(probT[u % 2][:, 4 * half:4 * half + 4, :], probT_ps[:, 4 * half:4 * half + 4, :],
                               ACT.Copy).then_inc(s_pTe, 1)

            for slot in range(2 * BLOCK):
                if slot == 2:
                    act.wait_ge(s_qz, 2)
                front(0, 0, 0, slot)

            def body(block0, att, nxt, first):
                for n, u, b, par, t, here, ahead in steps(block0, att, nxt, first):
                    if not (first and u < 2):
                        evacuate_probs(n - 2, (u - 2) % 8, 0)
                    if not (first and u < 3):
                        evacuate_out(n - 3)
                    if not (first and u < 2):
                        evacuate_probs(n - 2, (u - 2) % 8, 1)
                    if not (first and u < 1):
                        exponentials(n - 1, (u - 1) % 8)
                    front(b + 1, 1 - par, ahead, 2 * t)
                    front(b + 1, 1 - par, ahead, 2 * t + 1)

            schedule(act, body, None)
            n = PAIRS
            evacuate_probs(n - 2, 6, 0)
            evacuate_out(n - 3)
            evacuate_probs(n - 2, 6, 1)
            exponentials(n - 1, 7)
            evacuate_probs(n - 1, 7, 0)
            evacuate_out(n - 2)
            evacuate_probs(n - 1, 7, 1)
            evacuate_out(n - 1)

        @block.vector
        def _(dve):
            for i in range(2):
                dve.memset(v_bd[i][:, :, :, :, :], 0.0).then_inc(s_vz, 1)
            dve.wait_ge(s_vz, 2)
            for i in range(2):
                for h in range(2):
                    dve.memset(v_bd[i][64 * h:64 * h + 64, :, :, h, HD:HD + 1], 1.0).then_inc(s_vz, 1)

            def stats_of(n, t, b, par):
                dve.bn_stats(stats[:, t, :], x_all[:, n, :]).then_inc(s_bn, 1)

            def aggregate(b, par):
                dve.wait_ge(s_bn, BLOCK * (b + 1))
                if not isinstance(b, int) or b >= 2:
                    dve.wait_ge(s_rstd, b - 1)
                    dve.wait_ge(s_ln, b - 1)
                    passed(dve, s_passed_v)
                for t in range(BLOCK):
                    ins = dve.bn_aggr(mv[par][:, t, :], stats[:, t, :])
                ins.then_inc(s_stat, 1)

            def normalise(b, par):
                dve.wait_ge(s_rstd, b + 1)
                after(dve, s_xT, b)
                for t in range(BLOCK):
                    ins = dve.tensor_scalar(xn[:, t, :], xn_source(b, t), mv[par][:, t, 0:1], rstd[par][:, t:t + 1],
                                            ALU.subtract, ALU.mult)
                ins.then_inc(s_ln, 1)

            def tile_of(b, t):
                return (b * BLOCK + t) % TILES if isinstance(b, int) else b * BLOCK + t

            shift = [0]

            def xn_source(b, t):
                n = tile_of(b, t)
                return x_all[:, n, :] if isinstance(n, int) else x_all[:, bass.ds(n - shift[0], 1), :].rearrange(
                    "p o d -> p (o d)")

            def stat_source(b, t):
                return xn_source(b, t)

            for b in range(2):
                dve.wait_ge(s_x[b], 16)
                for t in range(BLOCK):
                    dve.bn_stats(stats[:, t, :], stat_source(b, t)).then_inc(s_bn, 1)
                aggregate(b, b)
                if b == 0:
                    dve.wait_ge(s_stat, 1)
            dve.wait_ge(s_cst, 16)
            normalise(0, 0)

            dve.wait_ge(s_small, 16 * N_SMALL)
            dve.wait_ge(s_symz, 1)
            for i in range(3):
                dve.tensor_copy(sym_at[:, i, 4 + i:5 + i], sym_in[:, :]).then_inc(s_symz, 1)

            dve.wait_ge(s_symps, 1)
            dve.tensor_copy(tab[:, 1, :], out_ps[0:8, 0:D]).then_inc(s_tab, 1)
            dve.tensor_copy(rows[:, :], rows32[:, :]).then_inc(s_rows, 1)
            dve.wait_ge(s_tab, 1)
            dve.tensor_copy(split[:, :, 0, :], tab[:, :, :]).then_inc(s_split, 1)
            dve.wait_ge(s_split, 1)
            dve.tensor_tensor(rem1[:, :, :], tab[:, :, :], split[:, :, 0, :], ALU.subtract).then_inc(s_split, 1)
            dve.wait_ge(s_split, 2)
            dve.tensor_copy(split[:, :, 1, :], rem1[:, :, :]).then_inc(s_split, 1)
            dve.wait_ge(s_split, 3)
            dve.tensor_tensor(rem2[:, :, :], rem1[:, :, :], split[:, :, 1, :], ALU.subtract).then_inc(s_split, 1)
            dve.wait_ge(s_split, 4)
            dve.tensor_copy(split[:, :, 2, :], rem2[:, :, :]).then_inc(s_split, 1)
            dve.wait_ge(s_xba, 2)
            dve.reciprocal(sc[:, 1:2], sc[:, 0:1]).then_inc(s_xbias, 1)
            dve.tensor_scalar(xb1[:, :], xb1[:, :], scal[:, 0:1], None, ALU.mult).then_inc(s_xbias, 1)
            dve.wait_ge(s_xbias, 2)
            dve.scalar_tensor_tensor(out=xb2[:, :], in0=cst[:, C_PARITY:C_PARITY + SEQ], scalar=scal[:, 1:2],
                                     in1=xb1[:, :], op0=ALU.mult, op1=ALU.add).then_inc(s_xbias, 1)
            dve.tensor_scalar(xb3[:, :], cst[:, C_DIST:C_DIST + SEQ], sc[:, 1:2], None, ALU.mult).then_inc(s_xbias, 1)
            dve.wait_ge(s_xbias, 4)
            dve.tensor_tensor(xb2[:, :], xb2[:, :], xb3[:, :], ALU.subtract).then_inc(s_xbias, 1)
            dve.wait_ge(s_xbias, 5)
            dve.tensor_scalar(xbias[:, :], xb2[:, :], float(HD) ** -0.5, None, ALU.mult).then_inc(s_xbias, 1)
            def evacuate_v(b, par):
                dve.wait_ge(s_v, b + 1)
                after(dve, s_pv, (b - 1) * BLOCK)
                for h in range(2):
                    src = v_ps[64 * h:64 * h + 64].rearrange("p i m e -> p (i m) e")
                    dst = v_bd[par][64 * h:64 * h + 64].rearrange("p i m h e -> p (i m) h e")[:, :, h, 0:HD]
                    ins = dve.tensor_copy(dst, src)
                ins.then_inc(s_ve, 1)

            def front(b, par, att, t):
                if att is not None and t == BLOCK - 1:
                    evacuate_v(b, par)

            def add_bias(n, u, par, t, att):
                dve.wait_ge(s_score, n + 1)
                after(dve, s_pT, 2 * (n - 3))
                if att:
                    dve.wait_ge(s_mb, (n - t) // BLOCK - BLOCKS + 1 if isinstance(n, int) else block_of(n, t) - BLOCKS + 1)
                bias = mbias[par][:, t, :] if att else cst[:, C_DECAY:C_DECAY + SEQ]
                dve.tensor_tensor(logit[u % 4][:, :, :], score_ps[u % 2][:, :, :],
                                  bias.unsqueeze(1).to_broadcast([P, HEADS, SEQ]), ALU.add).then_inc(s_logit, 1)

            cur = [None]

            def block_of(n, t):
                return cur[0]

            def maximum(n, u):
                dve.wait_ge(s_logit, n + 1)
                dve.tensor_reduce(top[u % 4][:, :], logit[u % 4][:, :, :], AX.X, ALU.max).then_inc(s_top, 1)

            def normalise_out(n):
                dve.wait_ge(s_pv, n + 1)
                after(dve, s_norm, n)
                dve.reciprocal(rden[:, :, :], o_ps[:, :, 0, :, HD]).then_inc(s_rden, 1)
                dve.wait_ge(s_rden, n + 1)
                for s in range(2):
                    r = slice(64 * s, 64 * s + 64)
                    ins = dve.tensor_tensor(o_sb[r, :, :, :], o_ps[r, :, s, :, 0:HD],
                                            rden[r, :, :].unsqueeze(3).to_broadcast([64, 8, 2, HD]), ALU.mult)
                ins.then_inc(s_norm, 1)

            def residual(n, off):
                dve.wait_ge(s_y, n + 1)
                if isinstance(n, int):
                    x = x_all[:, n % TILES, :]
                else:
                    x = x_all[:, bass.ds(n - off, 1), :].rearrange("p o d -> p (o d)")
                dve.tensor_tensor(x, x, y_ps, ALU.add).then_inc(s_res, 1)

            evacuate_v(0, 0)

            def body(block0, att, nxt, first):
                static = isinstance(block0, int)
                for n, u, b, par, t, here, ahead in steps(block0, att, nxt, first):
                    cur[0] = b
                    shift[0] = TILES if att else 0
                    if t == 0 and ahead is not None:
                        normalise(b + 1, 1 - par)
                    if not (first and u < 3):
                        residual(n - 3, TILES if att else 0)
                    add_bias(n, u, par, t, att)
                    maximum(n, u)
                    if not (first and u < 2):
                        normalise_out(n - 2)
                    front(b + 1, 1 - par, ahead, t)
                    stats_ahead = not (static and block0 + par + 2 >= 2 * BLOCKS)
                    if stats_ahead and t < BLOCK - 1:
                        if first and par == 0 and t == 0:
                            dve.wait_ge(s_x[2], 16)
                        if t == 0:
                            dve.wait_ge(s_stat, b + 2)
                        for k in (t, t + 1) if t == BLOCK - 2 else (t,):
                            if static:
                                src = x_all[:, ((b + 2) * BLOCK + k) % TILES, :]
                            else:
                                src = x_all[:, bass.ds((b + 2) * BLOCK + k - shift[0], 1), :].rearrange("p o d -> p (o d)")
                            dve.bn_stats(stats[:, k, :], src).then_inc(s_bn, 1)
                        if t == BLOCK - 2:
                            aggregate(b + 2, par)
                if first:
                    dve.wait_ge(s_x[3], 16)

            schedule(dve, body, None)
            n = PAIRS
            residual(n - 3, 0)
            normalise_out(n - 2)
            residual(n - 2, 0)
            normalise_out(n - 1)
            residual(n - 1, 0)

        @block.gpsimd
        def _(pool):
            pool.memset(mhalf[:, :], -0.5).then_inc(s_mhalf, 1)
            pool.memset(sym_at[:, :, :], 0.0).then_inc(s_symz, 1)
            for i in range(2):
                pool.memset(q_bd[i][:, :, :, :, :], 0.0).then_inc(s_qz, 1)
            pool.wait_ge(s_mhalf, 1)

            def inverse_deviation(b, par):
                pool.wait_ge(s_stat, b + 1)
                after(pool, s_rstd, b)
                passed(pool, s_passed_g)
                pool.tensor_scalar(vareps[:, :], mv[par][:, :, 1], EPS, 1.0, ALU.add, ALU.mult).then_inc(s_veps, 1)
                pool.wait_ge(s_veps, b + 1)
                after(pool, s_ln, b - 1)
                pool.tensor_tensor(rstd[par][:, :], vareps[:, :], mhalf[:, :], ALU.pow).then_inc(s_rstd, 1)

            def spread_k(b, par):
                pool.wait_ge(s_ke, b + 1)
                after(pool, s_score, (b - 1) * BLOCK)
                passed(pool, s_passed_g)
                for h in range(4):
                    dst = k_bd[par][:, :, :, h, :].rearrange("p g t q -> p (g t) q")
                    ins = pool.tensor_scalar(dst, k_sb[:, :, :, :].rearrange("p g t q -> p (g t) q"),
                                             cst[:, C_HEAD + h:C_HEAD + h + 1], 1.0, ALU.mult, ALU.mult)
                ins.then_inc(s_kbd, 1)

            def mask_bias(b, par):
                c = b - BLOCKS
                pool.wait_ge(s_mask[par], (c - par) * 8 + 16)
                after(pool, s_mb, c)
                passed(pool, s_passed_g)
                pool.tensor_scalar(mask_f[:, :, :], mask_in[par][:, :, :], -1.0, -NEG, ALU.add, ALU.mult).then_inc(s_mf, 1)
                pool.wait_ge(s_mf, c + 1)
                pool.wait_ge(s_xbias, 6)
                pool.wait_ge(s_logit, (b - 1) * BLOCK)
                pool.tensor_tensor(mbias[par][:, :, :], mask_f[:, :, :],
                                   xbias[:, :].unsqueeze(1).to_broadcast([P, BLOCK, SEQ]), ALU.add).then_inc(s_mb, 1)

            def front(b, par, att, slot):
                if att is None:
                    return
                if slot == 4:
                    spread_k(b, par)
                elif slot == 6 and att:
                    mask_bias(b, par)

            def subtract_max(n, u):
                pool.wait_ge(s_top, n + 1)
                pool.tensor_tensor(logit[u % 4][:, :, :], logit[u % 4][:, :, :],
                                   top[u % 4][:, :].unsqueeze(2).to_broadcast([P, HEADS, SEQ]),
                                   ALU.subtract).then_inc(s_sub, 1)

            inverse_deviation(0, 0)
            inverse_deviation(1, 1)
            pool.wait_ge(s_cst, 16)
            for slot in range(2 * BLOCK):
                front(0, 0, 0, slot)

            def body(block0, att, nxt, first):
                static = isinstance(block0, int)
                for n, u, b, par, t, here, ahead in steps(block0, att, nxt, first):
                    if t == BLOCK - 1 and not (static and block0 + par + 2 >= 2 * BLOCKS):
                        inverse_deviation(b + 2, par)
                    subtract_max(n, u)
                    front(b + 1, 1 - par, ahead, 2 * t)
                    front(b + 1, 1 - par, ahead, 2 * t + 1)

            schedule(pool, body, None)


def router(nc, a, x_all, cst, sh):
    ctx = ExitStack()
    with ctx:
        def sb(name, shape, dt=F32):
            return ctx.enter_context(nc.sbuf_tensor(name, shape, dt))

        def pb(name, shape):
            return ctx.enter_context(nc.psum_tensor(name, shape, F32))

        def sem(name):
            return ctx.enter_context(nc.semaphore(name))

        E, HI = EXPERTS, 4
        LO = TILES // HI
        BITS = 30
        w_g = sb("w_g", [P, E])
        stats = sb("r_stats", [P, BLOCK, 6])
        mv = [sb(f"r_mv{i}", [P, BLOCK, 2]) for i in range(2)]
        vareps = sb("r_vareps", [P, BLOCK])
        mhalf = sb("r_mhalf", [P, BLOCK])
        rstd = [sb(f"r_rstd{i}", [P, BLOCK]) for i in range(2)]
        xn = [sb(f"r_xn{i}", [P, BLOCK, D]) for i in range(2)]
        xT = [sb(f"r_xT{i}", [P, BLOCK, P]) for i in range(2)]
        logits = sb("logits", [P, TILES, E])
        tmax = sb("tmax", [P, TILES])
        tsum = sb("tsum", [P, TILES])
        prob = sb("prob", [P, HI, LO, E])
        lane = sb("lane", [P, HI * P])
        junk = sb("junk", [P, HI * P])
        bits = sb("bits", [P, BITS + 1], I32)
        count = sb("count", [P, 1])
        thr = sb("thr", [P, 1], I32)
        cand = sb("cand", [P, 1], I32)
        keep = sb("keep", [P, 1], I32)
        above = sb("above", [P, HI * P])
        equal = sb("equal", [P, HI * P])
        rank = sb("rank", [P, HI * P])
        low = sb("low", [P, HI * P])
        tie = sb("tie", [P, HI * P])
        chosen = sb("chosen", [P, HI * P])
        n_above = sb("n_above", [P, 1])
        need = sb("need", [P, 1])
        before = sb("before", [P, 1])
        sel = sb("sel", [P, TILES, E])
        free = sb("free", [P, TILES])
        allow = sb("allow", [P, TILES, E])
        key0 = sb("key0", [P, TILES, E])
        key = sb("key", [P, TILES, E])
        gate = sb("gate", [P, TILES])
        hit = sb("hit", [P, TILES, E])
        hit2 = sb("hit2", [P, TILES, E])
        first = sb("first", [P, TILES])
        onehot = sb("onehot", [P, TILES, E])
        total = sb("total", [P, E, TILES])
        runs = sb("runs", [P, E, TILES])
        excl = sb("excl", [P, E, TILES])
        n_tiles_i = sb("n_tiles_i", [P, E], I32)
        n_tiles_s = sb("n_tiles_s", [P, E], I32)
        n_tiles = sb("n_tiles", [P, E])
        last_tile = sb("last_tile", [P, E])
        base = sb("base", [P, E])
        base2 = sb("base2", [P, E])
        place3 = sb("place3", [P, E, TILES])
        place2 = sb("place2", [P, TILES, E])
        place1 = sb("place1", [P, TILES, E])
        place = sb("place", [P, TILES])
        place_i = sb("place_i", [P, TILES], I32)
        part_i = sb("part_i", [P, 2, TILES], I32)
        part = sb("part", [P, 2, TILES])
        owner = sb("owner", [P, ROUTED, E])
        owner1 = sb("owner1", [P, ROUTED])
        row_is = [sb(f"row_is{i}", [P, P]) for i in range(4)]
        tile_is = [sb(f"tile_is{i}", [P, 2, ROUTED]) for i in range(4)]
        slot_token = sb("slot_token", [P, ROUTED])
        slot_empty = sb("slot_empty", [P, ROUTED])

        xT_ps = [pb(f"xT_ps{i}", [P, BLOCK, P]) for i in range(2)]
        logit_ps = [pb(f"logit_ps{i}", [P, BLOCK, E]) for i in range(2)]
        lane_ps = pb("lane_ps", [P, HI, P])
        count_ps = pb("count_ps", [P, 4])
        rank_ps = pb("rank_ps", [P, TILES, E])
        total_ps = pb("total_ps", [P, TILES, E])
        slot_ps = xT_ps[0][:, 0:2, :].rearrange("p a b -> p (a b)")[:, 0:2 * ROUTED]

        ident = cst[:, C_IDENT:C_IDENT + P]
        same = cst[:, C_SAME:C_SAME + P]

        s_w = sem("r_w")
        s_mh = sem("r_mh")
        s_bn = sem("r_bn")
        s_stat = sem("r_stat")
        s_veps = sem("r_veps")
        s_rstd = sem("r_rstd_s")
        s_ln = sem("r_ln")
        s_xT = sem("r_xTs")
        s_xTe = sem("r_xTe")
        s_lg = sem("r_lg")
        s_lge = sem("r_lge")
        s_st = [sem(f"r_st{i}") for i in range(2)]
        s_stx = sem("r_stx")
        s_sm = sem("r_sm")
        s_exp = sem("r_exp")
        s_shift = sem("r_shift")
        s_prob = sem("r_prob")
        s_lane = sem("r_lane")
        s_cnt = sem("r_cnt")
        s_tot = sem("r_tot")
        s_keep = sem("r_keep")
        s_thr = sem("r_thr")
        s_cand = sem("r_cand")
        s_above = sem("r_above")
        s_above_t = sem("r_above_t")
        s_eq = sem("r_eq")
        s_before = sem("r_before")
        s_chosen = sem("r_chosen")
        s_sel = sem("r_sel")
        s_onehot = sem("r_onehot")
        s_rank = sem("r_rank")
        s_parts = sem("r_parts")
        s_is = sem("r_is")
        s_map = sem("r_map")
        s_tab = sem("r_tab")
        s_passed_g = sem("r_passed_g")
        s_passed_v = sem("r_passed_v")

        rec = a["rec"].rearrange("(t p) c d -> p t c d", p=P)
        UNROLL = 5
        DEPTH = 4

        block = ctx.enter_context(nc.Block())

        @block.sync
        def _(sp):
            sp.dma_start(w_g[:, :], a["L0_ffn_Wg"]).then_inc(s_w, 16)

            def store(b, par):
                sp.dma_start(rec[:, bass.ds(b * BLOCK, BLOCK), 0, :],
                             x_all[:, bass.ds(b * BLOCK, BLOCK), :]).then_inc(s_stx, 16)
                sp.wait_ge(s_ln, b + 1)
                sp.dma_start(rec[:, bass.ds(b * BLOCK, BLOCK), 1, :], xn[par][:, :, :]).then_inc(s_st[par], 16)

            with sp.Fori(0, BLOCKS // 2) as i:
                for par in range(2):
                    store(i * 2 + par, par)
            for par in range(2):
                sp.wait_ge(s_st[par], 16 * (BLOCKS // 2))
            sp.wait_ge(s_stx, 16 * BLOCKS)

        @block.gpsimd
        def _(pool):
            pool.memset(mhalf[:, :], -0.5).then_inc(s_mh, 1)
            pool.wait_ge(s_mh, 1)

            def inverse_deviation(b, par):
                pool.wait_ge(s_stat, b + 1)
                after(pool, s_rstd, b)
                passed(pool, s_passed_g)
                pool.tensor_scalar(vareps[:, :], mv[par][:, :, 1], EPS, 1.0, ALU.add, ALU.mult).then_inc(s_veps, 1)
                pool.wait_ge(s_veps, b + 1)
                pool.tensor_tensor(rstd[par][:, :], vareps[:, :], mhalf[:, :], ALU.pow).then_inc(s_rstd, 1)

            for b in range(2):
                inverse_deviation(b, b)
            with pool.Fori(1, BLOCKS // 2) as i:
                for par in range(2):
                    inverse_deviation(i * 2 + par, par)

        @block.scalar
        def _(act):
            def evacuate(b, par):
                act.wait_ge(s_xT, b + 1)
                after(act, s_lg, b - 1)
                act.activation(xT[par][:, :, :], xT_ps[par][:, :, :], ACT.Copy).then_inc(s_xTe, 1)

            for b in range(2):
                evacuate(b, b)
            with act.Fori(1, BLOCKS // 2) as i:
                for par in range(2):
                    evacuate(i * 2 + par, par)
            act.wait_ge(s_shift, 1)
            act.activation(logits[:, :, :], logits[:, :, :], ACT.Exp).then_inc(s_exp, 1)

        @block.tensor
        def _(pe):
            pe.wait_ge(s_w, 16)

            def tile_block(b, par):
                pe.wait_ge(s_ln, b + 1)
                after(pe, s_xTe, b - 1)
                for t in range(BLOCK):
                    mm = pe.transpose(xT_ps[par][:, t, :], xn[par][:, t, :], ident)
                mm.then_inc(s_xT, 1)
                pe.wait_ge(s_xTe, b + 1)
                after(pe, s_lge, b - 1)
                for t in range(BLOCK):
                    mm = pe.matmul(logit_ps[par][:, t, :], xT[par][:, t, :], w_g[:, :], start=True, stop=True)
                mm.then_inc(s_lg, 1)

            for b in range(2):
                tile_block(b, b)
            with pe.Fori(1, BLOCKS // 2) as i:
                for par in range(2):
                    tile_block(i * 2 + par, par)

            pe.wait_ge(s_prob, 1)
            for h in range(HI):
                mm = pe.transpose(lane_ps[:, h, :], prob[:, h, :, :].rearrange("p l e -> p (l e)"), ident)
            mm.then_inc(s_lane, 1)

            with pe.Fori(0, BITS // UNROLL) as i:
                for k in range(UNROLL):
                    pe.wait_ge(s_cnt, i * UNROLL + (k + 1))
                    pe.matmul(count_ps[:, 0:1], same, count[:, :], start=True, stop=True).then_inc(s_tot, 1)
            pe.wait_ge(s_above, 1)
            pe.matmul(count_ps[:, 1:2], same, n_above[:, :], start=True, stop=True).then_inc(s_above_t, 1)
            pe.wait_ge(s_eq, 2)
            pe.wait_ge(s_above, 2)
            pe.matmul(count_ps[:, 2:3], cst[:, C_BEFORE:C_BEFORE + P], rank[:, HI * P - 1:HI * P],
                      start=True, stop=True).then_inc(s_before, 1)
            pe.wait_ge(s_chosen, 1)
            for h in range(HI):
                mm = pe.transpose(lane_ps[:, h, :], chosen[:, h * P:h * P + P], ident)
            mm.then_inc(s_sel, 1)
            pe.wait_ge(s_onehot, 1)
            pe.matmul(rank_ps[:, :, :], cst[:, C_LOWER:C_LOWER + P], onehot[:, :, :], start=True, stop=True)
            pe.matmul(total_ps[:, :, :], cst[:, C_ONES:C_ONES + P], onehot[:, :, :],
                      start=True, stop=True).then_inc(s_rank, 1)

            def add_tile(n, d, start, stop):
                pe.wait_ge(s_is, n + 1)
                pe.matmul(slot_ps, row_is[d][:, :], tile_is[d][:, :, :].rearrange("p a r -> p (a r)"),
                          start=start, stop=stop).then_inc(s_map, 1)

            for d in range(DEPTH):
                add_tile(d, d, d == 0, False)
            with pe.Fori(1, TILES // DEPTH - 1) as i:
                for d in range(DEPTH):
                    add_tile(i * DEPTH + d, d, False, False)
            for d in range(DEPTH):
                add_tile(TILES - DEPTH + d, d, False, d == DEPTH - 1)

        @block.vector
        def _(dve):
            def stats_block(b, par):
                after(dve, s_stat, b)
                for t in range(BLOCK):
                    dve.bn_stats(stats[:, t, :], x_all[:, bass.ds(b * BLOCK + t, 1), :].rearrange(
                        "p o d -> p (o d)")).then_inc(s_bn, 1)
                dve.wait_ge(s_bn, BLOCK * (b + 1))
                after(dve, s_ln, b - 1)
                passed(dve, s_passed_v)
                for t in range(BLOCK):
                    ins = dve.bn_aggr(mv[par][:, t, :], stats[:, t, :])
                ins.then_inc(s_stat, 1)

            def normalise(b, par):
                dve.wait_ge(s_rstd, b + 1)
                after(dve, s_xT, b - 1)
                after(dve, s_st[par], (b - par) * 8)
                for t in range(BLOCK):
                    x = x_all[:, bass.ds(b * BLOCK + t, 1), :].rearrange("p o d -> p (o d)")
                    ins = dve.tensor_scalar(xn[par][:, t, :], x, mv[par][:, t, 0:1], rstd[par][:, t:t + 1],
                                            ALU.subtract, ALU.mult)
                ins.then_inc(s_ln, 1)

            def take_logits(b, par):
                dve.wait_ge(s_lg, b + 1)
                dve.tensor_copy(logits[:, bass.ds(b * BLOCK, BLOCK), :], logit_ps[par][:, :, :]).then_inc(s_lge, 1)

            stats_block(0, 0)
            stats_block(1, 1)
            normalise(0, 0)
            stats_block(2, 0)
            normalise(1, 1)
            stats_block(3, 1)
            normalise(2, 0)
            take_logits(0, 0)
            with dve.Fori(1, BLOCKS // 2 - 1) as i:
                for par in range(2):
                    b = i * 2 + par + 2
                    stats_block(b, par)
                    normalise(b - 1, 1 - par)
                    take_logits(b - 3, 1 - par)
            normalise(BLOCKS - 1, 1)
            for b in range(BLOCKS - 3, BLOCKS):
                take_logits(b, b % 2)

            chain = [0]

            def link(ins):
                chain[0] += 1
                ins.then_inc(s_sm, 1)
                dve.wait_ge(s_sm, chain[0])

            def by_tile(x):
                return x.unsqueeze(2).to_broadcast([P, TILES, E])

            dve.wait_ge(s_lge, BLOCKS)
            link(dve.tensor_reduce(tmax[:, :], logits[:, :, :], AX.X, ALU.max))
            dve.tensor_tensor(logits[:, :, :], logits[:, :, :], by_tile(tmax[:, :]), ALU.subtract).then_inc(s_shift, 1)
            dve.wait_ge(s_exp, 1)
            link(dve.tensor_reduce(tsum[:, :], logits[:, :, :], AX.X, ALU.add))
            link(dve.reciprocal(tsum[:, :], tsum[:, :]))
            dve.tensor_tensor(prob[:, :, :, :].rearrange("p h l e -> p l h e"),
                              logits[:, :, :].rearrange("p (l h) e -> p l h e", h=HI),
                              tsum[:, :].rearrange("p (l h) -> p l h", h=HI).unsqueeze(3).to_broadcast([P, LO, HI, E]),
                              ALU.mult).then_inc(s_prob, 1)

            bits_f = cst[:, C_BITS:C_BITS + BITS + 1]
            link(dve.tensor_copy(bits[:, :], bits_f))
            link(dve.memset(thr[:, :], 0))
            dve.tensor_copy(cand[:, :], bits[:, 0:1]).then_inc(s_cand, 1)
            dve.wait_ge(s_lane, 1)
            link(dve.tensor_copy(lane[:, :], lane_ps[:, :, :].rearrange("p h t -> p (h t)")))
            with dve.Fori(0, BITS // UNROLL) as i:
                for k in range(UNROLL):
                    n = i * UNROLL + k
                    dve.wait_ge(s_cand, n + 1)
                    dve.tensor_scalar(junk[:, :], lane[:, :], cand[:, :].bitcast(F32), None, ALU.is_ge, ALU.add,
                                      accum_out=count[:, :]).then_inc(s_cnt, 1)
                    dve.wait_ge(s_tot, n + 1)
                    dve.tensor_scalar(keep[:, :], count_ps[:, 0:1], float(CAP), bits_f[:, bass.ds(n, 1)],
                                      ALU.is_ge, ALU.mult).then_inc(s_keep, 1)
                    dve.wait_ge(s_keep, n + 1)
                    dve.tensor_tensor(thr[:, :], thr[:, :], keep[:, :], ALU.bitwise_or).then_inc(s_thr, 1)
                    dve.wait_ge(s_thr, n + 1)
                    dve.tensor_tensor(cand[:, :], thr[:, :], bits[:, bass.ds(n + 1, 1)],
                                      ALU.bitwise_or).then_inc(s_cand, 1)
            dve.wait_ge(s_cand, BITS + 1)
            level = thr[:, :].bitcast(F32)
            dve.tensor_scalar(above[:, :], lane[:, :], level, None, ALU.is_gt, ALU.add,
                              accum_out=n_above[:, :]).then_inc(s_above, 1)
            dve.tensor_scalar(equal[:, :], lane[:, :], level, None, ALU.is_equal).then_inc(s_eq, 1)
            dve.wait_ge(s_above_t, 1)
            dve.tensor_scalar(need[:, :], count_ps[:, 1:2], -1.0, float(CAP), ALU.mult, ALU.add).then_inc(s_above, 1)
            dve.wait_ge(s_eq, 1)
            link(dve.memset(junk[:, :], 1.0))
            dve.tensor_tensor_scan(rank[:, :], junk[:, :], equal[:, :], 0.0, ALU.mult, ALU.add).then_inc(s_eq, 1)
            dve.wait_ge(s_before, 1)
            dve.wait_ge(s_eq, 2)
            dve.wait_ge(s_above, 2)
            link(dve.tensor_copy(before[:, :], count_ps[:, 2:3]))
            link(dve.tensor_scalar(low[:, :], rank[:, :], before[:, :], need[:, :], ALU.add, ALU.is_le))
            link(dve.tensor_tensor(tie[:, :], equal[:, :], low[:, :], ALU.mult))
            dve.tensor_tensor(chosen[:, :], above[:, :], tie[:, :], ALU.add).then_inc(s_chosen, 1)

            pr = prob[:, :, :, :].rearrange("p h l e -> p (h l) e")
            dve.wait_ge(s_sel, 1)
            link(dve.tensor_copy(sel[:, :, :].rearrange("p t e -> p (t e)"), lane_ps[:, :, :].rearrange("p h t -> p (h t)")))
            link(dve.tensor_reduce(first[:, :], sel[:, :, :], AX.X, ALU.max))
            link(dve.tensor_scalar(free[:, :], first[:, :], -1.0, 1.0, ALU.mult, ALU.add))
            link(dve.tensor_tensor(allow[:, :, :], sel[:, :, :], by_tile(free[:, :]), ALU.max))
            link(dve.tensor_tensor(key0[:, :, :], pr, allow[:, :, :], ALU.mult))
            link(dve.scalar_tensor_tensor(out=key[:, :, :], in0=allow[:, :, :], scalar=-1.0, in1=key0[:, :, :],
                                          op0=ALU.add, op1=ALU.add))
            link(dve.tensor_reduce(gate[:, :], key[:, :, :], AX.X, ALU.max))
            link(dve.tensor_tensor(hit[:, :, :], key[:, :, :], by_tile(gate[:, :]), ALU.is_equal))
            link(dve.tensor_tensor(hit2[:, :, :], hit[:, :, :],
                                   cst[:, C_REST:C_RUN].rearrange("p (t e) -> p t e", e=E), ALU.mult))
            link(dve.tensor_reduce(first[:, :], hit2[:, :, :], AX.X, ALU.max))
            dve.tensor_tensor(onehot[:, :, :], hit2[:, :, :], by_tile(first[:, :]), ALU.is_equal).then_inc(s_onehot, 1)

            dve.wait_ge(s_rank, 1)
            dve.wait_ge(s_onehot, 1)
            link(dve.tensor_copy(total[:, :, :], total_ps[:, :, :].rearrange("p t e -> p e t")))
            link(dve.tensor_tensor_scan(runs[:, :, :].rearrange("p e t -> p (e t)"), cst[:, C_RUN:C_TOKEN],
                                        total[:, :, :].rearrange("p e t -> p (e t)"), 0.0, ALU.mult, ALU.add))
            link(dve.tensor_tensor(excl[:, :, :], runs[:, :, :], total[:, :, :], ALU.subtract))
            link(dve.tensor_scalar(n_tiles_i[:, :], runs[:, :, TILES - 1], float(P - 1), None, ALU.add))
            link(dve.tensor_scalar(n_tiles_s[:, :], n_tiles_i[:, :], 7, None, ALU.logical_shift_right))
            link(dve.tensor_copy(n_tiles[:, :], n_tiles_s[:, :]))
            link(dve.tensor_tensor_scan(last_tile[:, :], cst[:, C_ONES:C_ONES + E], n_tiles[:, :], 0.0, ALU.mult, ALU.add))
            link(dve.tensor_tensor(base2[:, :], last_tile[:, :], n_tiles[:, :], ALU.subtract))
            link(dve.tensor_scalar(base[:, :], base2[:, :], float(P), None, ALU.mult))
            link(dve.tensor_tensor(place3[:, :, :], excl[:, :, :], base[:, :].unsqueeze(2).to_broadcast([P, E, TILES]),
                                   ALU.add))
            link(dve.tensor_tensor(place2[:, :, :], rank_ps[:, :, :], place3[:, :, :].rearrange("p e t -> p t e"), ALU.add))
            link(dve.tensor_tensor(place1[:, :, :], place2[:, :, :], onehot[:, :, :], ALU.mult))
            link(dve.tensor_reduce(place[:, :], place1[:, :, :], AX.X, ALU.add))
            link(dve.tensor_copy(place_i[:, :], place[:, :]))
            dve.tensor_scalar(part_i[:, 0, :], place_i[:, :], 7, None, ALU.logical_shift_right)
            link(dve.tensor_scalar(part_i[:, 1, :], place_i[:, :], P - 1, None, ALU.bitwise_and))
            dve.tensor_copy(part[:, :, :], part_i[:, :, :]).then_inc(s_parts, 1)
            dve.wait_ge(s_parts, 1)

            def one_tile(n, d):
                after(dve, s_map, n - (DEPTH - 1))
                at = bass.ds(n, 1)
                dve.tensor_scalar(row_is[d][:, :], cst[:, C_IOTA:C_IOTA + P], part[:, 1, at], None, ALU.is_equal)
                tile = part[:, 0, at]
                dve.tensor_scalar(tile_is[d][:, 0, :], cst[:, C_IOTA:C_IOTA + ROUTED], tile,
                                  cst[:, bass.ds(n + C_TOKEN, 1)], ALU.is_equal, ALU.mult)
                dve.tensor_scalar(tile_is[d][:, 1, :], cst[:, C_IOTA:C_IOTA + ROUTED], tile, gate[:, at],
                                  ALU.is_equal, ALU.mult).then_inc(s_is, 1)

            for d in range(DEPTH):
                one_tile(d, d)
            with dve.Fori(1, TILES // DEPTH) as i:
                for d in range(DEPTH):
                    one_tile(i * DEPTH + d, d)

            link(dve.tensor_tensor(owner[:, :, :], last_tile[:, :].unsqueeze(1).to_broadcast([P, ROUTED, E]),
                                   cst[:, C_IOTA:C_IOTA + ROUTED].unsqueeze(2).to_broadcast([P, ROUTED, E]), ALU.is_le))
            link(dve.tensor_reduce(owner1[:, :], owner[:, :, :], AX.X, ALU.add))
            link(dve.tensor_scalar(sh["expert_of"][:, :], owner1[:, :], float(E - 1), None, ALU.min))
            dve.wait_ge(s_map, TILES)
            dve.tensor_copy(sh["gate_of"][:, :], slot_ps[:, ROUTED:2 * ROUTED]).then_inc(s_tab, 1)
            link(dve.tensor_copy(slot_token[:, :], slot_ps[:, 0:ROUTED]))
            dve.tensor_scalar(sh["gather_at"][:, :], slot_token[:, :], -1.0, 0.0, ALU.add, ALU.max).then_inc(s_tab, 1)
            link(dve.tensor_scalar(slot_empty[:, :], slot_token[:, :], 0.0, float(TOKENS + 1), ALU.is_equal, ALU.mult))
            link(dve.scalar_tensor_tensor(out=sh["scatter_at"][:, :], in0=slot_token[:, :], scalar=-1.0,
                                          in1=slot_empty[:, :], op0=ALU.add, op1=ALU.add))
            dve.wait_ge(s_tab, 2)


def experts(nc, a, cst, sh):
    ctx = ExitStack()
    with ctx:
        def sb(name, shape, dt=F32):
            return ctx.enter_context(nc.sbuf_tensor(name, shape, dt))

        def pb(name, shape):
            return ctx.enter_context(nc.psum_tensor(name, shape, F32))

        def sem(name):
            return ctx.enter_context(nc.semaphore(name))

        FC = FF // P
        ROUND = 8
        GATHER_AHEAD = 5
        INDEX_AHEAD = 6
        assert ROUTED % ROUND == 0
        ROUNDS = ROUTED // ROUND
        gat = [sb(f"gat{i}", [P, 1], I32) for i in range(ROUND)]
        sca = [sb(f"sca{i}", [P, 1], I32) for i in range(ROUND)]
        xr = [sb(f"xr{i}", [P, 2, D]) for i in range(ROUND)]
        xT = [sb(f"f_xT{i}", [P, P]) for i in range(2)]
        hT = [sb(f"hT{i}", [P, FC, P]) for i in range(2)]
        res = [sb(f"res{i}", [P, D]) for i in range(ROUND)]
        xT_ps = [pb(f"f_xT_ps{i}", [P, P]) for i in range(2)]
        h_ps = [pb(f"h_ps{i}", [P, FC, P]) for i in range(2)]
        y_ps = [pb(f"f_y_ps{i}", [P, D]) for i in range(2)]
        ident = cst[:, C_IDENT:C_IDENT + P]
        w1, w2 = sh["w1"], sh["w2"]
        w1_now = [sb(f"w1_now{i}", [P, FC, P]) for i in range(4)]

        s_idx = sem("f_idx")
        s_w1 = sem("f_w1")
        s_gat = [sem(f"f_gat{i}") for i in range(ROUND)]
        s_xT = sem("f_xTs")
        s_xTe = sem("f_xTe")
        s_h = sem("f_h")
        s_gelu = sem("f_gelu")
        s_y = sem("f_y")
        s_res = sem("f_res")
        s_sca = [sem(f"f_sca{i}") for i in range(ROUND)]
        s_passed_g = sem("f_passed_g")

        rec = a["rec"].rearrange("t c d -> t (c d)")

        block = ctx.enter_context(nc.Block())

        def landed(n, u):
            return (n - u) * (16 // ROUND) + 16

        @block.gpsimd
        def _(pool):
            def gather(n, u):
                pool.wait_ge(s_idx, n + 1)
                after(pool, s_res, n - ROUND + 1)
                passed(pool, s_passed_g)
                pool.indirect_dma_start(xr[u][:, :, :].rearrange("p c d -> p (c d)"), None, rec,
                                        bass.IndirectOffsetOnAxis(ap=gat[u][:, :].bitcast(U32), axis=0)).then_inc(s_gat[u], 16)

            def scatter(n, u):
                pool.wait_ge(s_res, n + 1)
                passed(pool, s_passed_g)
                pool.indirect_dma_start(a["out"], bass.IndirectOffsetOnAxis(ap=sca[u][:, :].bitcast(U32), axis=0),
                                        res[u][:, :], None, bounds_check=TOKENS - 1, oob_is_err=False).then_inc(s_sca[u], 16)

            def step(n, u, ahead):
                if ahead:
                    gather(n + GATHER_AHEAD, (u + GATHER_AHEAD) % ROUND)
                scatter(n, u)

            for n in range(GATHER_AHEAD):
                gather(n, n)
            for u in range(ROUND):
                step(u, u, True)
            with pool.Fori(1, ROUNDS - 1) as i:
                for u in range(ROUND):
                    step(i * ROUND + u, u, True)
            for u in range(ROUND):
                step(ROUTED - ROUND + u, u, u + GATHER_AHEAD < ROUND)
            for u in range(ROUND):
                pool.wait_ge(s_sca[u], 16 * ROUNDS)

        @block.tensor
        def _(pe):
            def turn(n, u):
                pe.wait_ge(s_gat[u], landed(n, u))
                after(pe, s_xTe, n - 1)
                pe.transpose(xT_ps[u % 2][:, :], xr[u][:, 1, :], ident).then_inc(s_xT, 1)

            def up(n, u):
                pe.wait_ge(s_w1, n + 1)
                pe.wait_ge(s_xTe, n + 1)
                after(pe, s_gelu, n - 1)
                for c in range(FC):
                    mm = pe.matmul(h_ps[u % 2][:, c, :], w1_now[u % 4][:, c, :],
                                   xT[u % 2][:, :], start=True, stop=True)
                mm.then_inc(s_h, 1)

            def down(n, u, e):
                pe.wait_ge(s_gelu, n + 1)
                after(pe, s_res, n - 1)
                for c in range(FC):
                    mm = pe.matmul(y_ps[u % 2][:, :], hT[u % 2][:, c, :],
                                   w2[:, bass.ds(e * FC + c, 1), :].rearrange("p o d -> p (o d)"),
                                   start=(c == 0), stop=(c == FC - 1))
                mm.then_inc(s_y, 1)

            def expert(n):
                return pe.value_load(sh["expert_of"][0:1, bass.ds(n, 1)], min_val=0, max_val=EXPERTS - 1)

            def tile(n, u, first, last):
                if not last:
                    turn(n + 1, (u + 1) % ROUND)
                if not first:
                    down(n - 1, (u - 1) % ROUND, expert(n - 1))
                up(n, u)

            turn(0, 0)
            for u in range(ROUND):
                tile(u, u, u == 0, False)
            with pe.Fori(1, ROUNDS - 1) as i:
                for u in range(ROUND):
                    tile(i * ROUND + u, u, False, False)
            for u in range(ROUND):
                tile(ROUTED - ROUND + u, u, False, u == ROUND - 1)
            down(ROUTED - 1, ROUND - 1, expert(ROUTED - 1))

        @block.scalar
        def _(act):
            def gelu(n, u):
                act.wait_ge(s_h, n + 1)
                after(act, s_y, n - 1)
                act.activation(hT[u % 2][:, :, :], h_ps[u % 2][:, :, :], ACT.Gelu).then_inc(s_gelu, 1)

            def fetch(n, u):
                after(act, s_h, n - 3)
                e = act.value_load(sh["expert_of"][0:1, bass.ds(n, 1)], min_val=0, max_val=EXPERTS - 1)
                act.activation(w1_now[u % 4][:, :, :], w1[:, bass.ds(e * FC, FC), :], ACT.Copy).then_inc(s_w1, 1)

            def step(n, u, left):
                gelu(n, u)
                if left > 3:
                    fetch(n + 3, u + 3)

            for n in range(3):
                fetch(n, n)
            for u in range(ROUND):
                step(u, u, ROUTED)
            with act.Fori(1, ROUNDS - 1) as i:
                for u in range(ROUND):
                    step(i * ROUND + u, u, ROUTED)
            for u in range(ROUND):
                step(ROUTED - ROUND + u, u, ROUND - u)

        @block.vector
        def _(dve):
            def indices(n, u, again):
                if again:
                    dve.wait_ge(s_gat[u], landed(n, u) - 16)
                    dve.wait_ge(s_sca[u], landed(n, u) - 16)
                dve.tensor_copy(sca[u][:, :], sh["scatter_at"][:, bass.ds(n, 1)])
                dve.tensor_copy(gat[u][:, :], sh["gather_at"][:, bass.ds(n, 1)]).then_inc(s_idx, 1)

            def evacuate(n, u):
                dve.wait_ge(s_xT, n + 1)
                after(dve, s_h, n - 1)
                dve.tensor_copy(xT[u % 2][:, :], xT_ps[u % 2][:, :]).then_inc(s_xTe, 1)

            def weigh(n, u):
                dve.wait_ge(s_y, n + 1)
                dve.scalar_tensor_tensor(out=res[u][:, :], in0=y_ps[u % 2][:, :], scalar=sh["gate_of"][:, bass.ds(n, 1)],
                                         in1=xr[u][:, 0, :], op0=ALU.mult, op1=ALU.add).then_inc(s_res, 1)

            def step(n, u, left, again):
                weigh(n, u)
                if left > INDEX_AHEAD:
                    indices(n + INDEX_AHEAD, (u + INDEX_AHEAD) % ROUND, again or u + INDEX_AHEAD >= ROUND)
                if left > 2:
                    evacuate(n + 2, (u + 2) % ROUND)

            for n in range(INDEX_AHEAD):
                indices(n, n, False)
            evacuate(0, 0)
            evacuate(1, 1)
            for u in range(ROUND):
                step(u, u, ROUTED, False)
            with dve.Fori(1, ROUNDS - 1) as i:
                for u in range(ROUND):
                    step(i * ROUND + u, u, ROUTED, True)
            for u in range(ROUND):
                step(ROUTED - ROUND + u, u, ROUND - u, True)


_INS = ['x', 'ctx_1024', 'mask_Bx1xSxS2_bf1', 'L0_xattn_Wsym', 'L0_ffn_Wg', 'L0_ffn_W1', 'L0_ffn_W2']


def layout(inputs):
    import numpy as np

    arrays = {n: np.ascontiguousarray(inputs[n]) for n in _INS}
    arrays['mask_Bx1xSxS2_bf1'] = arrays['mask_Bx1xSxS2_bf1'].view(np.uint8)
    biases = [inputs[pre + n] for pre in ("L0_attn_b", "L0_xattn_b") for n in NAMES]
    arrays["biases"] = np.stack([np.asarray(b) for b in biases])
    arrays["w_self"] = np.stack([np.asarray(inputs[f"L0_attn_W{n}"]).T for n in NAMES], axis=1)
    arrays["w_cross"] = np.stack([np.asarray(inputs[f"L0_xattn_W{n}"])[0:D] for n in NAMES], axis=1)
    arrays["w_sym"] = np.stack([np.asarray(inputs[f"L0_xattn_W{n}"])[D:] for n in "qkv"], axis=1)
    arrays["scalars"] = np.concatenate([np.asarray(inputs["L0_xattn_" + n])
                                        for n in ("distance_scale", "parity_strength", "localization_length")])
    arrays["cst"], arrays["rows"] = constants()
    return arrays


def declare(nc, arrays, stop_after=3):
    args = {n: nc.dram_tensor(f"in_{n}", v.shape, mybir.dt.from_np(v.dtype), kind="ExternalInput").ap()
            for n, v in arrays.items()}
    if stop_after < 3:
        args["x3"] = nc.dram_tensor("x3", [TOKENS, D], F32, kind="ExternalOutput").ap()
    args["rec"] = nc.dram_tensor("rec", [TOKENS, 2, D], F32, kind="Internal").ap()
    args["out"] = nc.dram_tensor("out", [TOKENS, D], F32, kind="ExternalOutput").ap()
    build(nc, args, stop_after)


def kernel(**inputs):
    import concourse.bacc as bacc
    from concourse.bass_utils import run_bass_kernel_spmd

    arrays = layout(inputs)
    nc = bacc.Bacc("TRN2", target_bir_lowering=False, num_devices=1)
    declare(nc, arrays)
    r = run_bass_kernel_spmd(nc, [{f"in_{n}": v for n, v in arrays.items()}], core_ids=[0])
    return r.results[0]["out"].reshape(BATCH, SEQ, D)
```

```python
from contextlib import ExitStack

import concourse.bass as bass
from concourse import mybir
from concourse.alu_op_type import AluOpType as ALU

ACT = mybir.ActivationFunctionType
F32 = mybir.dt.float32
BF16 = mybir.dt.bfloat16
I32 = mybir.dt.int32
U32 = mybir.dt.uint32
U8 = mybir.dt.uint8
AX = mybir.AxisListType

P = 128
BATCH, SEQ, D = 128, 64, 128
HEADS = 16
HD = D // HEADS
TOKENS = BATCH * SEQ
TILES = TOKENS // P
BLOCK = 4
BLOCKS = TILES // BLOCK
EXPERTS = 8
FF = 256
CAP = TOKENS // EXPERTS
SYM = 64
EPS = 1e-5
NEG = -(2.0 ** 100)
R_NORM, R_TOKEN, R_GATE, REC = D, 2 * D, 2 * D + 1, 2 * D + 2
ROUND = 8
ROUTED = -(-(TILES + EXPERTS - 1) // 8) * 8

C_IDENT = 0
C_HEAD = C_IDENT + P
C_DECAY = C_HEAD + 4
C_DIST = C_DECAY + SEQ
C_PARITY = C_DIST + SEQ
C_SAME = C_PARITY + SEQ
C_BEFORE = C_SAME + P
C_LOWER = C_BEFORE + P
C_ONES = C_LOWER + P
C_IOTA = C_ONES + P
C_REST = C_IOTA + P
C_RUN = C_REST + EXPERTS * TILES
C_TOKEN = C_RUN + EXPERTS * TILES
C_BITS = C_TOKEN + TILES
DIGITS = 15
C_PACK = C_BITS + 3 * (DIGITS + 1)
C_COLS = C_PACK + ROUTED


def constants():
    import numpy as np

    c = np.zeros((P, C_COLS), np.float32)
    p = np.arange(P)
    c[:, C_IDENT:C_IDENT + P] = np.eye(P)
    c[p, C_HEAD + (p // HD) % 4] = 1.0
    q, k = np.arange(P)[:, None] % SEQ, np.arange(SEQ)[None, :]
    c[:, C_DECAY:C_DECAY + SEQ] = np.where(k <= q, k - q, NEG)
    c[:, C_DIST:C_DIST + SEQ] = abs(q - k)
    c[:, C_PARITY:C_PARITY + SEQ] = 1.0 - 2.0 * ((q + k) % 2)
    same = (p[:, None] % EXPERTS) == (p[None, :] % EXPERTS)
    c[:, C_SAME:C_SAME + P] = same
    c[:, C_BEFORE:C_BEFORE + P] = same & (p[:, None] < p[None, :])
    c[:, C_LOWER:C_LOWER + P] = p[:, None] < p[None, :]
    c[:, C_ONES:C_ONES + P] = 1.0
    c[:, C_IOTA:C_IOTA + P] = p[None, :]
    c[:, C_REST:C_RUN] = np.tile(EXPERTS - np.arange(EXPERTS), TILES)[None, :]
    c[:, C_RUN:C_TOKEN] = np.tile(np.arange(TILES) > 0, EXPERTS)[None, :]
    place = np.arange(TILES)
    c[:, C_TOKEN:C_BITS] = ((place % 16) * 4 + place // 16)[None, :] * P + p[:, None]
    digit = 4.0 ** np.arange(DIGITS - 1, -1, -1)
    c[:, C_BITS:C_BITS + 3 * DIGITS] = (digit[:, None] * np.array([1, 2, 3])).reshape(1, -1)
    c[:, C_PACK:C_COLS] = float(EXPERTS) ** (np.arange(ROUTED) % ROUND)
    rows = np.ones((6, BLOCK * P), np.float32)
    rows[3:] = np.arange(BLOCK * P)[None, :] % 2
    return c, rows


NAMES = ["q", "k", "v", "o"]


def after(engine, semaphore, value):
    if isinstance(value, int) and value <= 0:
        return
    engine.wait_ge(semaphore, value)


def passed(engine, semaphore):
    engine.sem_inc(semaphore, 1)


def build(nc, a):
    ctx = ExitStack()
    with ctx:
        def sb(name, shape, dt=F32):
            return ctx.enter_context(nc.sbuf_tensor(name, shape, dt))

        def sem(name):
            return ctx.enter_context(nc.semaphore(name))

        x_all = sb("x_all", [P, TILES, D])
        cst = sb("cst", [P, C_COLS])
        w1 = sb("w1", [P, EXPERTS * FF // P, P])
        w2 = sb("w2", [P, EXPERTS * FF // P, D])
        s_we = sem("s_we")
        empty = sb("empty", [P, REC])
        mean3 = sb("mean3", [P, TILES])
        rstd3 = sb("rstd3", [P, TILES])
        attention(nc, a, x_all, cst, w1, w2, s_we, empty, mean3, rstd3)
        sh = dict(experts_of=sb("experts_of", [P, ROUTED // ROUND], I32), w1=w1, w2=w2, mean3=mean3, rstd3=rstd3)
        router(nc, a, x_all, cst, sh)
        experts(nc, a, cst, sh)


def attention(nc, a, x_all, cst, w1, w2, s_we, empty, mean3, rstd3):
    ctx = ExitStack()
    with ctx:
        def sb(name, shape, dt=F32):
            return ctx.enter_context(nc.sbuf_tensor(name, shape, dt))

        def pb(name, shape):
            return ctx.enter_context(nc.psum_tensor(name, shape, F32))

        def sem(name):
            return ctx.enter_context(nc.semaphore(name))

        w_in = sb("w_in", [P, 2, 4, D])
        w_v, w_o = w_in[:, :, 2, :], w_in[:, :, 3, :]
        w_sym = sb("w_sym", [SYM, 3, D])
        b_out = sb("b_out", [P, 2, D])
        sym_in = sb("sym_in", [SYM, 1])
        sym_at = sb("sym_at", [SYM, 3, EXPERTS])
        tab = sb("tab", [8, 2, D])
        rem1 = sb("rem1", [8, 2, D])
        rem2 = sb("rem2", [8, 2, D])
        split = sb("split", [8, 2, 3, D], BF16)
        bt = sb("bt", [6, 8, D], BF16)
        rows32 = sb("rows32", [6, BLOCK * P])
        rows = sb("rows", [6, BLOCK * P], BF16)
        scal = sb("scal", [P, 3])
        sc = sb("sc", [P, 4])
        xbias = sb("xbias", [P, SEQ])
        xb1 = sb("xb1", [P, SEQ])
        xb2 = sb("xb2", [P, SEQ])
        xb3 = sb("xb3", [P, SEQ])

        ctx_in = [sb(f"ctx_in{i}", [P, BLOCK, D]) for i in range(2)]
        mask_in = [sb(f"mask_in{i}", [P, BLOCK, SEQ], U8) for i in range(2)]
        mask_f = sb("mask_f", [P, BLOCK, SEQ])
        mbias = [sb(f"mbias{i}", [P, BLOCK, SEQ]) for i in range(2)]
        stats = sb("stats", [P, BLOCK, 6])
        mv = [sb(f"mv{i}", [P, BLOCK, 2]) for i in range(2)]
        vareps = sb("vareps", [P, BLOCK])
        mhalf = sb("mhalf", [P, BLOCK])
        rstd = [sb(f"rstd{i}", [P, BLOCK]) for i in range(2)]
        stats3 = sb("stats3", [P, BLOCK, 6])
        mv3 = sb("mv3", [P, BLOCK, 2])
        vareps3 = sb("vareps3", [P, BLOCK])
        xn = sb("xn", [P, BLOCK, D])
        xT = sb("xT", [P, BLOCK, 2, SEQ])
        cT = sb("cT", [P, BLOCK, 2, SEQ])
        k_sb = sb("k_sb", [P, 2, BLOCK, SEQ])
        q_bd = [sb(f"q_bd{i}", [P, 2, BLOCK, 2, SEQ]) for i in range(2)]
        k_bd = [sb(f"k_bd{i}", [P, 2, BLOCK, 4, SEQ]) for i in range(2)]
        v_bd = [sb(f"v_bd{i}", [P, 2 * BLOCK, 8, 2, HD + 1]) for i in range(2)]
        logit = [sb(f"logit{i}", [P, HEADS, SEQ]) for i in range(4)]
        top = [sb(f"top{i}", [P, HEADS]) for i in range(4)]
        probT = [sb(f"probT{i}", [P, 8, P]) for i in range(2)]
        o_sb = sb("o_sb", [P, 8, 2, HD])
        oT = sb("oT", [P, P])
        rden = sb("rden", [P, 8, 2])

        score_ps = [pb(f"score_ps{i}", [P, HEADS, SEQ]) for i in range(2)]
        probT_ps = pb("probT_ps", [P, 8, P])
        front_ps = pb("front_ps", [P, BLOCK, P])
        out_ps = pb("out_ps", [P, 512])
        o_ps = out_ps[:, 0:288].rearrange("p (m s h e) -> p m s h e", m=8, s=2, h=2)
        oT_ps = out_ps[:, 288:288 + P]
        y_ps = out_ps[:, 288:288 + D]

        ident = cst[:, C_IDENT:C_IDENT + P]

        s_cst = sem("s_cst")
        s_x = [sem(f"s_x{i}") for i in range(4)]
        s_qz = sem("s_qz")
        s_empty = sem("s_empty")
        s_slots = sem("s_slots")
        s_w = [sem(f"s_w{i}") for i in range(2)]
        s_small = sem("s_small")
        s_symz = sem("s_symz")
        s_symps = sem("s_symps")
        s_tab = sem("s_tab")
        s_split = sem("s_split")
        s_bt = sem("s_bt")
        s_rows = sem("s_rows")
        s_xbias = sem("s_xbias")
        s_xba = sem("s_xba")
        s_vz = sem("s_vz")
        s_mhalf = sem("s_mhalf")
        s_ctx = [sem(f"s_ctx{i}") for i in range(2)]
        s_mask = [sem(f"s_mask{i}") for i in range(2)]
        s_bn = sem("s_bn")
        s_stat = sem("s_stat")
        s_veps = sem("s_veps")
        s_rstd = sem("s_rstd")
        s_ln = sem("s_ln")
        s_xT = sem("s_xT")
        s_xTe = sem("s_xTe")
        s_cT = sem("s_cT")
        s_cTe = sem("s_cTe")
        s_q = sem("s_q")
        s_qe = sem("s_qe")
        s_k = sem("s_k")
        s_ke = sem("s_ke")
        s_v = sem("s_v")
        s_ve = sem("s_ve")
        s_va = sem("s_va")
        s_kbd = sem("s_kbd")
        s_mf = sem("s_mf")
        s_mb = sem("s_mb")
        s_score = sem("s_score")
        s_logit = sem("s_logit")
        s_top = sem("s_top")
        s_sub = sem("s_sub")
        s_prob = sem("s_prob")
        s_pT = sem("s_pT")
        s_pTe = sem("s_pTe")
        s_pv = sem("s_pv")
        s_rden = sem("s_rden")
        s_norm = sem("s_norm")
        s_oT = sem("s_oT")
        s_oTe = sem("s_oTe")
        s_y = sem("s_y")
        s_bin = sem("s_bin")
        s_bo = sem("s_bo")
        s_res = sem("s_res")
        s_st = sem("s_st")
        s_bn3 = sem("s_bn3")
        s_stat3 = sem("s_stat3")
        s_mean3 = sem("s_mean3")
        s_veps3 = sem("s_veps3")
        s_rstd3 = sem("s_rstd3")
        s_passed_v = sem("s_passed_v")
        s_passed_g = sem("s_passed_g")
        s_passed_s = sem("s_passed_s")

        x_dram = a["x"].rearrange("b s d -> (b s) d").rearrange("(t p) d -> p t d", p=P)
        ctx_dram = a["ctx_1024"].rearrange("b s d -> (b s) d").rearrange("(t p) d -> p t d", p=P)
        mask_dram = a["mask_Bx1xSxS2_bf1"].rearrange("b o q k -> (b o q) k").rearrange("(t p) k -> p t k", p=P)

        X_CHUNKS = [(0, 1), (1, 2), (2, 4), (4, BLOCKS)]
        N_SMALL = 5

        PAIRS = 2 * TILES
        HALF = 2
        ITERS = 2 * BLOCKS // HALF
        MID = ITERS // 2

        def schedule(engine, body, step):
            body(0, 0, 0, True)
            with engine.Fori(1, MID - 1) as it:
                body(it * HALF, 0, 0, False)
            body((MID - 1) * HALF, 0, 1, False)
            body(MID * HALF, 1, 1, False)
            with engine.Fori(MID + 1, ITERS - 1) as it:
                body(it * HALF, 1, 1, False)
            body((ITERS - 1) * HALF, 1, None, False)

        def finished(att, block0):
            return att == 1 and not (isinstance(block0, int) and block0 == BLOCKS)

        def spread_values(par, s, h):
            src = front_ps[64 * s:64 * s + 64].rearrange("p t (m h e) -> p t m h e", m=8, h=2)[:, :, :, h, :]
            dst = v_bd[par][64 * h:64 * h + 64].rearrange("p (t s) m h e -> p t s m h e", s=2)
            return dst[:, :, s, :, h, 0:HD], src

        def steps(block0, att, nxt, first):
            for u in range(HALF * BLOCK):
                h = u // BLOCK
                ahead = att if h == 0 else nxt
                yield block0 * BLOCK + u, u, block0 + h, h, u % BLOCK, att, ahead

        block = ctx.enter_context(nc.Block())

        @block.sync
        def _(sp):
            def load_x(i):
                b0, b1 = X_CHUNKS[i]
                sp.dma_start(x_all[:, b0 * BLOCK:b1 * BLOCK, :], x_dram[:, b0 * BLOCK:b1 * BLOCK, :]).then_inc(s_x[i], 16)

            load_x(0)
            sp.dma_start(cst[:, 0:C_SAME], a["cst"][:, 0:C_SAME]).then_inc(s_cst, 16)
            sp.dma_start(tab[:, 0, :], a["biases"]).then_inc(s_small, 16)
            sp.dma_start(rows32[:, :], a["rows"]).then_inc(s_small, 16)
            sp.dma_start(scal[:, :], a["scalars"].rearrange("(o c) -> o c", o=1).to_broadcast([P, 3])).then_inc(s_small, 16)
            sp.dma_start(w_sym[:, :, :], a["w_sym"]).then_inc(s_small, 16)
            sp.dma_start(sym_in[:, :], a["L0_xattn_Wsym"].rearrange("o d -> d o")).then_inc(s_small, 16)
            sp.dma_start(w_in[:, 0, :, :], a["w_self"]).then_inc(s_w[0], 16)
            for att in range(2):
                sp.dma_start(b_out[:, att, :],
                             a["biases"][4 * att + 3:4 * att + 4, :].to_broadcast([P, D])).then_inc(s_bin, 16)
            load_x(1)
            sp.wait_ge(s_split, 5)
            for c in range(2):
                for part in range(3):
                    sp.dma_start(bt[c * 3 + part:c * 3 + part + 1, :, :], split[:, c, part, :]).then_inc(s_bt, 16)

            load_x(2)
            sp.dma_start(w_in[:, 1, :, :], a["w_cross"]).then_inc(s_w[1], 16)
            load_x(3)
            sp.dma_start(cst[:, C_SAME:C_COLS], a["cst"][:, C_SAME:C_COLS]).then_inc(s_cst, 16)

            sp.wait_ge(s_empty, 2)
            sp.dma_start(a["slots"].rearrange("(n p) r -> p n r", p=P),
                         empty[:, :].unsqueeze(1).to_broadcast([P, ROUTED, REC])).then_inc(s_slots, 16)

            def load(c, par):
                after(sp, s_cT, c - 1)
                sp.dma_start(ctx_in[par][:, :, :], ctx_dram[:, bass.ds(c * BLOCK, BLOCK), :]).then_inc(s_ctx[par], 16)
                after(sp, s_mf, c - 1)
                passed(sp, s_passed_s)
                sp.dma_start(mask_in[par][:, :, :], mask_dram[:, bass.ds(c * BLOCK, BLOCK), :]).then_inc(s_mask[par], 16)

            for c in range(2):
                load(c, c)
            with sp.Fori(1, BLOCKS // 2) as i:
                for par in range(2):
                    load(i * 2 + par, par)
            for e in range(EXPERTS):
                sp.dma_start(w1[:, e * (FF // P):(e + 1) * (FF // P), :].rearrange("p c f -> p (c f)"),
                             a["L0_ffn_W1"][e]).then_inc(s_we, 16)
                sp.dma_start(w2[:, e * (FF // P):(e + 1) * (FF // P), :],
                             a["L0_ffn_W2"][e].rearrange("(c f) d -> f c d", f=P)).then_inc(s_we, 16)
            sp.wait_ge(s_we, 2 * 16 * EXPERTS)
            sp.wait_ge(s_cst, 32)
            sp.wait_ge(s_slots, 16)

            if "x3" in a:
                sp.wait_ge(s_res, 2 * TILES)
                sp.dma_start(a["x3"].rearrange("(t p) d -> p t d", p=P), x_all[:, :, :]).then_inc(s_st, 16)
                sp.wait_ge(s_st, 16)

        @block.tensor
        def _(pe):
            pe.wait_ge(s_cst, 16)
            pe.wait_ge(s_symz, 1 + 3)
            for i in range(3):
                mm = pe.matmul(out_ps[0:8, 0:D], sym_at[:, i, :], w_sym[:, i, :], start=(i == 0), stop=(i == 2))
            mm.then_inc(s_symps, 1)

            def transpose_x(b):
                pe.wait_ge(s_ln, b + 1)
                after(pe, s_ve, b)
                after(pe, s_va, b)
                for t in range(BLOCK):
                    mm = pe.transpose(front_ps[:, t, :], xn[:, t, :], ident)
                mm.then_inc(s_xT, 1)

            def transpose_ctx(b, par):
                c = b - BLOCKS
                pe.wait_ge(s_ctx[par], (c - par) * 8 + 16)
                pe.wait_ge(s_xTe, b + 1)
                for t in range(BLOCK):
                    mm = pe.transpose(front_ps[:, t, :], ctx_in[par][:, t, :], ident)
                mm.then_inc(s_cT, 1)

            def project(t, src, signal):
                out = front_ps[:, :, :].rearrange("p t c -> p (t c)")
                att, i = t // 2, t % 2
                pe.matmul(out, bt[:, 4 * att + i, :], rows[:, :], start=True, stop=False)
                pe.matmul(out, w_in[:, att, i, :], src[:, :, :, :].rearrange("d t s q -> d (t s q)"),
                          start=False, stop=True).then_inc(signal, 1)

            def project_q(b, att):
                pe.wait_ge(s_xTe, b + 1)
                if att:
                    pe.wait_ge(s_cTe, b - BLOCKS + 1)
                project(2 * att, xT, s_q)

            def project_k(b, att):
                pe.wait_ge(s_qe, b + 1)
                project(2 * att + 1, cT if att else xT, s_k)

            def project_v(b, att):
                src = cT if att else xT
                pe.wait_ge(s_ke, b + 1)
                pe.matmul(front_ps[:, :, :], rows[:, 0:P], bt[:, 4 * att + 2, :].unsqueeze(1).to_broadcast([6, BLOCK, D]),
                          start=True, stop=False, skip_group_check=True)
                for t in range(BLOCK):
                    mm = pe.matmul(front_ps[:, t, :], src[:, t, :, :].rearrange("d s q -> d (s q)"), w_v[:, att, :],
                                   start=False, stop=(t == BLOCK - 1), skip_group_check=True)
                mm.then_inc(s_v, 1)

            def front(b, par, att, slot):
                if att is None:
                    return
                if slot == 0:
                    transpose_x(b)
                elif slot == 1 and att:
                    transpose_ctx(b, par)
                elif slot == 2:
                    project_q(b, att)
                elif slot == 4:
                    project_k(b, att)
                elif slot == 6:
                    project_v(b, att)

            def scores(n, u, b, par, t, g):
                if g == 0:
                    pe.wait_ge(s_qe, b + 1)
                    pe.wait_ge(s_kbd, b + 1)
                    after(pe, s_logit, n - 1)
                for j in range(2):
                    mm = pe.matmul(score_ps[u % 2][:, j * 8 + g * 4:j * 8 + g * 4 + 4, :],
                                   q_bd[par][64 * j:64 * j + 64, g, t, :, :], k_bd[par][64 * j:64 * j + 64, g, t, :, :],
                                   start=True, stop=True)
                if g == 1:
                    mm.then_inc(s_score, 1)

            def transpose_probs(n, u):
                pe.wait_ge(s_prob, n + 1)
                for half in range(2):
                    after(pe, s_pTe, 2 * n - 1 + half)
                    for m in range(4 * half, 4 * half + 4):
                        mm = pe.transpose(probT_ps[:, m, :], logit[u % 4][:, 2 * m:2 * m + 2, :], ident)
                    mm.then_inc(s_pT, 1)

            def values(n, u, b):
                par, t = u // BLOCK, u % BLOCK
                after(pe, s_res, n)
                pe.wait_ge(s_ve, b + 1)
                pe.wait_ge(s_va, b + 1)
                for m in range(8):
                    if m % 4 == 0:
                        pe.wait_ge(s_pTe, 2 * n + 1 + m // 4)
                    mm = pe.matmul(o_ps[:, m], probT[u % 2][:, m, :], v_bd[par][:, 2 * t:2 * t + 2, m],
                                   start=True, stop=True)
                mm.then_inc(s_pv, 1)

            def transpose_out(n):
                pe.wait_ge(s_norm, n + 1)
                pe.transpose(oT_ps, o_sb[:, :, :, :].rearrange("p m h e -> p (m h e)"), ident).then_inc(s_oT, 1)

            def project_out(n, att):
                pe.wait_ge(s_oTe, n + 1)
                pe.matmul(y_ps, oT[:, :], w_o[:, att, :], start=True, stop=True).then_inc(s_y, 1)

            for slot in range(2 * BLOCK):
                if slot == 2:
                    pe.wait_ge(s_w[0], 16)
                    pe.wait_ge(s_bt, 16 * 6)
                    pe.wait_ge(s_rows, 1)
                front(0, 0, 0, slot)
            pe.wait_ge(s_w[1], 16)

            def body(block0, att, nxt, first):
                for n, u, b, par, t, here, ahead in steps(block0, att, nxt, first):
                    if not (first and u < 2):
                        transpose_probs(n - 2, (u - 2) % 8)
                    scores(n, u, b, par, t, 0)
                    if not (first and u < 3):
                        transpose_out(n - 3)
                    scores(n, u, b, par, t, 1)
                    if not (first and u < 3):
                        late = 0 if (att == 1 and isinstance(block0, int) and block0 == BLOCKS and u < 3) else att
                        project_out(n - 3, late)
                    front(b + 1, 1 - par, ahead, 2 * t)
                    if not (first and u < 2):
                        values(n - 2, (u - 2) % 8, b if t >= 2 else b - 1)
                    front(b + 1, 1 - par, ahead, 2 * t + 1)

            schedule(pe, body, None)
            n = PAIRS
            transpose_probs(n - 2, 6)
            transpose_out(n - 3)
            project_out(n - 3, 1)
            values(n - 2, 6, 2 * BLOCKS - 1)
            transpose_probs(n - 1, 7)
            transpose_out(n - 2)
            project_out(n - 2, 1)
            values(n - 1, 7, 2 * BLOCKS - 1)
            transpose_out(n - 1)
            project_out(n - 1, 1)

        @block.scalar
        def _(act):
            act.wait_ge(s_cst, 16)
            act.wait_ge(s_small, 16 * N_SMALL)
            act.activation(xb1[:, :], cst[:, C_DIST:C_DIST + SEQ], ACT.Ln, bias=1.0).then_inc(s_xba, 1)
            act.activation(sc[:, 0:1], scal[:, 2:3], ACT.Exp).then_inc(s_xba, 1)

            def evacuate_x(b):
                after(act, s_xT, b + 1)
                act.activation(xT[:, :, :, :].rearrange("p t s q -> p t (s q)"), front_ps[:, :, :],
                               ACT.Copy).then_inc(s_xTe, 1)

            def evacuate_ctx(b):
                act.wait_ge(s_cT, b - BLOCKS + 1)
                act.activation(cT[:, :, :, :].rearrange("p t s q -> p t (s q)"), front_ps[:, :, :],
                               ACT.Copy).then_inc(s_cTe, 1)

            def quarters():
                for j in range(2):
                    for g in range(2):
                        for s in range(2):
                            yield g, s, slice(64 * j + 32 * g, 64 * j + 32 * g + 32), slice(64 * j + 32 * s,
                                                                                            64 * j + 32 * s + 32)

            def evacuate_q(b, par):
                act.wait_ge(s_q, b + 1)
                after(act, s_score, (b - 1) * BLOCK)
                for g, s, src, dst in quarters():
                    ins = act.activation(q_bd[par][dst, g, :, s, :], front_ps[src, :, 64 * s:64 * s + 64],
                                         ACT.Copy, scale=HD ** -0.5)
                ins.then_inc(s_qe, 1)

            def evacuate_k(b):
                act.wait_ge(s_k, b + 1)
                after(act, s_kbd, b)
                for g, s, src, dst in quarters():
                    ins = act.activation(k_sb[dst, g, :, :], front_ps[src, :, 64 * s:64 * s + 64], ACT.Copy)
                ins.then_inc(s_ke, 1)

            def front(b, par, att, slot):
                if att is None:
                    return
                if slot == 0:
                    evacuate_x(b)
                elif slot == 1 and att:
                    evacuate_ctx(b)
                elif slot == 2:
                    evacuate_q(b, par)
                elif slot == 4:
                    evacuate_k(b)
                elif slot == 6:
                    evacuate_v(b, par)

            def evacuate_v(b, par):
                act.wait_ge(s_v, b + 1)
                after(act, s_pv, (b - 1) * BLOCK)
                for h in range(2):
                    ins = act.activation(*spread_values(par, 1, h), ACT.Copy)
                ins.then_inc(s_va, 1)

            def exponentials(n, u):
                act.wait_ge(s_sub, n + 1)
                act.activation(logit[u % 4][:, :, :], logit[u % 4][:, :, :], ACT.Exp).then_inc(s_prob, 1)

            def evacuate_out(n):
                act.wait_ge(s_oT, n + 1)
                act.activation(oT[:, :], oT_ps, ACT.Copy).then_inc(s_oTe, 1)

            def evacuate_probs(n, u, half):
                if half == 0:
                    after(act, s_pv, n - 1)
                act.wait_ge(s_pT, 2 * n + 1 + half)
                act.activation(probT[u % 2][:, 4 * half:4 * half + 4, :], probT_ps[:, 4 * half:4 * half + 4, :],
                               ACT.Copy).then_inc(s_pTe, 1)

            for slot in range(2 * BLOCK):
                if slot == 2:
                    act.wait_ge(s_qz, 2)
                    act.wait_ge(s_vz, 6)
                front(0, 0, 0, slot)

            def body(block0, att, nxt, first):
                for n, u, b, par, t, here, ahead in steps(block0, att, nxt, first):
                    if not (first and u < 2):
                        evacuate_probs(n - 2, (u - 2) % 8, 0)
                        evacuate_probs(n - 2, (u - 2) % 8, 1)
                    if not (first and u < 3):
                        evacuate_out(n - 3)
                    if not (first and u < 1):
                        exponentials(n - 1, (u - 1) % 8)
                    front(b + 1, 1 - par, ahead, 2 * t)
                    front(b + 1, 1 - par, ahead, 2 * t + 1)

            schedule(act, body, None)
            n = PAIRS
            evacuate_probs(n - 2, 6, 0)
            evacuate_out(n - 3)
            evacuate_probs(n - 2, 6, 1)
            exponentials(n - 1, 7)
            evacuate_probs(n - 1, 7, 0)
            evacuate_out(n - 2)
            evacuate_probs(n - 1, 7, 1)
            evacuate_out(n - 1)

        @block.vector
        def _(dve):
            for i in range(2):
                dve.memset(v_bd[i][:, :, :, :, :], 0.0).then_inc(s_vz, 1)
            dve.wait_ge(s_vz, 2)
            for i in range(2):
                for h in range(2):
                    dve.memset(v_bd[i][64 * h:64 * h + 64, :, :, h, HD:HD + 1], 1.0).then_inc(s_vz, 1)

            def stats_of(n, t, b, par):
                dve.bn_stats(stats[:, t, :], x_all[:, n, :]).then_inc(s_bn, 1)

            def aggregate(b, par):
                dve.wait_ge(s_bn, BLOCK * (b + 1))
                if not isinstance(b, int) or b >= 2:
                    dve.wait_ge(s_rstd, b - 1)
                    dve.wait_ge(s_ln, b - 1)
                    passed(dve, s_passed_v)
                for t in range(BLOCK):
                    ins = dve.bn_aggr(mv[par][:, t, :], stats[:, t, :])
                ins.then_inc(s_stat, 1)

            def normalise(b, par):
                dve.wait_ge(s_rstd, b + 1)
                after(dve, s_xT, b)
                for t in range(BLOCK):
                    ins = dve.tensor_scalar(xn[:, t, :], xn_source(b, t), mv[par][:, t, 0:1], rstd[par][:, t:t + 1],
                                            ALU.subtract, ALU.mult)
                ins.then_inc(s_ln, 1)

            def tile_of(b, t):
                return (b * BLOCK + t) % TILES if isinstance(b, int) else b * BLOCK + t

            shift = [0]

            def xn_source(b, t):
                n = tile_of(b, t)
                return x_all[:, n, :] if isinstance(n, int) else x_all[:, bass.ds(n - shift[0], 1), :].rearrange(
                    "p o d -> p (o d)")

            def stat_source(b, t):
                return xn_source(b, t)

            for b in range(2):
                dve.wait_ge(s_x[b], 16)
                for t in range(BLOCK):
                    dve.bn_stats(stats[:, t, :], stat_source(b, t)).then_inc(s_bn, 1)
                aggregate(b, b)
                if b == 0:
                    dve.wait_ge(s_stat, 1)
            dve.wait_ge(s_cst, 16)
            normalise(0, 0)

            dve.wait_ge(s_small, 16 * N_SMALL)
            dve.wait_ge(s_symz, 1)
            for i in range(3):
                dve.tensor_copy(sym_at[:, i, 4 + i:5 + i], sym_in[:, :]).then_inc(s_symz, 1)

            dve.wait_ge(s_symps, 1)
            dve.tensor_copy(tab[:, 1, :], out_ps[0:8, 0:D]).then_inc(s_tab, 1)
            dve.tensor_copy(rows[:, :], rows32[:, :]).then_inc(s_rows, 1)
            dve.wait_ge(s_tab, 1)
            dve.tensor_copy(split[:, :, 0, :], tab[:, :, :]).then_inc(s_split, 1)
            dve.wait_ge(s_split, 1)
            dve.tensor_tensor(rem1[:, :, :], tab[:, :, :], split[:, :, 0, :], ALU.subtract).then_inc(s_split, 1)
            dve.wait_ge(s_split, 2)
            dve.tensor_copy(split[:, :, 1, :], rem1[:, :, :]).then_inc(s_split, 1)
            dve.wait_ge(s_split, 3)
            dve.tensor_tensor(rem2[:, :, :], rem1[:, :, :], split[:, :, 1, :], ALU.subtract).then_inc(s_split, 1)
            dve.wait_ge(s_split, 4)
            dve.tensor_copy(split[:, :, 2, :], rem2[:, :, :]).then_inc(s_split, 1)
            dve.wait_ge(s_xba, 2)
            dve.reciprocal(sc[:, 1:2], sc[:, 0:1]).then_inc(s_xbias, 1)
            dve.tensor_scalar(xb1[:, :], xb1[:, :], scal[:, 0:1], None, ALU.mult).then_inc(s_xbias, 1)
            dve.wait_ge(s_xbias, 2)
            dve.scalar_tensor_tensor(out=xb2[:, :], in0=cst[:, C_PARITY:C_PARITY + SEQ], scalar=scal[:, 1:2],
                                     in1=xb1[:, :], op0=ALU.mult, op1=ALU.add).then_inc(s_xbias, 1)
            dve.tensor_scalar(xb3[:, :], cst[:, C_DIST:C_DIST + SEQ], sc[:, 1:2], None, ALU.mult).then_inc(s_xbias, 1)
            dve.wait_ge(s_xbias, 4)
            dve.tensor_tensor(xb2[:, :], xb2[:, :], xb3[:, :], ALU.subtract).then_inc(s_xbias, 1)
            dve.wait_ge(s_xbias, 5)
            dve.tensor_scalar(xbias[:, :], xb2[:, :], float(HD) ** -0.5, None, ALU.mult).then_inc(s_xbias, 1)

            def evacuate_v(b, par):
                dve.wait_ge(s_v, b + 1)
                after(dve, s_pv, (b - 1) * BLOCK)
                for h in range(2):
                    ins = dve.tensor_copy(*spread_values(par, 0, h))
                ins.then_inc(s_ve, 1)

            def front(b, par, att, t):
                if att is not None and t == BLOCK - 1:
                    evacuate_v(b, par)

            def add_bias(n, u, par, t, att):
                dve.wait_ge(s_score, n + 1)
                after(dve, s_pT, 2 * (n - 3))
                if att:
                    dve.wait_ge(s_mb, (n - t) // BLOCK - BLOCKS + 1 if isinstance(n, int) else block_of(n, t) - BLOCKS + 1)
                bias = mbias[par][:, t, :] if att else cst[:, C_DECAY:C_DECAY + SEQ]
                dve.tensor_tensor(logit[u % 4][:, :, :], score_ps[u % 2][:, :, :],
                                  bias.unsqueeze(1).to_broadcast([P, HEADS, SEQ]), ALU.add).then_inc(s_logit, 1)

            cur = [None]

            def block_of(n, t):
                return cur[0]

            def maximum(n, u):
                dve.wait_ge(s_logit, n + 1)
                dve.tensor_reduce(top[u % 4][:, :], logit[u % 4][:, :, :], AX.X, ALU.max).then_inc(s_top, 1)

            def normalise_out(n):
                dve.wait_ge(s_pv, n + 1)
                after(dve, s_norm, n)
                dve.reciprocal(rden[:, :, :], o_ps[:, :, 0, :, HD]).then_inc(s_rden, 1)
                dve.wait_ge(s_rden, n + 1)
                for s in range(2):
                    r = slice(64 * s, 64 * s + 64)
                    ins = dve.tensor_tensor(o_sb[r, :, :, :], o_ps[r, :, s, :, 0:HD],
                                            rden[r, :, :].unsqueeze(3).to_broadcast([64, 8, 2, HD]), ALU.mult)
                ins.then_inc(s_norm, 1)

            def residual(n, off, b):
                dve.wait_ge(s_bo, b + 1)
                dve.wait_ge(s_y, n + 1)
                if isinstance(n, int):
                    x = x_all[:, n % TILES, :]
                else:
                    x = x_all[:, bass.ds(n - off, 1), :].rearrange("p o d -> p (o d)")
                dve.tensor_tensor(x, x, y_ps, ALU.add).then_inc(s_res, 1)

            def final_stats(b):
                j = b - BLOCKS - 2
                dve.wait_ge(s_res, (b - 1) * BLOCK)
                after(dve, s_stat3, j)
                for t in range(BLOCK):
                    x = x_all[:, bass.ds(j * BLOCK + t, 1), :].rearrange("p o d -> p (o d)")
                    dve.bn_stats(stats3[:, t, :], x).then_inc(s_bn3, 1)
                dve.wait_ge(s_bn3, BLOCK * (j + 1))
                after(dve, s_veps3, j)
                after(dve, s_mean3, j)
                passed(dve, s_passed_v)
                for t in range(BLOCK):
                    ins = dve.bn_aggr(mv3[:, t, :], stats3[:, t, :])
                ins.then_inc(s_stat3, 1)
                dve.wait_ge(s_stat3, j + 1)
                dve.tensor_copy(mean3[:, bass.ds(j * BLOCK, BLOCK)], mv3[:, :, 0]).then_inc(s_mean3, 1)

            evacuate_v(0, 0)
            normalise(1, 1)

            def body(block0, att, nxt, first):
                static = isinstance(block0, int)
                for n, u, b, par, t, here, ahead in steps(block0, att, nxt, first):
                    cur[0] = b
                    shift[0] = TILES if att else 0
                    if not (first and u < 3):
                        residual(n - 3, TILES if att else 0, b if t == 3 else b - 1)
                    add_bias(n, u, par, t, att)
                    maximum(n, u)
                    if not (first and u < 2):
                        normalise_out(n - 2)
                    front(b + 1, 1 - par, ahead, t)
                    if t == BLOCK - 1 and not (static and b + 2 >= 2 * BLOCKS):
                        normalise(b + 2, par)
                    if t == 0 and finished(att, block0):
                        final_stats(b)
                    stats_ahead = not (static and block0 + par + 2 >= 2 * BLOCKS)
                    if stats_ahead and t < BLOCK - 1:
                        if first and par == 0 and t == 0:
                            dve.wait_ge(s_x[2], 16)
                        if t == 0:
                            dve.wait_ge(s_stat, b + 2)
                        for k in (t, t + 1) if t == BLOCK - 2 else (t,):
                            if static:
                                src = x_all[:, ((b + 2) * BLOCK + k) % TILES, :]
                            else:
                                src = x_all[:, bass.ds((b + 2) * BLOCK + k - shift[0], 1), :].rearrange("p o d -> p (o d)")
                            dve.bn_stats(stats[:, k, :], src).then_inc(s_bn, 1)
                        if t == BLOCK - 2:
                            aggregate(b + 2, par)
                if first:
                    dve.wait_ge(s_x[3], 16)

            schedule(dve, body, None)
            n = PAIRS
            residual(n - 3, 0, 2 * BLOCKS - 1)
            normalise_out(n - 2)
            residual(n - 2, 0, 2 * BLOCKS - 1)
            normalise_out(n - 1)
            residual(n - 1, 0, 2 * BLOCKS - 1)

        @block.gpsimd
        def _(pool):
            pool.memset(mhalf[:, :], -0.5).then_inc(s_mhalf, 1)
            pool.memset(sym_at[:, :, :], 0.0).then_inc(s_symz, 1)
            pool.memset(empty[:, :], 0.0).then_inc(s_empty, 1)
            pool.wait_ge(s_empty, 1)
            pool.memset(empty[:, R_TOKEN:R_TOKEN + 1].bitcast(I32), TOKENS).then_inc(s_empty, 1)
            for i in range(2):
                pool.memset(q_bd[i][:, :, :, :, :], 0.0).then_inc(s_qz, 1)
            pool.wait_ge(s_mhalf, 1)

            def inverse_deviation(b, par):
                pool.wait_ge(s_stat, b + 1)
                after(pool, s_rstd, b)
                passed(pool, s_passed_g)
                pool.tensor_scalar(vareps[:, :], mv[par][:, :, 1], EPS, 1.0, ALU.add, ALU.mult).then_inc(s_veps, 1)
                pool.wait_ge(s_veps, b + 1)
                after(pool, s_ln, b - 1)
                pool.tensor_tensor(rstd[par][:, :], vareps[:, :], mhalf[:, :], ALU.pow).then_inc(s_rstd, 1)

            def spread_k(b, par):
                pool.wait_ge(s_ke, b + 1)
                after(pool, s_score, (b - 1) * BLOCK)
                passed(pool, s_passed_g)
                for h in range(4):
                    dst = k_bd[par][:, :, :, h, :].rearrange("p g t q -> p (g t) q")
                    ins = pool.tensor_scalar(dst, k_sb[:, :, :, :].rearrange("p g t q -> p (g t) q"),
                                             cst[:, C_HEAD + h:C_HEAD + h + 1], 1.0, ALU.mult, ALU.mult)
                ins.then_inc(s_kbd, 1)

            def mask_bias(b, par):
                c = b - BLOCKS
                pool.wait_ge(s_mask[par], (c - par) * 8 + 16)
                after(pool, s_mb, c)
                passed(pool, s_passed_g)
                pool.tensor_scalar(mask_f[:, :, :], mask_in[par][:, :, :], -1.0, -NEG, ALU.add, ALU.mult).then_inc(s_mf, 1)
                pool.wait_ge(s_mf, c + 1)
                pool.wait_ge(s_xbias, 6)
                pool.wait_ge(s_logit, (b - 1) * BLOCK)
                pool.tensor_tensor(mbias[par][:, :, :], mask_f[:, :, :],
                                   xbias[:, :].unsqueeze(1).to_broadcast([P, BLOCK, SEQ]), ALU.add).then_inc(s_mb, 1)

            def front(b, par, att, slot):
                if att is None:
                    return
                if slot == 2:
                    add_out_bias(b, att)
                elif slot == 4:
                    spread_k(b, par)
                elif slot == 6 and att:
                    mask_bias(b, par)

            def add_out_bias(b, att):
                pool.wait_ge(s_ln, b + 1)
                if isinstance(b, int):
                    at = slice(b % BLOCKS * BLOCK, b % BLOCKS * BLOCK + BLOCK)
                else:
                    at = bass.ds((b - BLOCKS * att) * BLOCK, BLOCK)
                pool.tensor_tensor(x_all[:, at, :], x_all[:, at, :],
                                   b_out[:, att, :].unsqueeze(1).to_broadcast([P, BLOCK, D]), ALU.add).then_inc(s_bo, 1)

            def final_deviation(b):
                j = b - BLOCKS - 2
                pool.wait_ge(s_stat3, j + 1)
                after(pool, s_rstd3, j)
                passed(pool, s_passed_g)
                pool.tensor_scalar(vareps3[:, :], mv3[:, :, 1], EPS, 1.0, ALU.add, ALU.mult).then_inc(s_veps3, 1)
                pool.wait_ge(s_veps3, j + 1)
                pool.tensor_tensor(rstd3[:, bass.ds(j * BLOCK, BLOCK)], vareps3[:, :], mhalf[:, :],
                                   ALU.pow).then_inc(s_rstd3, 1)

            def subtract_max(n, u):
                pool.wait_ge(s_top, n + 1)
                pool.tensor_tensor(logit[u % 4][:, :, :], logit[u % 4][:, :, :],
                                   top[u % 4][:, :].unsqueeze(2).to_broadcast([P, HEADS, SEQ]),
                                   ALU.subtract).then_inc(s_sub, 1)

            inverse_deviation(0, 0)
            inverse_deviation(1, 1)
            pool.wait_ge(s_bin, 32)
            pool.wait_ge(s_cst, 16)
            for slot in range(2 * BLOCK):
                front(0, 0, 0, slot)

            def body(block0, att, nxt, first):
                static = isinstance(block0, int)
                for n, u, b, par, t, here, ahead in steps(block0, att, nxt, first):
                    if t == BLOCK - 1 and not (static and block0 + par + 2 >= 2 * BLOCKS):
                        inverse_deviation(b + 2, par)
                    subtract_max(n, u)
                    if t == 1 and finished(att, block0):
                        final_deviation(b)
                    front(b + 1, 1 - par, ahead, 2 * t)
                    front(b + 1, 1 - par, ahead, 2 * t + 1)

            schedule(pool, body, None)


def router(nc, a, x_all, cst, sh):
    ctx = ExitStack()
    with ctx:
        def sb(name, shape, dt=F32):
            return ctx.enter_context(nc.sbuf_tensor(name, shape, dt))

        def pb(name, shape):
            return ctx.enter_context(nc.psum_tensor(name, shape, F32))

        def sem(name):
            return ctx.enter_context(nc.semaphore(name))

        E, HI = EXPERTS, 4
        LO = TILES // HI
        w_g = sb("w_g", [P, E])
        LAST = 2
        FROM = (BLOCKS - LAST) * BLOCK
        stats = sb("r_stats", [P, LAST * BLOCK, 6])
        mv = sb("r_mv", [P, LAST * BLOCK, 2])
        vareps = sb("r_vareps", [P, LAST * BLOCK])
        mhalf = sb("r_mhalf", [P, LAST * BLOCK])
        xn_now = [sb(f"r_xn_now{i}", [P, BLOCK, D]) for i in range(2)]
        xn = sb("r_xn", [P, TILES, D])
        xT = [sb(f"r_xT{i}", [P, BLOCK, P]) for i in range(2)]
        row = [sb(f"r_row{i}", [E, BLOCK * P]) for i in range(2)]
        logits = sb("logits", [P, TILES, E])
        tmax = sb("tmax", [P, TILES])
        tsum = sb("tsum", [P, TILES])
        prob = sb("prob", [P, HI, LO, E])
        lane = sb("lane", [P, HI * P])
        flags = sb("flags", [P, 3, HI * P])
        ones = sb("ones", [P, HI * P])
        digits = sb("digits", [P, 3 * (DIGITS + 1)], I32)
        count = sb("count", [P, 3])
        thr = sb("thr", [P, 1], I32)
        cand = sb("cand", [P, 3], I32)
        kept = sb("kept", [P, 3])
        keep = sb("keep", [P, 1], I32)
        above = sb("above", [P, HI * P])
        equal = sb("equal", [P, HI * P])
        rank = sb("rank", [P, HI * P])
        low = sb("low", [P, HI * P])
        tie = sb("tie", [P, HI * P])
        chosen = sb("chosen", [P, HI * P])
        n_above = sb("n_above", [P, 1])
        need = sb("need", [P, 1])
        before = sb("before", [P, 1])
        free = sb("free", [P, TILES])
        allow = sb("allow", [P, TILES, E])
        key0 = sb("key0", [P, TILES, E])
        key = sb("key", [P, TILES, E])
        gate = sb("gate", [P, TILES])
        hit = sb("hit", [P, TILES, E])
        hit2 = sb("hit2", [P, TILES, E])
        first = sb("first", [P, TILES])
        onehot = sb("onehot", [P, TILES, E])
        total = sb("total", [P, E, TILES])
        runs = sb("runs", [P, E, TILES])
        excl = sb("excl", [P, E, TILES])
        n_tiles_i = sb("n_tiles_i", [P, E], I32)
        n_tiles_s = sb("n_tiles_s", [P, E], I32)
        n_tiles = sb("n_tiles", [P, E])
        last_tile = sb("last_tile", [P, E])
        base = sb("base", [P, E])
        base2 = sb("base2", [P, E])
        place3 = sb("place3", [P, E, TILES])
        place2 = sb("place2", [P, TILES, E])
        place1 = sb("place1", [P, TILES, E])
        place = sb("place", [P, TILES])
        place_i = sb("place_i", [P, TILES], I32)
        token_i = sb("token_i", [P, TILES], I32)
        owner = sb("owner", [P, ROUTED, E])
        owner1 = sb("owner1", [P, ROUTED])
        owner2 = sb("owner2", [P, ROUTED])
        owner3 = sb("owner3", [P, ROUTED])
        packed = sb("packed", [P, ROUTED // ROUND])
        record = [sb(f"record{i}", [P, REC]) for i in range(ROUND)]
        slot_of = [sb(f"slot_of{i}", [P, 1], I32) for i in range(ROUND)]

        xT_ps = [pb(f"xT_ps{i}", [P, BLOCK, P]) for i in range(2)]
        logit_ps = [pb(f"logit_ps{i}", [P, BLOCK, E]) for i in range(2)]
        lane_ps = pb("lane_ps", [P, HI, P])
        count_ps = pb("count_ps", [P, 8])
        rank_ps = pb("rank_ps", [P, TILES, E])
        total_ps = pb("total_ps", [P, TILES, E])
        row_ps = [x[:, :, :].rearrange("p t e -> p (t e)") for x in (rank_ps, total_ps)]

        ident = cst[:, C_IDENT:C_IDENT + P]
        same = cst[:, C_SAME:C_SAME + P]

        s_w = sem("r_w")
        s_mh = sem("r_mh")
        s_bn = sem("r_bn")
        s_stat = sem("r_stat")
        s_veps = sem("r_veps")
        s_mean = sem("r_mean")
        s_rstd = sem("r_rstd_s")
        s_ln = sem("r_ln")
        s_xT = sem("r_xTs")
        s_xTe = sem("r_xTe")
        s_row = sem("r_row")
        s_rowe = sem("r_rowe")
        s_lg = sem("r_lg")
        s_lge = sem("r_lge")
        s_kept = sem("r_kept")
        s_moved = sem("r_moved")
        s_places = sem("r_places")
        s_stored = [sem(f"r_stored{i}") for i in range(ROUND)]
        s_sm = sem("r_sm")
        s_exp = sem("r_exp")
        s_shift = sem("r_shift")
        s_prob = sem("r_prob")
        s_lane = sem("r_lane")
        s_cnt = sem("r_cnt")
        s_tot = sem("r_tot")
        s_reach = sem("r_reach")
        s_keep = sem("r_keep")
        s_thr = sem("r_thr")
        s_cand = sem("r_cand")
        s_above = sem("r_above")
        s_above_t = sem("r_above_t")
        s_eq = sem("r_eq")
        s_before = sem("r_before")
        s_chosen = sem("r_chosen")
        s_sel = sem("r_sel")
        s_onehot = sem("r_onehot")
        s_rank = sem("r_rank")
        s_place = sem("r_place")
        s_passed_g = sem("r_passed_g")
        s_passed_p = sem("r_passed_p")

        UNROLL = 5

        def stored(n, u):
            return (n - u) * (16 // ROUND) + 16

        block = ctx.enter_context(nc.Block())

        @block.sync
        def _(sp):
            sp.dma_start(w_g[:, :], a["L0_ffn_Wg"]).then_inc(s_w, 16)


        @block.gpsimd
        def _(pool):
            pool.memset(mhalf[:, :], -0.5).then_inc(s_mh, 1)
            pool.wait_ge(s_mh, 1)

            pool.wait_ge(s_stat, 1)
            pool.tensor_scalar(vareps[:, :], mv[:, :, 1], EPS, 1.0, ALU.add, ALU.mult).then_inc(s_veps, 1)
            pool.wait_ge(s_veps, 1)
            pool.tensor_tensor(sh["rstd3"][:, FROM:TILES], vareps[:, :], mhalf[:, :], ALU.pow).then_inc(s_rstd, 1)

            def store(n, u):
                pool.wait_ge(s_moved, n + 1)
                pool.wait_ge(s_places, n + 1)
                passed(pool, s_passed_g)
                pool.indirect_dma_start(a["slots"], bass.IndirectOffsetOnAxis(ap=slot_of[u][:, :].bitcast(U32), axis=0),
                                        record[u][:, :], None).then_inc(s_stored[u], 16)

            for u in range(ROUND):
                store(u, u)
            with pool.Fori(1, TILES // ROUND) as i:
                for u in range(ROUND):
                    store(i * ROUND + u, u)
            for u in range(ROUND):
                pool.wait_ge(s_stored[u], 16 * (TILES // ROUND))

        @block.scalar
        def _(act):
            def evacuate(b, par):
                act.wait_ge(s_xT, b + 1)
                after(act, s_row, b - 1)
                act.activation(xT[par][:, :, :], xT_ps[par][:, :, :], ACT.Copy).then_inc(s_xTe, 1)

            def evacuate_row(b, par):
                act.wait_ge(s_row, b + 1)
                after(act, s_lg, b - 1)
                act.activation(row[par][:, :], row_ps[par][0:E, :], ACT.Copy).then_inc(s_rowe, 1)

            def take_logits(b, par):
                act.wait_ge(s_lg, b + 1)
                act.activation(logits[:, bass.ds(b * BLOCK, BLOCK), :], logit_ps[par][:, :, :], ACT.Copy).then_inc(s_lge, 1)

            evacuate(0, 0)
            evacuate(1, 1)
            evacuate_row(0, 0)
            with act.Fori(1, BLOCKS // 2) as i:
                for par in range(2):
                    b = i * 2 + par
                    evacuate(b, par)
                    evacuate_row(b - 1, 1 - par)
                    take_logits(b - 2, par)
            evacuate_row(BLOCKS - 1, 1)
            take_logits(BLOCKS - 2, 0)
            take_logits(BLOCKS - 1, 1)
            act.wait_ge(s_shift, 1)
            act.activation(logits[:, :, :], logits[:, :, :], ACT.Exp).then_inc(s_exp, 1)

            act.wait_ge(s_kept, BLOCKS)

            def move(n, u, again):
                if again:
                    act.wait_ge(s_stored[u], stored(n, u) - 16)
                for at, rows in ((0, x_all), (R_NORM, xn)):
                    ins = act.activation(record[u][:, at:at + D], rows[:, bass.ds(n, 1), :].rearrange("p o d -> p (o d)"),
                                         ACT.Copy)
                ins.then_inc(s_moved, 1)

            for u in range(ROUND):
                move(u, u, False)
            with act.Fori(1, TILES // ROUND) as i:
                for u in range(ROUND):
                    move(i * ROUND + u, u, True)

        @block.tensor
        def _(pe):
            pe.wait_ge(s_w, 16)

            def transpose(b, par):
                pe.wait_ge(s_ln, b + 1)
                after(pe, s_xTe, b - 1)
                for t in range(BLOCK):
                    mm = pe.transpose(xT_ps[par][:, t, :], xn_now[par][:, t, :], ident)
                mm.then_inc(s_xT, 1)

            def project(b, par):
                pe.wait_ge(s_xTe, b + 1)
                after(pe, s_rowe, b - 1)
                pe.matmul(row_ps[par][0:E, :], w_g[:, :], xT[par][:, :, :].rearrange("d t c -> d (t c)"),
                          start=True, stop=True).then_inc(s_row, 1)

            def turn(b, par):
                pe.wait_ge(s_rowe, b + 1)
                after(pe, s_lge, b - 1)
                passed(pe, s_passed_p)
                for t in range(BLOCK):
                    mm = pe.transpose(logit_ps[par][:, t, :], row[par][:, t * P:t * P + P], ident[0:E, 0:E])
                mm.then_inc(s_lg, 1)

            transpose(0, 0)
            transpose(1, 1)
            project(0, 0)
            def pair(i):
                for par in range(2):
                    b = i * 2 + par
                    transpose(b, par)
                    project(b - 1, 1 - par)
                    turn(b - 2, par)

            pair(1)
            with pe.Fori(2, BLOCKS // 2) as i:
                pair(i)
            project(BLOCKS - 1, 1)
            turn(BLOCKS - 2, 0)
            turn(BLOCKS - 1, 1)

            pe.wait_ge(s_prob, 1)
            for h in range(HI):
                mm = pe.transpose(lane_ps[:, h, :], prob[:, h, :, :].rearrange("p l e -> p (l e)"), ident)
            mm.then_inc(s_lane, 1)

            with pe.Fori(0, DIGITS // UNROLL) as i:
                for k in range(UNROLL):
                    pe.wait_ge(s_cnt, i * UNROLL + (k + 1))
                    pe.matmul(count_ps[:, 0:3], same, count[:, :], start=True, stop=True).then_inc(s_tot, 1)
            pe.wait_ge(s_above, 1)
            pe.matmul(count_ps[:, 4:5], same, n_above[:, :], start=True, stop=True).then_inc(s_above_t, 1)
            pe.wait_ge(s_eq, 2)
            pe.wait_ge(s_above, 2)
            pe.matmul(count_ps[:, 5:6], cst[:, C_BEFORE:C_BEFORE + P], rank[:, HI * P - 1:HI * P],
                      start=True, stop=True).then_inc(s_before, 1)
            pe.wait_ge(s_chosen, 1)
            for h in range(HI):
                mm = pe.transpose(lane_ps[:, h, :], chosen[:, h * P:h * P + P], ident)
            mm.then_inc(s_sel, 1)
            pe.wait_ge(s_onehot, 1)
            pe.matmul(rank_ps[:, :, :], cst[:, C_LOWER:C_LOWER + P], onehot[:, :, :], start=True, stop=True)
            pe.matmul(total_ps[:, :, :], cst[:, C_ONES:C_ONES + P], onehot[:, :, :],
                      start=True, stop=True).then_inc(s_rank, 1)

        @block.vector
        def _(dve):
            for t in range(LAST * BLOCK):
                dve.bn_stats(stats[:, t, :], x_all[:, FROM + t, :]).then_inc(s_bn, 1)
            dve.wait_ge(s_bn, LAST * BLOCK)
            for t in range(LAST * BLOCK):
                ins = dve.bn_aggr(mv[:, t, :], stats[:, t, :])
            ins.then_inc(s_stat, 1)
            dve.wait_ge(s_stat, 1)
            dve.tensor_copy(sh["mean3"][:, FROM:TILES], mv[:, :, 0]).then_inc(s_mean, 1)
            dve.wait_ge(s_mean, 1)

            def normalise(b, par):
                after(dve, s_xT, b - 1)
                for t in range(BLOCK):
                    x = x_all[:, bass.ds(b * BLOCK + t, 1), :].rearrange("p o d -> p (o d)")
                    at = bass.ds(b * BLOCK + t, 1)
                    ins = dve.tensor_scalar(xn_now[par][:, t, :], x, sh["mean3"][:, at], sh["rstd3"][:, at],
                                            ALU.subtract, ALU.mult)
                ins.then_inc(s_ln, 1)
                dve.wait_ge(s_ln, b + 1)
                dve.tensor_copy(xn[:, bass.ds(b * BLOCK, BLOCK), :], xn_now[par][:, :, :]).then_inc(s_kept, 1)

            normalise(0, 0)
            normalise(1, 1)
            with dve.Fori(1, BLOCKS // 2 - 1) as i:
                for par in range(2):
                    normalise(i * 2 + par, par)
            dve.wait_ge(s_rstd, 1)
            normalise(BLOCKS - 2, 0)
            normalise(BLOCKS - 1, 1)

            chain = [0]

            def link(ins):
                chain[0] += 1
                ins.then_inc(s_sm, 1)
                dve.wait_ge(s_sm, chain[0])

            def by_tile(x):
                return x.unsqueeze(2).to_broadcast([P, TILES, E])

            dve.wait_ge(s_lge, BLOCKS)
            link(dve.tensor_reduce(tmax[:, :], logits[:, :, :], AX.X, ALU.max))
            dve.tensor_tensor(logits[:, :, :], logits[:, :, :], by_tile(tmax[:, :]), ALU.subtract).then_inc(s_shift, 1)
            dve.wait_ge(s_exp, 1)
            link(dve.tensor_reduce(tsum[:, :], logits[:, :, :], AX.X, ALU.add))
            link(dve.reciprocal(tsum[:, :], tsum[:, :]))
            dve.tensor_tensor(prob[:, :, :, :].rearrange("p h l e -> p l h e"),
                              logits[:, :, :].rearrange("p (l h) e -> p l h e", h=HI),
                              tsum[:, :].rearrange("p (l h) -> p l h", h=HI).unsqueeze(3).to_broadcast([P, LO, HI, E]),
                              ALU.mult).then_inc(s_prob, 1)

            digits_f = cst[:, C_BITS:C_PACK]
            link(dve.tensor_copy(digits[:, :], digits_f))
            link(dve.memset(ones[:, :], 1.0))
            link(dve.memset(thr[:, :], 0))
            dve.tensor_copy(cand[:, :], digits[:, 0:3]).then_inc(s_cand, 1)
            dve.wait_ge(s_lane, 1)
            link(dve.tensor_copy(lane[:, :], lane_ps[:, :, :].rearrange("p h t -> p (h t)")))
            with dve.Fori(0, DIGITS // UNROLL) as i:
                for k in range(UNROLL):
                    n = i * UNROLL + k
                    dve.wait_ge(s_cand, n + 1)
                    for c in range(3):
                        ins = dve.tensor_scalar(flags[:, c, :], lane[:, :], cand[:, c:c + 1].bitcast(F32), None, ALU.is_ge,
                                                ALU.add, accum_out=count[:, c:c + 1])
                    ins.then_inc(s_cnt, 1)
                    dve.wait_ge(s_tot, n + 1)
                    dve.scalar_tensor_tensor(out=kept[:, :], in0=count_ps[:, 0:3], scalar=float(CAP),
                                             in1=cst[:, bass.ds(n * 3 + C_BITS, 3)],
                                             op0=ALU.is_ge, op1=ALU.mult).then_inc(s_reach, 1)
                    dve.wait_ge(s_reach, n + 1)
                    dve.tensor_reduce(keep[:, :], kept[:, :], AX.X, ALU.max).then_inc(s_keep, 1)
                    dve.wait_ge(s_keep, n + 1)
                    dve.tensor_tensor(thr[:, :], thr[:, :], keep[:, :], ALU.bitwise_or).then_inc(s_thr, 1)
                    dve.wait_ge(s_thr, n + 1)
                    dve.tensor_tensor(cand[:, :], thr[:, :].to_broadcast([P, 3]), digits[:, bass.ds(n * 3 + 3, 3)],
                                      ALU.bitwise_or).then_inc(s_cand, 1)
            dve.wait_ge(s_cand, DIGITS + 1)
            level = thr[:, :].bitcast(F32)
            dve.tensor_scalar(above[:, :], lane[:, :], level, None, ALU.is_gt, ALU.add,
                              accum_out=n_above[:, :]).then_inc(s_above, 1)
            dve.tensor_scalar(equal[:, :], lane[:, :], level, None, ALU.is_equal).then_inc(s_eq, 1)
            dve.wait_ge(s_above_t, 1)
            dve.tensor_scalar(need[:, :], count_ps[:, 4:5], -1.0, float(CAP), ALU.mult, ALU.add).then_inc(s_above, 1)
            dve.wait_ge(s_eq, 1)
            dve.tensor_tensor_scan(rank[:, :], ones[:, :], equal[:, :], 0.0, ALU.mult, ALU.add).then_inc(s_eq, 1)
            dve.wait_ge(s_before, 1)
            dve.wait_ge(s_eq, 2)
            dve.wait_ge(s_above, 2)
            link(dve.tensor_copy(before[:, :], count_ps[:, 5:6]))
            link(dve.tensor_scalar(low[:, :], rank[:, :], before[:, :], need[:, :], ALU.add, ALU.is_le))
            link(dve.tensor_tensor(tie[:, :], equal[:, :], low[:, :], ALU.mult))
            dve.tensor_tensor(chosen[:, :], above[:, :], tie[:, :], ALU.add).then_inc(s_chosen, 1)

            pr = prob[:, :, :, :].rearrange("p h l e -> p (h l) e")
            dve.wait_ge(s_sel, 1)
            sel = lane_ps[:, :, :].rearrange("p h (l e) -> p (h l) e", e=E)
            link(dve.tensor_reduce(first[:, :], sel, AX.X, ALU.max))
            link(dve.tensor_scalar(free[:, :], first[:, :], -1.0, 1.0, ALU.mult, ALU.add))
            link(dve.tensor_tensor(allow[:, :, :], sel, by_tile(free[:, :]), ALU.max))
            link(dve.tensor_tensor(key0[:, :, :], pr, allow[:, :, :], ALU.mult))
            link(dve.scalar_tensor_tensor(out=key[:, :, :], in0=allow[:, :, :], scalar=-1.0, in1=key0[:, :, :],
                                          op0=ALU.add, op1=ALU.add))
            link(dve.tensor_reduce(gate[:, :], key[:, :, :], AX.X, ALU.max))
            link(dve.tensor_tensor(hit[:, :, :], key[:, :, :], by_tile(gate[:, :]), ALU.is_equal))
            link(dve.tensor_tensor(hit2[:, :, :], hit[:, :, :],
                                   cst[:, C_REST:C_RUN].rearrange("p (t e) -> p t e", e=E), ALU.mult))
            link(dve.tensor_reduce(first[:, :], hit2[:, :, :], AX.X, ALU.max))
            dve.tensor_tensor(onehot[:, :, :], hit2[:, :, :], by_tile(first[:, :]), ALU.is_equal).then_inc(s_onehot, 1)

            dve.wait_ge(s_rank, 1)
            dve.wait_ge(s_onehot, 1)
            link(dve.tensor_copy(total[:, :, :], total_ps[:, :, :].rearrange("p t e -> p e t")))
            link(dve.tensor_tensor_scan(runs[:, :, :].rearrange("p e t -> p (e t)"), cst[:, C_RUN:C_TOKEN],
                                        total[:, :, :].rearrange("p e t -> p (e t)"), 0.0, ALU.mult, ALU.add))
            link(dve.tensor_tensor(excl[:, :, :], runs[:, :, :], total[:, :, :], ALU.subtract))
            link(dve.tensor_scalar(n_tiles_i[:, :], runs[:, :, TILES - 1], float(P - 1), None, ALU.add))
            link(dve.tensor_scalar(n_tiles_s[:, :], n_tiles_i[:, :], 7, None, ALU.logical_shift_right))
            link(dve.tensor_copy(n_tiles[:, :], n_tiles_s[:, :]))
            link(dve.tensor_tensor_scan(last_tile[:, :], cst[:, C_ONES:C_ONES + E], n_tiles[:, :], 0.0, ALU.mult, ALU.add))
            link(dve.tensor_tensor(base2[:, :], last_tile[:, :], n_tiles[:, :], ALU.subtract))
            link(dve.tensor_scalar(base[:, :], base2[:, :], float(P), None, ALU.mult))
            link(dve.tensor_tensor(place3[:, :, :], excl[:, :, :], base[:, :].unsqueeze(2).to_broadcast([P, E, TILES]),
                                   ALU.add))
            link(dve.tensor_tensor(place2[:, :, :], rank_ps[:, :, :], place3[:, :, :].rearrange("p e t -> p t e"), ALU.add))
            link(dve.tensor_tensor(place1[:, :, :], place2[:, :, :], onehot[:, :, :], ALU.mult))
            link(dve.tensor_reduce(place[:, :], place1[:, :, :], AX.X, ALU.add))
            dve.tensor_copy(token_i[:, :], cst[:, C_TOKEN:C_TOKEN + TILES]).then_inc(s_place, 1)
            dve.tensor_copy(place_i[:, :], place[:, :]).then_inc(s_place, 1)
            dve.wait_ge(s_place, 2)

            def name(i, n, u, again):
                if again:
                    dve.wait_ge(s_stored[u], stored(n, u) - 16)
                at = bass.ds(i * (ROUND // HI) + (u % HI) * LO + u // HI, 1)
                dve.tensor_copy(slot_of[u][:, :], place_i[:, at])
                dve.tensor_copy(record[u][:, R_TOKEN:R_TOKEN + 1].bitcast(I32), token_i[:, at])
                dve.tensor_copy(record[u][:, R_GATE:R_GATE + 1], gate[:, at]).then_inc(s_places, 1)

            for u in range(ROUND):
                name(0, u, u, False)
            with dve.Fori(1, TILES // ROUND) as i:
                for u in range(ROUND):
                    name(i, i * ROUND + u, u, True)

            link(dve.tensor_tensor(owner[:, :, :], last_tile[:, :].unsqueeze(1).to_broadcast([P, ROUTED, E]),
                                   cst[:, C_IOTA:C_IOTA + ROUTED].unsqueeze(2).to_broadcast([P, ROUTED, E]), ALU.is_le))
            link(dve.tensor_reduce(owner1[:, :], owner[:, :, :], AX.X, ALU.add))
            link(dve.tensor_scalar(owner2[:, :], owner1[:, :], float(E - 1), None, ALU.min))
            link(dve.tensor_tensor(owner3[:, :], owner2[:, :], cst[:, C_PACK:C_COLS], ALU.mult))
            link(dve.tensor_reduce(packed[:, :], owner3[:, :].rearrange("p (r u) -> p r u", u=ROUND), AX.X, ALU.add))
            link(dve.tensor_copy(sh["experts_of"][:, :], packed[:, :]))


def experts(nc, a, cst, sh):
    ctx = ExitStack()
    with ctx:
        def sb(name, shape, dt=F32):
            return ctx.enter_context(nc.sbuf_tensor(name, shape, dt))

        def pb(name, shape):
            return ctx.enter_context(nc.psum_tensor(name, shape, F32))

        def sem(name):
            return ctx.enter_context(nc.semaphore(name))

        FC = FF // P
        assert ROUTED % ROUND == 0
        ROUNDS = ROUTED // ROUND
        record = [sb(f"f_record{i}", [P, REC]) for i in range(ROUND)]
        token = [sb(f"token{i}", [P, 1], I32) for i in range(ROUND)]
        xT = [sb(f"f_xT{i}", [P, P]) for i in range(4)]
        hT = [sb(f"hT{i}", [P, FC, P]) for i in range(4)]
        res = [sb(f"res{i}", [P, D]) for i in range(ROUND)]
        xT_ps = [pb(f"f_xT_ps{i}", [P, P]) for i in range(4)]
        h_ps = [pb(f"h_ps{i}", [P, FC, P]) for i in range(2)]
        y_ps = [pb(f"f_y_ps{i}", [P, D]) for i in range(2)]
        ident = cst[:, C_IDENT:C_IDENT + P]
        w1, w2 = sh["w1"], sh["w2"]
        w2_now = [sb(f"w2_now{i}", [P, FC, D]) for i in range(4)]
        w1_now = [sb(f"w1_now{i}", [P, FC, P]) for i in range(4)]

        s_w1 = sem("f_w1")
        s_w2 = sem("f_w2")
        s_gat = [sem(f"f_gat{i}") for i in range(ROUND)]
        s_xT = sem("f_xTs")
        s_xTe = sem("f_xTe")
        s_h = sem("f_h")
        s_gelu = sem("f_gelu")
        s_y = sem("f_y")
        s_res = sem("f_res")
        s_sca = [sem(f"f_sca{i}") for i in range(ROUND)]
        s_passed_g = sem("f_passed_g")

        block = ctx.enter_context(nc.Block())

        BITS = EXPERTS.bit_length() - 1
        assert EXPERTS == 1 << BITS

        def experts_of(engine, n, u):
            at = (n - u) // ROUND
            return engine.value_load(sh["experts_of"][0:1, bass.ds(at, 1)], min_val=0, max_val=EXPERTS ** ROUND - 1)

        def expert(packed, u):
            return (packed >> (BITS * u)) & (EXPERTS - 1)

        def landed(n, u):
            return (n - u) * (16 // ROUND) + 16

        @block.sync
        def _(sp):
            def load(n, u):
                after(sp, s_res, n - ROUND + 1)
                sp.dma_start(record[u][:, :], a["slots"][bass.ds(n * P, P), :]).then_inc(s_gat[u], 16)

            for u in range(ROUND):
                load(u, u)
            with sp.Fori(1, ROUNDS) as i:
                for u in range(ROUND):
                    load(i * ROUND + u, u)

        @block.gpsimd
        def _(pool):
            def scatter(n, u):
                pool.wait_ge(s_res, n + 1)
                passed(pool, s_passed_g)
                pool.indirect_dma_start(a["out"], bass.IndirectOffsetOnAxis(ap=token[u][:, :].bitcast(U32), axis=0),
                                        res[u][:, :], None, bounds_check=TOKENS - 1, oob_is_err=False).then_inc(s_sca[u], 16)

            for u in range(ROUND):
                scatter(u, u)
            with pool.Fori(1, ROUNDS) as i:
                for u in range(ROUND):
                    scatter(i * ROUND + u, u)
            for u in range(ROUND):
                pool.wait_ge(s_sca[u], 16 * ROUNDS)

        @block.tensor
        def _(pe):
            def turn(n, u):
                pe.wait_ge(s_gat[u], landed(n, u))
                after(pe, s_xTe, n - 3)
                pe.transpose(xT_ps[u % 4][:, :], record[u][:, R_NORM:R_NORM + D], ident).then_inc(s_xT, 1)

            def up(n, u):
                pe.wait_ge(s_w1, n + 1)
                pe.wait_ge(s_xTe, n + 1)
                after(pe, s_gelu, n - 1)
                for c in range(FC):
                    mm = pe.matmul(h_ps[u % 2][:, c, :], w1_now[u % 4][:, c, :],
                                   xT[u % 4][:, :], start=True, stop=True)
                mm.then_inc(s_h, 1)

            def down(n, u):
                pe.wait_ge(s_w2, n + 1)
                pe.wait_ge(s_gelu, n + 1)
                after(pe, s_res, n - 1)
                for c in range(FC):
                    mm = pe.matmul(y_ps[u % 2][:, :], hT[u % 4][:, c, :],
                                   w2_now[u % 4][:, c, :],
                                   start=(c == 0), stop=(c == FC - 1))
                mm.then_inc(s_y, 1)

            def tile(n, u, first, last):
                if not last:
                    turn(n + 2, (u + 2) % ROUND)
                up(n, u)
                if not first:
                    down(n - 2, (u - 2) % ROUND)

            turn(0, 0)
            turn(1, 1)
            for u in range(ROUND):
                tile(u, u, u < 2, False)
            with pe.Fori(1, ROUNDS - 1) as i:
                for u in range(ROUND):
                    tile(i * ROUND + u, u, False, False)
            for u in range(ROUND):
                tile(ROUTED - ROUND + u, u, False, u >= ROUND - 2)
            down(ROUTED - 2, ROUND - 2)
            down(ROUTED - 1, ROUND - 1)

        @block.scalar
        def _(act):
            def gelu(n, u):
                act.wait_ge(s_h, n + 1)
                after(act, s_y, n - 3)
                act.activation(hT[u % 4][:, :, :], h_ps[u % 2][:, :, :], ACT.Gelu).then_inc(s_gelu, 1)

            packed = [None]

            def fetch(n, u):
                if u == 0:
                    packed[0] = experts_of(act, n, u)
                e = expert(packed[0], u)
                after(act, s_h, n - 3)
                act.activation(w1_now[u % 4][:, :, :], w1[:, bass.ds(e * FC, FC), :], ACT.Copy).then_inc(s_w1, 1)

            def step(n, u, left):
                gelu(n, u)
                if left > 3:
                    fetch(n + 3, (u + 3) % ROUND)

            for n in range(3):
                fetch(n, n)
            for u in range(ROUND):
                step(u, u, ROUTED)
            with act.Fori(1, ROUNDS - 1) as i:
                packed[0] = experts_of(act, i * ROUND, 0)
                for u in range(ROUND):
                    step(i * ROUND + u, u, ROUTED)
            packed[0] = experts_of(act, ROUTED - ROUND, 0)
            for u in range(ROUND):
                step(ROUTED - ROUND + u, u, ROUND - u)

        @block.vector
        def _(dve):
            def evacuate(n, u):
                dve.wait_ge(s_xT, n + 1)
                after(dve, s_h, n - 3)
                dve.tensor_copy(xT[u % 4][:, :], xT_ps[u % 4][:, :]).then_inc(s_xTe, 1)

            def weigh(n, u, again):
                dve.wait_ge(s_y, n + 1)
                if again:
                    dve.wait_ge(s_sca[u], landed(n, u) - 16)
                dve.tensor_copy(token[u][:, :], record[u][:, R_TOKEN:R_TOKEN + 1].bitcast(I32))
                dve.scalar_tensor_tensor(out=res[u][:, :], in0=y_ps[u % 2][:, :], scalar=record[u][:, R_GATE:R_GATE + 1],
                                         in1=record[u][:, 0:D], op0=ALU.mult, op1=ALU.add).then_inc(s_res, 1)

            packed = [None]

            def fetch(n, u):
                if u == 0:
                    packed[0] = experts_of(dve, n, u)
                e = expert(packed[0], u)
                after(dve, s_y, n - 3)
                dve.tensor_copy(w2_now[u % 4][:, :, :], w2[:, bass.ds(e * FC, FC), :]).then_inc(s_w2, 1)

            def step(n, u, left, again):
                if left > 4:
                    evacuate(n + 4, (u + 4) % ROUND)
                weigh(n, u, again)
                if left > 4:
                    fetch(n + 4, (u + 4) % ROUND)

            for n in range(4):
                fetch(n, n)
            for n in range(4):
                evacuate(n, n)
            for u in range(ROUND):
                step(u, u, ROUTED, False)
            with dve.Fori(1, ROUNDS - 1) as i:
                packed[0] = experts_of(dve, i * ROUND, 0)
                for u in range(ROUND):
                    step(i * ROUND + u, u, ROUTED, True)
            packed[0] = experts_of(dve, ROUTED - ROUND, 0)
            for u in range(ROUND):
                step(ROUTED - ROUND + u, u, ROUND - u, True)


_INS = ['x', 'ctx_1024', 'mask_Bx1xSxS2_bf1', 'L0_xattn_Wsym', 'L0_ffn_Wg', 'L0_ffn_W1', 'L0_ffn_W2']


def layout(inputs):
    import numpy as np

    arrays = {n: np.ascontiguousarray(inputs[n]) for n in _INS}
    arrays['mask_Bx1xSxS2_bf1'] = arrays['mask_Bx1xSxS2_bf1'].view(np.uint8)
    biases = [inputs[pre + n] for pre in ("L0_attn_b", "L0_xattn_b") for n in NAMES]
    arrays["biases"] = np.stack([np.asarray(b) for b in biases])
    arrays["w_self"] = np.stack([np.asarray(inputs[f"L0_attn_W{n}"]).T for n in NAMES], axis=1)
    arrays["w_cross"] = np.stack([np.asarray(inputs[f"L0_xattn_W{n}"])[0:D] for n in NAMES], axis=1)
    arrays["w_sym"] = np.stack([np.asarray(inputs[f"L0_xattn_W{n}"])[D:] for n in "qkv"], axis=1)
    arrays["scalars"] = np.concatenate([np.asarray(inputs["L0_xattn_" + n])
                                        for n in ("distance_scale", "parity_strength", "localization_length")])
    arrays["cst"], arrays["rows"] = constants()
    return arrays


def declare(nc, arrays):
    args = {n: nc.dram_tensor(f"in_{n}", v.shape, mybir.dt.from_np(v.dtype), kind="ExternalInput").ap()
            for n, v in arrays.items()}
    args["slots"] = nc.dram_tensor("slots", [ROUTED * P, REC], F32, kind="Internal").ap()
    args["out"] = nc.dram_tensor("out", [TOKENS, D], F32, kind="ExternalOutput").ap()
    build(nc, args)


def kernel(**inputs):
    import concourse.bacc as bacc
    from concourse.bass_utils import run_bass_kernel_spmd

    arrays = layout(inputs)
    nc = bacc.Bacc("TRN2", target_bir_lowering=False, num_devices=1)
    declare(nc, arrays)
    r = run_bass_kernel_spmd(nc, [{f"in_{n}": v for n, v in arrays.items()}], core_ids=[0])
    return r.results[0]["out"].reshape(BATCH, SEQ, D)
```
